# Optimizing a Trainium2 kernel written in Bass

```python
import numpy as np
import jax
import jax.numpy as jnp

def _softmax(x, axis=-1):
    return jax.nn.softmax(x, axis=axis)

def _gelu(x):
    return jax.nn.gelu(x, approximate=True)

def _silu(x):
    return jax.nn.silu(x)

def _sigmoid(x):
    return jax.nn.sigmoid(x)

def _layernorm(x, axis=-1, eps=1e-05):
    m = jnp.mean(x, axis=axis, keepdims=True)
    v = jnp.var(x, axis=axis, keepdims=True)
    return (x - m) / jnp.sqrt(v + eps)

def _scatter_add(tgt, idx, src, axis=0):
    return tgt.at[idx].add(src)

def _segment_sum(src, seg, n):
    return jax.ops.segment_sum(src, seg, n)
kernel_name = 'mk_perceiver_d2_seqx_r2_e4c3b0'

def setup_inputs(seed: int=0):
    np.random.seed(seed)
    _w = jnp.asarray

    def _rec_inputs():
        import jax
        import jax.numpy as jnp
        _rk = jax.random.key(seed)
        x = -0.0002928 + 1 * jax.random.normal(jax.random.fold_in(_rk, 1), (1, 512, 512), jnp.float32)
        _lenS = 512 - jax.random.randint(jax.random.fold_in(_rk, 7), (1,), 0, max(1, 512 // 4) + 1, jnp.int32)
        _lenS2 = 8192 - jax.random.randint(jax.random.fold_in(_rk, 8), (1,), 0, max(1, 8192 // 4) + 1, jnp.int32)
        _ctx_1024P = jax.random.normal(jax.random.fold_in(_rk, 11), (1, 16, 512), jnp.float32)
        _ctx_1024c = jax.random.dirichlet(jax.random.fold_in(_rk, 511), 0.3 * jnp.ones((16,), jnp.float32), (1, 8192))
        _ctx_1024t = jnp.einsum('bsk,bkd->bsd', _ctx_1024c, _ctx_1024P)
        _ctx_1024t = _ctx_1024t * jax.lax.rsqrt(jnp.mean(jnp.square(_ctx_1024t)) + 1e-12) * 0.953939
        ctx_1024 = -0.000191848 + 0.999787 * (_ctx_1024t + 0.3 * jax.random.normal(jax.random.fold_in(_rk, 611), (1, 8192, 512), jnp.float32))
        _validS = jnp.arange(512)[None, :] < _lenS[:, None]
        _validS2 = jnp.arange(8192)[None, :] < _lenS2[:, None]
        _causal = jnp.tril(jnp.ones((512, 512), dtype=bool))
        mask_BxS2_bk0 = jnp.logical_not(jnp.broadcast_to(_validS2[:, :], (1, 8192)))
        mask_Bx1xSxS2_ik1 = jnp.where(jnp.broadcast_to(_validS2[:, None, None, :], (1, 1, 512, 8192)), 1, 0).astype(jnp.int32)
        return (x, ctx_1024, mask_BxS2_bk0, mask_Bx1xSxS2_ik1)
    x, ctx_1024, mask_BxS2_bk0, mask_Bx1xSxS2_ik1 = _rec_inputs()

    def _L0_xattn_setup():
        import jax, jax.numpy as jnp
        import numpy as np
        NUM_HEADS = 16
        EPS = 1e-06

        def _ln(t, w, b):
            mu = jnp.mean(t, axis=-1, keepdims=True)
            var = jnp.mean(jnp.square(t - mu), axis=-1, keepdims=True)
            return (t - mu) * jax.lax.rsqrt(var + EPS) * w + b
        key = jax.random.key(seed)
        ks = jax.random.split(key, 10)
        b, s1, s2, qdim, kdim = (2, 1024, 1536, 512, 512)
        d = qdim // NUM_HEADS
        x = jax.random.normal(ks[0], (b, s1, qdim), dtype=jnp.float32)
        y = jax.random.normal(ks[1], (b, s2, kdim), dtype=jnp.float32)
        padding_mask = jax.random.randint(ks[2], (b, s2), 0, 2) > 0
        padding_mask = padding_mask.at[:, 0].set(True)
        w = 0.02
        Wq = jax.random.normal(ks[3], (qdim, qdim), dtype=jnp.float32) * w
        bq = jnp.zeros((qdim,), jnp.float32)
        Wkv = jax.random.normal(ks[4], (2 * qdim, kdim), dtype=jnp.float32) * w
        bkv = jnp.zeros((2 * qdim,), jnp.float32)
        qn_w = jnp.ones((d,), jnp.float32)
        qn_b = jnp.zeros((d,), jnp.float32)
        kn_w = jnp.ones((d,), jnp.float32)
        kn_b = jnp.zeros((d,), jnp.float32)
        Wo = jax.random.normal(ks[5], (qdim, qdim), dtype=jnp.float32) * w
        bo = jnp.zeros((qdim,), jnp.float32)
        return {'x': x, 'y': y, 'padding_mask': padding_mask, 'Wq': Wq, 'bq': bq, 'Wkv': Wkv, 'bkv': bkv, 'qn_w': qn_w, 'qn_b': qn_b, 'kn_w': kn_w, 'kn_b': kn_b, 'Wo': Wo, 'bo': bo}
    _L0_xattn_all = _L0_xattn_setup()
    _L0_xattn_in = {k: v for k, v in _L0_xattn_all.items() if k in ('Wq', 'bq', 'Wkv', 'bkv', 'qn_w', 'qn_b', 'kn_w', 'kn_b', 'Wo', 'bo')}
    del _L0_xattn_all

    def _L0_attn_setup():
        import jax, jax.numpy as jnp
        import numpy as np
        NUM_HEADS = 16
        key = jax.random.key(seed)
        ks = jax.random.split(key, 5)
        B, S, H = (2, 1024, 512)
        scale = 0.02
        return {'x': jax.random.normal(ks[0], (B, S, H), dtype=jnp.float32), 'w_qkv': jax.random.normal(ks[1], (H, 3 * H), dtype=jnp.float32) * scale, 'b_qkv': jax.random.normal(ks[2], (3 * H,), dtype=jnp.float32) * scale, 'w_out': jax.random.normal(ks[3], (H, H), dtype=jnp.float32) * scale, 'b_out': jax.random.normal(ks[4], (H,), dtype=jnp.float32) * scale}
    _L0_attn_all = _L0_attn_setup()
    _L0_attn_in = {k: v for k, v in _L0_attn_all.items() if k in ('w_qkv', 'b_qkv', 'w_out', 'b_out')}
    del _L0_attn_all

    def _L0_ffn_setup():
        import jax, jax.numpy as jnp
        import numpy as np
        D_MODEL, D_FF, N_EXPERTS, TOP_K = (512, 2048, 8, 2)
        key = jax.random.key(seed)
        k1, k2, k3, k4 = jax.random.split(key, 4)
        x = jax.random.normal(k1, (4, 1024, D_MODEL), dtype=jnp.float32)
        router = jax.random.normal(k2, (D_MODEL, N_EXPERTS), dtype=jnp.float32) * (1.0 / np.sqrt(D_MODEL))
        W1 = jax.random.normal(k3, (N_EXPERTS, D_MODEL, D_FF), dtype=jnp.float32) * (1.0 / np.sqrt(D_MODEL))
        W2 = jax.random.normal(k4, (N_EXPERTS, D_FF, D_MODEL), dtype=jnp.float32) * (1.0 / np.sqrt(D_FF))
        return {'x': x, 'router': router, 'W1': W1, 'W2': W2}
    _L0_ffn_all = _L0_ffn_setup()
    _L0_ffn_in = {k: v for k, v in _L0_ffn_all.items() if k in ('router', 'W1', 'W2')}
    del _L0_ffn_all

    def _L1_xattn_setup():
        import jax, jax.numpy as jnp
        import numpy as np
        EMB, HEADS = (512, 16)
        B, S = (4, 1024)
        key = jax.random.key(seed)
        ks = jax.random.split(key, 12)
        scale = 1.0 / np.sqrt(EMB)
        inp = {'q': jax.random.normal(ks[0], (B, S, EMB), jnp.float32), 'k': jax.random.normal(ks[1], (B, S, EMB), jnp.float32), 'v': jax.random.normal(ks[2], (B, S, EMB), jnp.float32), 'mask': jax.random.randint(ks[3], (B, 1, S, S), 0, 2, jnp.int32), 'Wq': jax.random.normal(ks[4], (EMB, EMB), jnp.float32) * scale, 'bq': jnp.zeros((EMB,), jnp.float32), 'Wk': jax.random.normal(ks[5], (EMB, EMB), jnp.float32) * scale, 'bk': jnp.zeros((EMB,), jnp.float32), 'Wv': jax.random.normal(ks[6], (EMB, EMB), jnp.float32) * scale, 'bv': jnp.zeros((EMB,), jnp.float32), 'Wo': jax.random.normal(ks[7], (EMB, EMB), jnp.float32) * scale, 'bo': jnp.zeros((EMB,), jnp.float32)}
        return inp
    _L1_xattn_all = _L1_xattn_setup()
    _L1_xattn_in = {k: v for k, v in _L1_xattn_all.items() if k in ('Wq', 'bq', 'Wk', 'bk', 'Wv', 'bv', 'Wo', 'bo')}
    del _L1_xattn_all

    def _L1_attn_setup():
        import jax, jax.numpy as jnp
        import numpy as np
        DIM = 512
        H = 16
        D = DIM // H
        K = 64
        key = jax.random.key(seed)
        ks = jax.random.split(key, 7)
        B, S = (2, 1024)
        x = jax.random.normal(ks[0], (B, S, DIM), dtype=jnp.float32)
        cantor_coords = jax.random.uniform(ks[1], (S,), dtype=jnp.float32)
        scale = 1.0 / np.sqrt(DIM)
        Wq = jax.random.normal(ks[2], (DIM, DIM), dtype=jnp.float32) * scale
        Wk = jax.random.normal(ks[3], (DIM, DIM), dtype=jnp.float32) * scale
        Wv = jax.random.normal(ks[4], (DIM, DIM), dtype=jnp.float32) * scale
        Wo = jax.random.normal(ks[5], (DIM, DIM), dtype=jnp.float32) * scale
        bo = jnp.zeros((DIM,), dtype=jnp.float32)
        return {'x': x, 'cantor_coords': cantor_coords, 'Wq': Wq, 'Wk': Wk, 'Wv': Wv, 'Wo': Wo, 'bo': bo}
    _L1_attn_all = _L1_attn_setup()
    _L1_attn_in = {k: v for k, v in _L1_attn_all.items() if k in ('cantor_coords', 'Wq', 'Wk', 'Wv', 'Wo', 'bo')}
    del _L1_attn_all

    def _L1_ffn_setup():
        import jax, jax.numpy as jnp
        import numpy as np
        TOP_K = 2
        key = jax.random.key(seed)
        kx, kg, k1, k2 = jax.random.split(key, 4)
        B, T, D, E, H = (4, 512, 512, 8, 1024)
        x = jax.random.normal(kx, (B, T, D), dtype=jnp.float32)
        Wg = jax.random.normal(kg, (D, E), dtype=jnp.float32) * 0.02
        W1 = jax.random.normal(k1, (E, D, H), dtype=jnp.float32) * 0.02
        W2 = jax.random.normal(k2, (E, H, D), dtype=jnp.float32) * 0.02
        return {'x': x, 'Wg': Wg, 'W1': W1, 'W2': W2}
    _L1_ffn_all = _L1_ffn_setup()
    _L1_ffn_in = {k: v for k, v in _L1_ffn_all.items() if k in ('Wg', 'W1', 'W2')}
    del _L1_ffn_all
    return {'x': x, 'ctx_1024': ctx_1024, 'mask_BxS2_bk0': mask_BxS2_bk0, 'mask_Bx1xSxS2_ik1': mask_Bx1xSxS2_ik1, 'L0_xattn_Wq': _L0_xattn_in['Wq'], 'L0_xattn_bq': _L0_xattn_in['bq'], 'L0_xattn_Wkv': _L0_xattn_in['Wkv'], 'L0_xattn_bkv': _L0_xattn_in['bkv'], 'L0_xattn_qn_w': _L0_xattn_in['qn_w'], 'L0_xattn_qn_b': _L0_xattn_in['qn_b'], 'L0_xattn_kn_w': _L0_xattn_in['kn_w'], 'L0_xattn_kn_b': _L0_xattn_in['kn_b'], 'L0_xattn_Wo': _L0_xattn_in['Wo'], 'L0_xattn_bo': _L0_xattn_in['bo'], 'L0_attn_w_qkv': _L0_attn_in['w_qkv'], 'L0_attn_b_qkv': _L0_attn_in['b_qkv'], 'L0_attn_w_out': _L0_attn_in['w_out'], 'L0_attn_b_out': _L0_attn_in['b_out'], 'L0_ffn_router': _L0_ffn_in['router'], 'L0_ffn_W1': _L0_ffn_in['W1'], 'L0_ffn_W2': _L0_ffn_in['W2'], 'L1_xattn_Wq': _L1_xattn_in['Wq'], 'L1_xattn_bq': _L1_xattn_in['bq'], 'L1_xattn_Wk': _L1_xattn_in['Wk'], 'L1_xattn_bk': _L1_xattn_in['bk'], 'L1_xattn_Wv': _L1_xattn_in['Wv'], 'L1_xattn_bv': _L1_xattn_in['bv'], 'L1_xattn_Wo': _L1_xattn_in['Wo'], 'L1_xattn_bo': _L1_xattn_in['bo'], 'L1_attn_cantor_coords': _L1_attn_in['cantor_coords'], 'L1_attn_Wq': _L1_attn_in['Wq'], 'L1_attn_Wk': _L1_attn_in['Wk'], 'L1_attn_Wv': _L1_attn_in['Wv'], 'L1_attn_Wo': _L1_attn_in['Wo'], 'L1_attn_bo': _L1_attn_in['bo'], 'L1_ffn_Wg': _L1_ffn_in['Wg'], 'L1_ffn_W1': _L1_ffn_in['W1'], 'L1_ffn_W2': _L1_ffn_in['W2']}

def reference(x, ctx_1024, mask_BxS2_bk0, mask_Bx1xSxS2_ik1, L0_xattn_Wq, L0_xattn_bq, L0_xattn_Wkv, L0_xattn_bkv, L0_xattn_qn_w, L0_xattn_qn_b, L0_xattn_kn_w, L0_xattn_kn_b, L0_xattn_Wo, L0_xattn_bo, L0_attn_w_qkv, L0_attn_b_qkv, L0_attn_w_out, L0_attn_b_out, L0_ffn_router, L0_ffn_W1, L0_ffn_W2, L1_xattn_Wq, L1_xattn_bq, L1_xattn_Wk, L1_xattn_bk, L1_xattn_Wv, L1_xattn_bv, L1_xattn_Wo, L1_xattn_bo, L1_attn_cantor_coords, L1_attn_Wq, L1_attn_Wk, L1_attn_Wv, L1_attn_Wo, L1_attn_bo, L1_ffn_Wg, L1_ffn_W1, L1_ffn_W2):
    import jax
    import jax.numpy as jnp

    def _L0_xattn_ref(x, y, padding_mask, Wq, bq, Wkv, bkv, qn_w, qn_b, kn_w, kn_b, Wo, bo):
        import jax, jax.numpy as jnp
        import numpy as np
        NUM_HEADS = 16
        EPS = 1e-06

        def _ln(t, w, b):
            mu = jnp.mean(t, axis=-1, keepdims=True)
            var = jnp.mean(jnp.square(t - mu), axis=-1, keepdims=True)
            return (t - mu) * jax.lax.rsqrt(var + EPS) * w + b
        b, s1, c = x.shape
        s2 = y.shape[1]
        h, d = (NUM_HEADS, c // NUM_HEADS)
        scale = d ** (-0.5)
        q = (x @ Wq.T + bq).reshape(b, s1, h, d)
        kv = (y @ Wkv.T + bkv).reshape(b, s2, 2, h, d)
        k, v = (kv[:, :, 0], kv[:, :, 1])
        q = _ln(q, qn_w, qn_b) * scale
        k = _ln(k, kn_w, kn_b)
        attn = jnp.einsum('bihd,bjhd->bhij', q, k)
        attn = jnp.where(padding_mask[:, None, None, :], attn, -jnp.inf)
        p = jax.nn.softmax(attn, axis=-1)
        ctx = jnp.einsum('bhij,bjhd->bihd', p, v).reshape(b, s1, c)
        out = ctx @ Wo.T + bo
        return out

    def _L0_attn_ref(x, w_qkv, b_qkv, w_out, b_out):
        import jax, jax.numpy as jnp
        import numpy as np
        NUM_HEADS = 16
        B, S, H = x.shape
        nh = NUM_HEADS
        hd = H // nh
        attn_scale = 1.0 / np.sqrt(hd).astype(np.float32)
        qkv = x @ w_qkv + b_qkv
        q, k, v = jnp.split(qkv, 3, axis=-1)
        to_heads = lambda t: t.reshape(B, S, nh, hd).transpose(0, 2, 1, 3)
        q, k, v = (to_heads(q), to_heads(k), to_heads(v))
        scores = jnp.einsum('bhid,bhjd->bhij', q, k) * attn_scale
        i = jnp.arange(S)[:, None]
        j = jnp.arange(S)[None, :]
        scores = jnp.where(j >= i, scores, -jnp.inf)
        attn = jax.nn.softmax(scores, axis=-1)
        out = jnp.einsum('bhij,bhjd->bhid', attn, v)
        out = out.transpose(0, 2, 1, 3).reshape(B, S, H)
        return out @ w_out + b_out

    def _L0_ffn_ref(x, router, W1, W2):
        import jax, jax.numpy as jnp
        import numpy as np
        D_MODEL, D_FF, N_EXPERTS, TOP_K = (512, 2048, 8, 2)
        B, S, d = x.shape
        E = router.shape[1]
        xf = x.reshape(-1, d)
        logits = xf @ router
        top_v, top_i = jax.lax.top_k(logits, TOP_K)
        w = jax.nn.softmax(top_v, axis=-1)
        gates = jnp.sum(jax.nn.one_hot(top_i, E, dtype=x.dtype) * w[..., None], axis=1)
        out = jnp.zeros_like(xf)
        for e in range(E):
            h = xf @ W1[e]
            h = h * jax.nn.sigmoid(h)
            out = out + gates[:, e:e + 1] * (h @ W2[e])
        return out.reshape(B, S, d)

    def _L1_xattn_ref(q, k, v, mask, Wq, bq, Wk, bk, Wv, bv, Wo, bo):
        import jax, jax.numpy as jnp
        import numpy as np
        EMB, HEADS = (512, 16)
        B, S = (4, 1024)
        Bq, Sq, E = q.shape
        H = HEADS
        D = E // H
        Q = (q @ Wq.T + bq).reshape(Bq, Sq, H, D).transpose(0, 2, 1, 3)
        K = (k @ Wk.T + bk).reshape(Bq, -1, H, D).transpose(0, 2, 1, 3)
        V = (v @ Wv.T + bv).reshape(Bq, -1, H, D).transpose(0, 2, 1, 3)
        scores = jnp.einsum('bhqd,bhkd->bhqk', Q, K) / jnp.sqrt(jnp.float32(D))
        scores = jnp.where(mask == 1, jnp.float32(-1000000000.0), scores)
        attn = jax.nn.softmax(scores, axis=-1)
        out = jnp.einsum('bhqk,bhkd->bhqd', attn, V)
        out = out.transpose(0, 2, 1, 3).reshape(Bq, Sq, E)
        return out @ Wo.T + bo

    def _L1_attn_ref(x, cantor_coords, Wq, Wk, Wv, Wo, bo):
        import jax, jax.numpy as jnp
        import numpy as np
        DIM = 512
        H = 16
        D = DIM // H
        K = 64
        B, S, Dim = x.shape
        q = jnp.einsum('bsd,ed->bse', x, Wq).reshape(B, S, H, D)
        k = jnp.einsum('bsd,ed->bse', x, Wk).reshape(B, S, H, D)
        v = jnp.einsum('bsd,ed->bse', x, Wv).reshape(B, S, H, D)
        idx = jnp.arange(S)[:, None]
        off = jnp.arange(-K // 2, K // 2)[None, :]
        routes = jnp.clip(idx + off, 0, S - 1)
        kg = k[:, routes]
        vg = v[:, routes]
        scores = jnp.einsum('bshd,bskhd->bshk', q, kg) / np.sqrt(D)
        attn = jax.nn.softmax(scores, axis=-1)
        out = jnp.einsum('bshk,bskhd->bshd', attn, vg).reshape(B, S, Dim)
        return jnp.einsum('bsd,ed->bse', out, Wo) + bo

    def _L1_ffn_ref(x, Wg, W1, W2):
        import jax, jax.numpy as jnp
        import numpy as np
        TOP_K = 2
        B, T, D = x.shape
        E = W1.shape[0]
        logits = jnp.einsum('btd,de->bte', x, Wg)
        probs = jax.nn.softmax(logits, axis=-1)
        top_w, top_i = jax.lax.top_k(probs, TOP_K)
        top_w = top_w / (jnp.sum(top_w, axis=-1, keepdims=True) + 1e-08)
        N = B * T
        oh = jax.nn.one_hot(top_i.reshape(N, TOP_K), E, dtype=x.dtype)
        combine = jnp.sum(oh * top_w.reshape(N, TOP_K)[..., None], axis=1)
        xt = x.reshape(N, D)
        h = jnp.einsum('td,edh->teh', xt, W1)
        h = jnp.square(jax.nn.relu(h))
        y = jnp.einsum('teh,ehd->ted', h, W2)
        out = jnp.einsum('te,ted->td', combine, y)
        return out.reshape(B, T, D)
    x = x + _L0_xattn_ref(_layernorm(x, axis=-1), ctx_1024, mask_BxS2_bk0, L0_xattn_Wq, L0_xattn_bq, L0_xattn_Wkv, L0_xattn_bkv, L0_xattn_qn_w, L0_xattn_qn_b, L0_xattn_kn_w, L0_xattn_kn_b, L0_xattn_Wo, L0_xattn_bo)
    x = x + _L0_attn_ref(_layernorm(x, axis=-1), L0_attn_w_qkv, L0_attn_b_qkv, L0_attn_w_out, L0_attn_b_out)
    x = x + _L0_ffn_ref(_layernorm(x, axis=-1), L0_ffn_router, L0_ffn_W1, L0_ffn_W2)
    x = x + _L1_xattn_ref(_layernorm(x, axis=-1), ctx_1024, ctx_1024, mask_Bx1xSxS2_ik1, L1_xattn_Wq, L1_xattn_bq, L1_xattn_Wk, L1_xattn_bk, L1_xattn_Wv, L1_xattn_bv, L1_xattn_Wo, L1_xattn_bo)
    x = x + _L1_attn_ref(_layernorm(x, axis=-1), L1_attn_cantor_coords, L1_attn_Wq, L1_attn_Wk, L1_attn_Wv, L1_attn_Wo, L1_attn_bo)
    x = x + _L1_ffn_ref(_layernorm(x, axis=-1), L1_ffn_Wg, L1_ffn_W1, L1_ffn_W2)
    return x

_drawn_inputs = setup_inputs


def setup_inputs(seed=0):
    import zlib

    import numpy as np

    out = dict(_drawn_inputs(seed))
    spreads = {'L0_xattn_bq': (0.0, 0.1),
     'L0_xattn_bkv': (0.0, 0.1),
     'L0_xattn_qn_w': (1.0, 0.6),
     'L0_xattn_qn_b': (0.0, 0.483),
     'L0_xattn_kn_w': (1.0, 0.6),
     'L0_xattn_kn_b': (0.0, 2.0),
     'L0_xattn_bo': (0.0, 0.1),
     'L1_xattn_bq': (0.0, 0.398),
     'L1_xattn_bk': (0.0, 2.0),
     'L1_xattn_bv': (0.0, 0.1),
     'L1_xattn_bo': (0.0, 0.1),
     'L1_attn_bo': (0.0, 0.1)}
    factors = {'L0_attn_b_qkv': 3.181}
    for name, (base, spread) in spreads.items():
        noise = np.random.default_rng([zlib.crc32(name.encode()), seed]).standard_normal(out[name].shape)
        drawn = base * np.exp(spread * noise) if base else spread * noise
        out[name] = jnp.asarray(drawn.astype(out[name].dtype))
    for name, factor in factors.items():
        out[name] = (out[name] * factor).astype(out[name].dtype)
    return out
```

```python
from contextlib import ExitStack

import numpy as np
import concourse.bass as bass
from concourse import mybir

F32 = mybir.dt.float32
BF16 = mybir.dt.bfloat16
I32 = mybir.dt.int32
U8 = mybir.dt.uint8
ALU = mybir.AluOpType
ACT = mybir.ActivationFunctionType
AX = mybir.AxisListType

P = 128
D = 512
T = 512
NQ = T // P
DC = D // P
H = 16
HD = D // H
G = P // HD
S2 = 8192
KB = 512
NB = S2 // KB
KT_ = KB // P
E = 8
NR = 15
SCALE = float(HD) ** -0.5
NEG = -1.0e30
LOWEST = -3.0e38
WINDOW = 32

VEC = ["L0x_bq", "L0x_bk", "L0x_bv", "L0a_bq", "L0a_bk", "L0a_bv", "L1x_bq", "L1x_bk", "L1x_bv", "zero",
       "qn_w", "qn_b", "kn_w", "kn_b"]
C_N0, C_L0, C_N1, C_L1, C_NR, C_E = 0, 1, 32, 33, 64, 65


def consts():
    p = np.arange(P)
    heads = np.zeros((P, P))
    spread = np.zeros((DC, P, P))
    for c in range(DC):
        heads[p, H * c + G * c + p // HD] = 1.0 / HD
        spread[c, G * c + p // HD, p] = 1.0
    c = {"ident": np.eye(P), "group_mean": (p[:, None] // HD == p[None, :] // HD) / HD,
         "before": (p[:, None] < p[None, :]) * 1.0, "upto": (p[:, None] <= p[None, :]) * 1.0,
         "ones": np.ones((P, P)), "ramp": np.tile(p[None, :], (P, 1)) * 1.0,
         "index": np.tile(p[:, None], (1, P)) * 1.0, "head_mean": heads,
         **{f"spread{k}": spread[k] for k in range(DC)}}
    return np.concatenate([c[k] for k in CONST], axis=1).astype(np.float32)


CONST = ["ident", "group_mean", "before", "upto", "ones", "ramp", "index", "head_mean",
         "spread0", "spread1", "spread2", "spread3"]


def fixed_biases():
    i = np.arange(T)
    later = np.where(i[None, :] >= i[:, None], 0.0, NEG)
    count = np.zeros((T, T))
    for off in range(-WINDOW, WINDOW):
        np.add.at(count, (i, np.clip(i + off, 0, T - 1)), 1.0)
    window = np.where(count > 0, np.log(np.maximum(count, 1.0)), NEG)
    out = np.zeros((2, 2, P, NQ, T), np.float32)
    for n, b in enumerate((later, window)):
        out[n, 0] = b.reshape(NQ, P, T).transpose(1, 0, 2)
        out[n, 1] = b.T.reshape(NQ, P, T).transpose(1, 0, 2)
    return out


def in_parts(a):
    bf = mybir.dt.np(BF16)
    parts = []
    for _ in range(3):
        parts.append(a.astype(bf))
        a = a - parts[-1].astype(np.float32)
    return np.stack(parts, axis=-3)


class Attention:

    def __init__(self, name, wq, wk, wv, wo, bo, fixed=None, count=None, norm=False, row_mask=False):
        self.name, self.wq, self.wk, self.wv, self.wo, self.bo = name, wq, wk, wv, wo, bo
        self.fixed = fixed
        self.count = count
        self.norm = norm
        self.row_mask = row_mask
        self.keys_of, self.queries_of = [(0, KB)] * NQ, [(0, T)] * KT_
        if fixed is not None:
            self.keys_of = [(max(0, P * q - WINDOW) if fixed else P * q, min(KB, P * q + P + WINDOW) if fixed else KB)
                            for q in range(NQ)]
            self.queries_of = [(max(0, P * k - WINDOW) if fixed else 0, min(T, P * k + P + WINDOW) if fixed else P * k + P)
                               for k in range(KT_)]
        self.order = list(range(KT_))[::-1] if fixed == 0 else list(range(KT_))
        self.bq, self.bk, self.bv = [f"{name}_b{x}" if name != "L1a" else "zero" for x in "qkv"]


class Chip:
    pass


def blocks_to_do(eng, m, L):
    if L.fixed is not None:
        return 1
    return eng.value_load(m.CTL[0:1, L.count:L.count + 1], min_val=0, max_val=NB)


UNWAITED = []


def wait_alone(eng, sem, value):
    eng.wait_ge(sem, value)
    eng.sem_inc(UNWAITED[0], 1)


def raised(nc, m, loops):
    fresh, m.fresh = m.fresh, []
    if not loops:
        return 0
    for sem in fresh:
        nc.gpsimd.sem_inc(sem, 1)
    nc.all_engine_barrier()
    return 1


def one(j):
    return slice(j, j + 1) if isinstance(j, int) else bass.ds(j, 1)


def first_iterations(nc, i):
    return nc.s_assert_within(i, 0, NB // 4 - 1, skip_runtime_bounds_check_because="inside If(i < NB // 4)")


def over_blocks(eng, L, n, body):
    if L.fixed is not None:
        body(0)
        return
    with eng.Fori(0, NB) as i:
        with eng.If(i < n):
            body(i)


def active_blocks(nc, m, tag, flags, count, unmasked=None):
    ch, mm, ld = m.sem(tag + "_dve"), m.sem(tag + "_pe"), m.sem(tag + "_loaded")
    F, POS, LST, RF = m.small[0:NB, 80:81], m.small[0:NB, 82:83], m.small[0:NB, 84:84 + NB], m.small[:, 116:120]
    with nc.Block() as block:
        @block.sync
        def _(sp):
            if unmasked is None:
                sp.dma_start(m.CON[:, :, :], m.d["consts"].rearrange("p (k n) -> p k n", n=P)).then_inc(ld, 16)
                sp.dma_start(m.KMW[0:NB, :], m.d["keymask"]).then_inc(ld, 16)
                sp.wait_ge(ld, 32)
                for t, src in ((m.VT[:, :, :], m.d["vectors"].rearrange("p (v c) -> p v c", c=4)),
                               (m.X[:, :, :], m.d["x"].rearrange("(t p) d -> p t d", p=P))):
                    sp.dma_start(t, src).then_inc(ld, 16)
                sp.wait_ge(ld, 64)

        @block.vector
        def _(dve):
            v = nc.vector
            k = 0
            if unmasked is None:
                v.memset(m.CTL[:, :], 0).then_inc(ch, 1)
                v.memset(m.MINUS1[:, :], -1.0).then_inc(ch, 1)
                dve.wait_ge(ld, 32)
                v.tensor_copy(m.IDB[:, :], m.ident[:, :]).then_inc(ch, 1)
                v.tensor_reduce(F, m.KM[0:NB, 0:KB], AX.X, ALU.max).then_inc(ch, 1)
                k = 4
            else:
                v.tensor_reduce(RF, unmasked, AX.X, ALU.max).then_inc(ch, 1)
                dve.wait_ge(ch, 1)
                v.tensor_scalar(m.RA[:, :], RF, 0.0, None, ALU.is_gt).then_inc(ch, 1)
                v.tensor_scalar(RF, RF, 0.0, None, ALU.is_le).then_inc(ch, 1)
                v.tensor_scalar(unmasked, unmasked, 0.0, None, ALU.is_gt).then_inc(ch, 1)
                dve.wait_ge(mm, 1)
                v.tensor_reduce(F, m.bank[0][0:NB, 0:5], AX.X, ALU.add).then_inc(ch, 1)
                v.tensor_copy(m.RAROW[:, :], m.bank[1][:, :]).then_inc(ch, 1)
                dve.wait_ge(ch, 6)
                v.tensor_scalar(m.RN[:, :], m.RA[:, :], NEG, None, ALU.mult).then_inc(ch, 1)
                v.tensor_scalar(m.RNROW[:, :], m.RAROW[:, :], NEG, None, ALU.mult).then_inc(ch, 1)
                k = 8
            dve.wait_ge(ch, k)
            v.tensor_scalar(F, F, 0.0, None, ALU.is_gt).then_inc(ch, 1)
            dve.wait_ge(mm, 1 if unmasked is None else 2)
            v.tensor_copy(POS, m.bank[2][0:NB, 0:1]).then_inc(ch, 1)
            dve.wait_ge(ch, k + 2)
            v.tensor_scalar(LST, m.ramp[0:NB, 1:NB + 1], POS, F, ALU.is_equal, ALU.mult).then_inc(ch, 1)
            dve.wait_ge(mm, 2 if unmasked is None else 3)
            v.tensor_copy(m.CTL[0:1, count:count + 1 + NB], m.bank[3][0:1, 0:1 + NB]).then_inc(ch, 1)
            dve.wait_ge(ch, k + 4)

        @block.tensor
        def _(pe):
            t = nc.tensor
            k = 5
            if unmasked is not None:
                k = 9
                pe.wait_ge(ch, 4)
                for q in range(NQ):
                    t.matmul(m.bank[0][0:NB, 0:1], unmasked[:, q, :], m.ones[:, 0:1], start=q == 0, stop=q == NQ - 1)
                for q in range(NQ):
                    t.matmul(m.bank[0][0:NB, 1 + q:2 + q], m.ones[:, 0:NB], RF[:, q:q + 1], start=False, stop=True,
                             skip_group_check=True)
                for q in range(NQ):
                    last = t.matmul(m.bank[1][:, q * P:(q + 1) * P], m.RA[:, q:q + 1].to_broadcast([P, P]), m.ident[:, :],
                                    start=True, stop=True)
                last.then_inc(mm, 1)
            else:
                pe.wait_ge(ld, 32)
            pe.wait_ge(ch, k)
            t.matmul(m.bank[2][0:NB, 0:1], m.upto[0:NB, 0:NB], F, start=True, stop=True).then_inc(mm, 1)
            pe.wait_ge(ch, k + 2)
            t.matmul(m.bank[3][0:1, 0:1], m.ones[0:NB, 0:1], F, start=True, stop=True)
            t.matmul(m.bank[3][0:1, 1:1 + NB], m.index[0:NB, 0:1], LST, start=True, stop=True).then_inc(mm, 1)


def normalise(nc, m, tag, L=None):
    ch, sq, tr, ev = m.sem(tag + "_ln"), m.sem(tag + "_ln_sqrt"), m.sem(tag + "_ln_tr"), m.sem(tag + "_ln_xnt")
    ST, MV, SD = m.small[:, 0:24], m.small[:, 24:32], m.small[:, 32:36]
    if L is not None:
        m.wq_loaded, m.wkv_loaded = m.sem(tag + "_wq"), m.sem(tag + "_wkv")
    with nc.Block() as block:
        @block.sync
        def _(sp):
            if L is not None:
                for t, src, sem in ((m.WQ, L.wq, m.wq_loaded), (m.WK, L.wk, m.wkv_loaded), (m.WV, L.wv, m.wkv_loaded)):
                    sp.dma_start(t[:, :, :], m.d[src].rearrange("(c p) n -> p c n", p=P)).then_inc(sem, 16)

        @block.vector
        def _(dve):
            v = nc.vector
            for t in range(NQ):
                v.bn_stats(ST[:, 6 * t:6 * t + 6], m.X[:, t, :]).then_inc(ch, 1)
            dve.wait_ge(ch, 4)
            for t in range(NQ):
                v.bn_aggr(MV[:, 2 * t:2 * t + 2], ST[:, 6 * t:6 * t + 6]).then_inc(ch, 1)
            dve.wait_ge(ch, 8)
            v.tensor_scalar(SD, MV.rearrange("p (t k) -> p t k", k=2)[:, :, 1], 1e-5, None, ALU.add).then_inc(ch, 1)
            dve.wait_ge(sq, 1)
            v.reciprocal(SD, SD).then_inc(ch, 1)
            dve.wait_ge(ch, 10)
            for t in range(NQ):
                v.tensor_scalar(m.XN[:, t, :], m.X[:, t, :], MV[:, 2 * t:2 * t + 1], SD[:, t:t + 1],
                                ALU.subtract, ALU.mult).then_inc(ch, 1)
            for c in (0, 2):
                dve.wait_ge(tr, c + 1)
                v.tensor_copy(m.XNT[:, c, :], m.bank[c][:, :]).then_inc(ev, 1)

        @block.scalar
        def _(act):
            act.wait_ge(ch, 9)
            nc.scalar.activation(SD, SD, ACT.Sqrt).then_inc(sq, 1)
            for c in (1, 3):
                act.wait_ge(tr, c + 1)
                nc.scalar.activation(m.XNT[:, c, :], m.bank[c][:, :], ACT.Copy).then_inc(ev, 1)
            act.wait_ge(ev, DC)

        @block.tensor
        def _(pe):
            pe.wait_ge(ch, 14)
            for c in range(DC):
                for t in range(NQ):
                    last = nc.tensor.transpose(m.bank[c][:, t * P:(t + 1) * P], m.XN[:, t, c * P:(c + 1) * P], m.ident[:, :])
                last.then_inc(tr, 1)


def centre(nc, m, dve, W, ch, k):
    v = nc.vector
    Wg = W[:, :, :].rearrange("p c (h f) -> p (c h) f", f=HD)
    MW = m.small[:, 0:DC * H]
    v.tensor_reduce(MW, Wg, AX.X, ALU.add).then_inc(ch, 1)
    dve.wait_ge(ch, k + 1)
    v.tensor_scalar(MW, MW, 1.0 / HD, None, ALU.mult).then_inc(ch, 1)
    dve.wait_ge(ch, k + 2)
    v.tensor_tensor(Wg, Wg, MW.unsqueeze(2).to_broadcast([P, DC * H, HD]), ALU.subtract).then_inc(ch, 1)
    return k + 3


def queries(nc, m, L):
    n = L.name
    z, ch, pj = m.sem(n + "_zeroed"), m.sem(n + "_q_dve"), m.sem(n + "_q_pe")
    sq, va, p1, r1 = m.sem(n + "_q_sq"), m.sem(n + "_q_var"), m.sem(n + "_q_part1"), m.sem(n + "_q_rest1")
    p2, p3, st, qf = m.sem(n + "_q_part2"), m.sem(n + "_q_part3"), m.sem(n + "_q_stored"), m.sem(n + "_q_full")
    ql = m.q_loaded = m.sem(n + "_q_stacks")
    QF, QP = m.KF, m.PARTS
    with nc.Block() as block:
        @block.sync
        def _(sp):
            for c in range(DC):
                sp.wait_ge(p3, c + 1)
                sp.dma_start(m.QSAVE[:, :, c, :].rearrange("j p n -> p j n"), QP[:, :, c, :]).then_inc(st, 16)
            sp.wait_ge(z, 1)
            for c in range(DC):
                sp.wait_ge(st, 16 * DC)
                for stack, parts in ((m.QA, (0, 1, 0)), (m.QB, (1, 2, 0))):
                    for j, part in enumerate(parts):
                        sp.dma_start(stack[HD * j:HD * j + HD, G * c:G * c + G, :],
                                     m.QSAVE[part, :, c, :].rearrange("(g f) n -> f g n", f=HD)).then_inc(ql, 16)
            sp.wait_ge(ql, 16 * 6 * DC)

        @block.gpsimd
        def _(pool):
            g = nc.gpsimd
            g.memset(m.QB[3 * HD:P, :, :], 0.0).then_inc(z, 1)
            pool.wait_ge(z, 1)
            for c in range(DC + 1):
                if c < DC:
                    pool.wait_ge(p1, c + 1)
                    g.tensor_tensor(QF[:, c, :], QF[:, c, :], QP[:, 0, c, :], ALU.subtract).then_inc(r1, 1)
                if c:
                    pool.wait_ge(p2, c)
                    g.tensor_tensor(QP[:, 2, c - 1, :], QF[:, c - 1, :], QP[:, 1, c - 1, :], ALU.subtract).then_inc(p3, 1)

        @block.vector
        def _(dve):
            v = nc.vector
            v.memset(m.MX[:, :], LOWEST).then_inc(ch, 1)
            k = 1
            if L.norm:
                dve.wait_ge(m.wq_loaded, 16)
                k = centre(nc, m, dve, m.WQ, ch, k)
                dve.wait_ge(m.wkv_loaded, 32)
                dve.wait_ge(ch, k)
                k = centre(nc, m, dve, m.WK, ch, k)
                dve.wait_ge(pj, 1)
                for j, b in enumerate((L.bq, L.bk)):
                    v.tensor_tensor(m.vec(b), m.vec(b), m.bank[7][:, 4 * j:4 * j + 4], ALU.subtract).then_inc(ch, 1)
                for b in ("qn_w", "qn_b"):
                    v.tensor_scalar(m.vec(b), m.vec(b), SCALE, None, ALU.mult).then_inc(ch, 1)
                v.memset(m.EPS[:, :], 1e-6).then_inc(ch, 1)
                k += 5
                dve.wait_ge(sq, 9)
                v.reciprocal(m.RSTD[:, :], m.RSTD[:, :]).then_inc(ch, 1)
                for c in range(DC):
                    dve.wait_ge(va, c + 2)
                    v.tensor_tensor(QF[:, c, :], QF[:, c, :], m.bank[2 + c][:, :], ALU.mult).then_inc(ch, 1)
            else:
                if not L.row_mask:
                    v.memset(m.RAROWS[:, :], SCALE).then_inc(ch, 1)
                else:
                    v.tensor_scalar(m.RAROWS[:, :], m.RAROW[:, :], SCALE, None, ALU.mult).then_inc(ch, 1)
                dve.wait_ge(ch, 2)
                for c in range(DC):
                    dve.wait_ge(pj, c + 1)
                    v.scalar_tensor_tensor(QF[:, c, :], m.bank[c % 2][:, :], m.vec(L.bq)[:, c:c + 1],
                                           m.RAROWS[:, :], ALU.add, ALU.mult).then_inc(qf, 1)

        @block.scalar
        def _(act):
            a = nc.scalar
            if L.norm:
                act.wait_ge(ch, 12)
                for c in range(DC):
                    act.wait_ge(pj, c + 2)
                    b = m.vec(L.bq)[:, c:c + 1]
                    a.activation(m.PB[:, 0, c, :], m.bank[c % 2][:, :], ACT.Square, bias=b).then_inc(sq, 1)
                    a.activation(QF[:, c, :], m.bank[c % 2][:, :], ACT.Identity, bias=b).then_inc(sq, 1)
                act.wait_ge(va, 1)
                a.activation(m.RSTD[:, :], m.bank[6][0:H, :], ACT.Sqrt, bias=m.EPS[0:H, :]).then_inc(sq, 1)
                for c in range(DC):
                    act.wait_ge(ch, 13 + c + 1)
                    a.activation(QF[:, c, :], QF[:, c, :], ACT.Identity, bias=m.vec("qn_b")[:, 0:1],
                                 scale=m.vec("qn_w")[:, 0:1]).then_inc(qf, 1)
            for c in range(DC + 1):
                if c < DC:
                    act.wait_ge(qf, c + 1)
                    a.activation(QP[:, 0, c, :], QF[:, c, :], ACT.Copy).then_inc(p1, 1)
                if c:
                    act.wait_ge(r1, c)
                    a.activation(QP[:, 1, c - 1, :], QF[:, c - 1, :], ACT.Copy).then_inc(p2, 1)

        @block.tensor
        def _(pe):
            t = nc.tensor
            pe.wait_ge(m.wq_loaded, 16)
            if L.norm:
                for j, b in enumerate((L.bq, L.bk)):
                    last = t.matmul(m.bank[7][:, 4 * j:4 * j + 4], m.gmean[:, :], m.vec(b), start=True, stop=True)
                last.then_inc(pj, 1)
                pe.wait_ge(ch, 4)
            for c in range(DC):
                if c >= 2:
                    pe.wait_ge(sq if L.norm else qf, 2 * (c - 1) if L.norm else c - 1)
                for d in range(DC):
                    last = t.matmul(m.bank[c % 2][:, :], m.WQ[:, d, c * P:(c + 1) * P], m.XNT[:, d, :],
                                    start=d == 0, stop=d == DC - 1)
                last.then_inc(pj, 1)
            if L.norm:
                pe.wait_ge(sq, 8)
                for c in range(DC):
                    last = t.matmul(m.bank[6][0:H, :], m.head_mean[:, H * c:H * c + H], m.PB[:, 0, c, :],
                                    start=c == 0, stop=c == DC - 1)
                last.then_inc(va, 1)
                pe.wait_ge(ch, 13)
                for c in range(DC):
                    t.matmul(m.bank[2 + c][:, :], m.spread[c][0:H, :], m.RSTD[:, :], start=True, stop=True).then_inc(va, 1)


def row_maxima(nc, m, L):
    m.fresh = []
    n = L.name + "_max"
    ld, lm, pj, sq, ve = m.sem(n + "_ctx"), m.sem(n + "_mask"), m.sem(n + "_proj"), m.sem(n + "_sq"), m.sem(n + "_v")
    sc, mx, bi = m.sem(n + "_scores"), m.sem(n + "_taken"), m.sem(n + "_bias")
    p1, r1, p2, p3 = m.sem(n + "_part1"), m.sem(n + "_rest1"), m.sem(n + "_part2"), m.sem(n + "_part3")
    sk, sv, va, sd, rs, kn, kf = (m.sem(n + x) for x in ("_kstored", "_vstored", "_var", "_std", "_rstd", "_knorm", "_kfull"))
    la = [m.sem(f"{n}_stack{c}") for c in range(DC)]
    cl, cc = [m.sem(f"{n}_count_mask{u}") for u in range(2)], m.sem(n + "_counted")
    NS = H * NQ
    dyn = L.fixed is None
    src = m.CT if dyn else m.XNT
    counting = L.norm
    B = raised(nc, m, dyn)

    with nc.Block() as block:
        @block.sync
        def _(sp):
            nb = blocks_to_do(sp, m, L)

            def load_context(j):
                b = sp.value_load(m.CTL[0:1, (bass.ds(j + (L.count + 1), 1) if not isinstance(j, int) else slice(j + L.count + 1, j + L.count + 2))],
                                  min_val=0, max_val=NB - 1)
                sp.dma_start(m.CT[:, :, :], m.d["ctx"][bass.ds(b, 1)].rearrange("a p c k -> (a p) c k")).then_inc(ld, 16)

            def load_mask(j):
                b = sp.value_load(m.CTL[0:1, (bass.ds(j + (L.count + 1), 1) if not isinstance(j, int) else slice(j + L.count + 1, j + L.count + 2))],
                                  min_val=0, max_val=NB - 1)
                if L.row_mask:
                    sp.dma_start(m.MI[:, :, :], m.d["mask_q"][bass.ds(b, 1)].rearrange("a p t k -> (a p) t k")).then_inc(lm, 16)
                else:
                    sp.dma_start(m.KMW[:, :], m.d["keymask"][bass.ds(b, 1)].to_broadcast([P, KB // 4])).then_inc(lm, 16)

            def keep(j):
                wait_alone(sp, p3, j * DC + DC + B)
                sp.dma_start(m.KSAVE[one(j)].rearrange("a p k c n -> (a p) k c n"), m.PARTS).then_inc(sk, 16)
                wait_alone(sp, ve, j * KT_ + KT_ + B)
                sp.dma_start(m.VSAVE[one(j)].rearrange("a p k n -> (a p) k n"), m.V[:, :, :]).then_inc(sv, 16)

            def stack(j, c):
                for r, part in enumerate((0, 0, 1)):
                    sp.dma_start(m.KA[HD * r:HD * r + HD, G * c:G * c + G, :],
                                 m.KSAVE[one(j), :, part, c, :].rearrange("a (g f) n -> (a f) g n", f=HD)).then_inc(la[c], 16)

            if dyn:
                load_context(0)
                load_mask(0)
            else:
                sp.dma_start(m.MB[:, :, :], m.d["biases"][L.fixed, 0]).then_inc(lm, 16)
            keep(0)
            if dyn:
                wait_alone(sp, pj, 2 * DC + B)
                load_context(1)
            wait_alone(sp, sk, 16 + B)
            for c in range(DC):
                stack(0, c)
            if not dyn:
                sp.wait_ge(sv, 16)
                return

            with sp.Fori(0, NB) as i:
                if counting:
                    with sp.If(i < NB // 4):
                        i4 = first_iterations(nc, i)
                        for u in range(4):
                            wait_alone(sp, cc, i * 4 * NQ + max(0, u - 1) * NQ + B)
                            sp.dma_start(m.COUNT[:, u % 2], m.d["mask_q"][bass.ds(i4 * 4 + u, 1)].rearrange("a p t k -> (a p) t k")).then_inc(cl[u % 2], 16)
                with sp.If(i < nb):
                    wait_alone(sp, bi, i + 1 + B)
                    load_mask(i + 1)
                    keep(i + 1)
                    wait_alone(sp, pj, i * (2 * DC) + 4 * DC + B)
                    load_context(i + 2)
                    wait_alone(sp, sk, i * 16 + 32 + B)
                    for c in range(DC):
                        wait_alone(sp, mx, i * NS + (c + 1) * G * NQ + B)
                        stack(i + 1, c)
            wait_alone(sp, sv, nb * 16 + 16 + B)
            wait_alone(sp, ld, nb * 16 + 32 + B)
            wait_alone(sp, lm, nb * 16 + 16 + B)
            for c in range(DC):
                wait_alone(sp, la[c], nb * 48 + 48 + B)

        @block.tensor
        def _(pe):
            nb = blocks_to_do(pe, m, L)
            t = nc.tensor

            def project(j, x):
                if x == 0 and dyn:
                    pe.wait_ge(ld, j * 16 + 16 + B)
                if x < DC:
                    pe.wait_ge(sq, j * (2 * DC) + max(0, x - 1) * 2 + B)
                    for d in range(DC):
                        last = t.matmul(m.bank[x % 2][:, :], m.WK[:, d, x * P:(x + 1) * P], src[:, d, :],
                                        start=d == 0, stop=d == DC - 1)
                    last.then_inc(pj, 1)
                    if x == DC - 1 and L.norm:
                        pe.wait_ge(sq, j * (2 * DC) + 2 * DC + B)
                        pe.wait_ge(kn, j * DC + B)
                        for d in range(DC):
                            last = t.matmul(m.bank[3][0:H, :], m.head_mean[:, H * d:H * d + H], m.PB[:, 0, d, :],
                                            start=d == 0, stop=d == DC - 1)
                        last.then_inc(va, 1)
                    return
                kb = x - DC
                pe.wait_ge(ve, j * KT_ + kb + B)
                for d in range(DC):
                    last = t.matmul(m.bank[2][:, :], src[:, d, kb * P:(kb + 1) * P], m.WV[:, d, :],
                                    start=d == 0, stop=d == DC - 1)
                last.then_inc(pj, 1)
                if L.norm:
                    pe.wait_ge(rs, j + 1 + B)
                    pe.wait_ge(kn, j * DC + kb + B)
                    t.matmul(m.bank[3][:, :], m.spread[kb][0:H, :], m.RSTD[:, :], start=True, stop=True).then_inc(va, 1)

            def scores(i, ahead):
                for k in range(NS):
                    h, q = k // NQ, k % NQ
                    k0, k1 = L.keys_of[q]
                    if k % (G * NQ) == 0:
                        pe.wait_ge(la[h // G], i * 48 + 48 + B)
                    pe.wait_ge(mx, i * NS + max(0, k - 3) + B)
                    t.matmul(m.bank[4 + k % 4][:, k0:k1], m.QA[0:3 * HD, h, q * P:(q + 1) * P], m.KA[0:3 * HD, h, k0:k1],
                             start=True, stop=True).then_inc(sc, 1)
                    if ahead and k % 8 == 7:
                        project(i + 1, k // 8)

            pe.wait_ge(m.wkv_loaded, 32)
            for x in range(2 * DC):
                project(0, x)
            if not dyn:
                scores(0, False)
                return
            with pe.Fori(0, NB) as i:
                with pe.If(i < nb):
                    scores(i, True)

        @block.scalar
        def _(act):
            nb = blocks_to_do(act, m, L)
            a = nc.scalar

            def count(i, u):
                act.wait_ge(cl[u % 2], i * 32 + 16 * (u // 2 + 1) + B)
                for q in range(NQ):
                    a.activation(m.COUNT[:, u % 2, q, :], m.COUNT[:, u % 2, q, :], ACT.Square, bias=m.MINUS1[:, :],
                                 accum_out=m.UNMASKED[:, q, bass.ds(i * 4 + u, 1)]).then_inc(cc, 1)

            def evacuate(j, i=None):
                def second(c):
                    act.wait_ge(r1, j * DC + c + 1 + B)
                    a.activation(m.PARTS[:, 1, c, :], m.KF[:, c, :], ACT.Copy).then_inc(p2, 1)

                def values(kb):
                    act.wait_ge(pj, j * (2 * DC) + DC + kb + 1 + B)
                    a.activation(m.V[:, kb, :], m.bank[2][:, :], ACT.Copy).then_inc(ve, 1)

                act.wait_ge(p3, j * DC + B)
                act.wait_ge(sk, j * 16 + B)
                for c in range(DC):
                    act.wait_ge(pj, j * (2 * DC) + c + 1 + B)
                    b = m.vec(L.bk)[:, c:c + 1]
                    if L.norm:
                        a.activation(m.PB[:, 0, c, :], m.bank[c % 2][:, :], ACT.Square, bias=b).then_inc(sq, 1)
                        a.activation(m.KF[:, c, :], m.bank[c % 2][:, :], ACT.Identity, bias=b).then_inc(sq, 1)
                    else:
                        a.activation(m.KF[:, c, :], m.bank[c % 2][:, :], ACT.Identity, bias=b).then_inc(sq, 1)
                        a.activation(m.PARTS[:, 0, c, :], m.bank[c % 2][:, :], ACT.Identity, bias=b).then_inc(sq, 1)
                        if c:
                            second(c - 1)
                if L.norm:
                    act.wait_ge(va, j * 5 + 1 + B)
                    a.activation(m.RSTD[:, :], m.bank[3][0:H, :], ACT.Sqrt, bias=m.EPS[0:H, :]).then_inc(sd, 1)
                act.wait_ge(sv, j * 16 + B)
                for kb in range(KT_):
                    values(kb)
                    if L.norm:
                        act.wait_ge(kn, j * DC + kb + 1 + B)
                        a.activation(m.KF[:, kb, :], m.KF[:, kb, :], ACT.Identity, bias=m.vec("kn_b")[:, 0:1],
                                     scale=m.vec("kn_w")[:, 0:1]).then_inc(kf, 1)
                        act.wait_ge(kf, j * DC + kb + 1 + B)
                        a.activation(m.PARTS[:, 0, kb, :], m.KF[:, kb, :], ACT.Copy).then_inc(p1, 1)
                        if kb:
                            second(kb - 1)
                    elif kb == 0:
                        second(DC - 1)
                if L.norm:
                    second(DC - 1)

            evacuate(0)
            if not dyn:
                return
            with act.Fori(0, NB) as i:
                if counting:
                    with act.If(i < NB // 4):
                        i4 = first_iterations(nc, i)
                        for u in range(4):
                            count(i4, u)
                with act.If(i < nb):
                    evacuate(i + 1)
            if counting:
                act.wait_ge(cc, NB * NQ + B)

        @block.gpsimd
        def _(pool):
            nb = blocks_to_do(pool, m, L)
            g = nc.gpsimd

            def split(j):
                for c in range(DC + 1):
                    if c < DC:
                        if L.norm:
                            pool.wait_ge(p1, j * DC + c + 1 + B)
                        else:
                            pool.wait_ge(sq, j * (2 * DC) + 2 * c + 2 + B)
                        g.tensor_tensor(m.KF[:, c, :], m.KF[:, c, :], m.PARTS[:, 0, c, :], ALU.subtract).then_inc(r1, 1)
                    if c:
                        pool.wait_ge(p2, j * DC + c + B)
                        g.tensor_tensor(m.PARTS[:, 2, c - 1, :], m.KF[:, c - 1, :], m.PARTS[:, 1, c - 1, :],
                                        ALU.subtract).then_inc(p3, 1)

            split(0)
            if not dyn:
                return
            with pool.Fori(0, NB) as i:
                with pool.If(i < nb):
                    split(i + 1)

        @block.vector
        def _(dve):
            nb = blocks_to_do(dve, m, L)
            v = nc.vector

            def inverse(j):
                dve.wait_ge(sd, j + 1 + B)
                v.reciprocal(m.RSTD[:, :], m.RSTD[:, :]).then_inc(rs, 1)

            def scale(j, c):
                dve.wait_ge(va, j * 5 + 2 + c + B)
                v.tensor_tensor(m.KF[:, c, :], m.KF[:, c, :], m.bank[3][:, :], ALU.mult).then_inc(kn, 1)

            def maxima(i, ahead):
                if dyn:
                    dve.wait_ge(mx, i * NS + B)
                    dve.wait_ge(lm, i * 16 + 16 + B)
                    if L.row_mask:
                        for q in range(NQ):
                            last = v.tensor_scalar(m.MB[:, q, :], m.MI[:, q, :], 1.0, m.RN[:, q:q + 1], ALU.is_equal, ALU.mult)
                    else:
                        last = v.tensor_scalar(m.MB[:, 0, :], m.KM[:, 0:KB], 1.0, -NEG, ALU.subtract, ALU.mult)
                    last.then_inc(bi, 1)
                    dve.wait_ge(bi, i + 1 + B)
                else:
                    dve.wait_ge(lm, 16)
                for k in range(NS):
                    q = k % NQ
                    k0, k1 = L.keys_of[q]
                    bias = m.MB[:, q if (L.row_mask or not dyn) else 0, k0:k1]
                    dve.wait_ge(mx, i * NS + max(0, k - 3) + B)
                    wait_alone(dve, sc, i * NS + k + 1 + B)
                    v.tensor_tensor_reduce(m.JUNK[:, k % 4, k0:k1], m.bank[4 + k % 4][:, k0:k1], bias, 1.0, m.MX[:, k:k + 1],
                                           ALU.add, ALU.max, m.MX[:, k:k + 1]).then_inc(mx, 1)
                    if ahead and L.norm:
                        if k == 39:
                            inverse(i + 1)
                        if k >= 43 and (k - 43) % 8 == 0:
                            scale(i + 1, (k - 43) // 8)
                if ahead and L.norm:
                    scale(i + 1, DC - 1)

            if L.norm:
                inverse(0)
                for c in range(DC):
                    scale(0, c)
            if not dyn:
                maxima(0, False)
                return
            with dve.Fori(0, NB) as i:
                with dve.If(i < nb):
                    maxima(i, True)


def shifts(nc, m, L):
    n = L.name
    ch, tr, st = m.sem(n + "_shift_dve"), m.sem(n + "_shift_tr"), m.sem(n + "_shift_stored")
    z = m.sem(n + "_ones")
    m.wo_loaded = m.sem(n + "_wo")
    R, PART = m.small[:, 0:64], m.MXB
    with nc.Block() as block:
        @block.sync
        def _(sp):
            sp.dma_start(m.WQ[:, :, :], m.d[L.wo].rearrange("(c p) n -> p c n", p=P)).then_inc(m.wo_loaded, 16)
            sp.dma_start(m.RAROWS[:, :], m.d["bo"][L.bo]).then_inc(m.wo_loaded, 16)
            sp.wait_ge(ch, 11)
            sp.dma_start(m.MSAVE, m.NM[:, :]).then_inc(st, 16)
            sp.wait_ge(st, 16)
            sp.dma_start(m.QB[3 * HD:3 * HD + 3, :, :], m.MSAVE.rearrange("(j h) n -> j h n", h=H)).then_inc(st, 16)
            sp.wait_ge(st, 32)

        @block.gpsimd
        def _(pool):
            nc.gpsimd.memset(m.KBS[3 * HD:P, :, :], 1.0).then_inc(z, 1)
            pool.wait_ge(z, 1)
            nc.gpsimd.memset(m.OACC[:, :, :], 0.0)
            nc.gpsimd.memset(m.DACC[:, :, :], 0.0)

        @block.vector
        def _(dve):
            v = nc.vector
            v.tensor_scalar(R, m.MX[:, :], -1.0, None, ALU.mult).then_inc(ch, 1)
            k = 1
            out = m.NMX[:, :].rearrange("p (q j h) -> p j q h", q=NQ, j=3)
            for j in range(3):
                dve.wait_ge(ch, k)
                v.tensor_copy(PART[:, :], R).then_inc(ch, 1)
                dve.wait_ge(ch, k + 1)
                v.tensor_copy(out[:, j], PART[:, :].rearrange("p (h q) -> p q h", q=NQ)).then_inc(ch, 1)
                v.tensor_tensor(R, R, PART[:, :], ALU.subtract).then_inc(ch, 1)
                k += 3
            dve.wait_ge(tr, 1)
            v.tensor_copy(m.NM[:, :], m.bank[0][0:3 * H, :]).then_inc(ch, 1)

        @block.tensor
        def _(pe):
            pe.wait_ge(ch, 10)
            for q in range(NQ):
                last = nc.tensor.transpose(m.bank[0][0:3 * H, q * P:(q + 1) * P], m.NMX[:, q * 3 * H:(q + 1) * 3 * H], m.ident[:, :])
            last.then_inc(tr, 1)


def weighted_values(nc, m, L):
    m.fresh = []
    n = L.name + "_pv"
    lm, sc, ex, pv, pa = (m.sem(n + x) for x in ("_mask", "_scores", "_exp", "_product", "_psum"))
    dn, oa, bi, zs = (m.sem(n + x) for x in ("_den", "_acc", "_bias", "_zeroed"))
    lk = [m.sem(f"{n}_keys{c}") for c in range(DC)]
    steps = [(c, k) for c in range(DC) for k in range(KT_)]
    NS = len(steps)
    dyn = L.fixed is None
    kt = L.order
    PER = 7 * 16
    B = raised(nc, m, dyn)
    with nc.Block() as block:
        @block.sync
        def _(sp):
            nb = blocks_to_do(sp, m, L)

            def load_mask(j):
                b = sp.value_load(m.CTL[0:1, (bass.ds(j + (L.count + 1), 1) if not isinstance(j, int) else slice(j + L.count + 1, j + L.count + 2))],
                                  min_val=0, max_val=NB - 1)
                if L.row_mask:
                    sp.dma_start(m.MI[:, :, :], m.d["mask_k"][bass.ds(b, 1)].rearrange("a p t k -> (a p) t k")).then_inc(lm, 16)
                else:
                    sp.dma_start(m.KMW[:, 0:1], m.d["keymask_k"][bass.ds(b, 1)].rearrange("a p t -> (a p) t")).then_inc(lm, 16)

            def load_keys(j, c):
                for stack, parts in ((m.KA, (0, 0, 1)), (m.KBS, (1, 0, 2))):
                    for r, part in enumerate(parts):
                        sp.dma_start(stack[HD * r:HD * r + HD, G * c:G * c + G, :],
                                     m.KSAVE[one(j), :, part, c, :].rearrange("a (g f) n -> (a f) g n", f=HD)).then_inc(lk[c], 16)
                sp.dma_start(m.V[:, :, c * P:(c + 1) * P],
                             m.VSAVE[one(j), :, :, c * P:(c + 1) * P].rearrange("a p k n -> (a p) k n")).then_inc(lk[c], 16)

            if dyn:
                load_mask(0)
            else:
                sp.dma_start(m.MBF, m.d["bias_parts"][L.fixed]).then_inc(lm, 16)
            for c in range(DC):
                load_keys(0, c)
            if not dyn:
                return
            with sp.Fori(0, NB) as i:
                with sp.If(i < nb):
                    wait_alone(sp, bi, i + 1 + B)
                    load_mask(i + 1)
                    for c in range(DC):
                        wait_alone(sp, pv, i * NS + (c + 1) * KT_ + B)
                        load_keys(i + 1, c)
            wait_alone(sp, lm, nb * 16 + 16 + B)
            for c in range(DC):
                wait_alone(sp, lk[c], nb * PER + PER + B)

        @block.tensor
        def _(pe):
            nb = blocks_to_do(pe, m, L)
            t = nc.tensor

            def body(i):
                def times_values(s):
                    c, k = steps[s]
                    q0, q1 = L.queries_of[kt[k]]
                    if k == 0:
                        pe.wait_ge(oa, i * (2 * DC) + 2 * max(0, c - 1) + B)
                    pe.wait_ge(ex, i * (NS * G) + G * s + G + B)
                    for g in range(G):
                        h = G * c + g
                        last = t.matmul(m.bank[2 + c % 2][HD * g:HD * g + HD, q0:q1], m.V[:, kt[k], HD * h:HD * h + HD],
                                        m.PB[:, s % 2, g, q0:q1], start=k == 0, stop=k == KT_ - 1,
                                        skip_group_check=not dyn)
                    last.then_inc(pv, 1)

                def denominators(c):
                    pe.wait_ge(pa, i * NS + KT_ * c + KT_ + B)
                    for g in range(G):
                        last = t.matmul(m.bank[c % 2][HD * g:HD * g + HD, :], m.ones[:, 0:HD], m.PS[:, g, :],
                                        start=True, stop=True)
                    last.then_inc(dn, 1)

                if not dyn:
                    pe.wait_ge(lm, 16)
                elif L.row_mask:
                    pe.wait_ge(bi, i + 1 + B)
                for s, (c, k) in enumerate(steps):
                    q0, q1 = L.queries_of[kt[k]]
                    if k == 0:
                        pe.wait_ge(lk[c], i * PER + PER + B)
                    for g in range(G):
                        h = G * c + g
                        pe.wait_ge(ex, i * (NS * G) + max(0, G * (s - 1) + g + 1) + B)
                        o = m.bank[4 + g][:, q0:q1]
                        ks = slice(kt[k] * P, (kt[k] + 1) * P)
                        biases = []
                        if L.row_mask:
                            biases = [m.MBK[:, kt[k], q0:q1]]
                        elif not dyn:
                            parts = 3 if L.fixed and kt[k] in (0, KT_ - 1) else 1
                            biases = [m.MBF[:, j, kt[k], q0:q1] for j in range(parts)]
                        for j, b in enumerate(biases):
                            t.matmul(o, m.IDB[:, :], b, start=j == 0, stop=False)
                        t.matmul(o, m.KA[0:3 * HD, h, ks], m.QA[0:3 * HD, h, q0:q1], start=not biases, stop=False)
                        t.matmul(o, m.KBS[:, h, ks], m.QB[:, h, q0:q1], start=False, stop=True).then_inc(sc, 1)
                    if s:
                        times_values(s - 1)
                    if k == 0 and c:
                        denominators(c - 1)
                times_values(NS - 1)
                denominators(DC - 1)
            over_blocks(pe, L, nb, body)

        @block.scalar
        def _(act):
            nb = blocks_to_do(act, m, L)
            a = nc.scalar

            def body(i):
                if dyn and not L.row_mask:
                    act.wait_ge(bi, i + 1 + B)
                for s, (c, k) in enumerate(steps):
                    q0, q1 = L.queries_of[kt[k]]
                    act.wait_ge(pv, i * NS + max(0, s - 1) + B)
                    act.wait_ge(pa, i * NS + max(0, s - 1) + B)
                    for g in range(G):
                        act.wait_ge(sc, i * (NS * G) + G * s + g + 1 + B)
                        kw = {}
                        if dyn and not L.row_mask:
                            kw["bias"] = m.KBIAS[:, kt[k]:kt[k] + 1]
                        a.activation(m.PB[:, s % 2, g, q0:q1], m.bank[4 + g][:, q0:q1], ACT.Exp, **kw).then_inc(ex, 1)
            over_blocks(act, L, nb, body)

        @block.vector
        def _(dve):
            nb = blocks_to_do(dve, m, L)
            v = nc.vector

            def body(i):
                if dyn:
                    dve.wait_ge(lm, i * 16 + 16 + B)
                    dve.wait_ge(ex, i * (NS * G) + B)
                    if L.row_mask:
                        for kb in range(KT_):
                            last = v.scalar_tensor_tensor(m.MBK[:, kb, :], m.MI[:, kb, :], 1.0, m.RNROW[:, :],
                                                          ALU.is_equal, ALU.mult)
                    else:
                        last = v.tensor_scalar(m.KBIAS[:, :], m.KM[:, 0:KT_], 1.0, -NEG, ALU.subtract, ALU.mult)
                    last.then_inc(bi, 1)

                def add_up(c):
                    dve.wait_ge(oa, i * (2 * DC) + 2 * c + B)
                    dve.wait_ge(pv, i * NS + KT_ * c + KT_ + B)
                    v.tensor_tensor(m.OACC[:, c, :], m.OACC[:, c, :], m.bank[2 + c % 2][:, :], ALU.add).then_inc(oa, 1)
                    dve.wait_ge(dn, i * DC + c + 1 + B)
                    v.tensor_tensor(m.DACC[:, c, :], m.DACC[:, c, :], m.bank[c % 2][:, :], ALU.add).then_inc(oa, 1)

                for s, (c, k) in enumerate(steps):
                    q0, q1 = L.queries_of[kt[k]]
                    if k == 0:
                        dve.wait_ge(dn, i * DC + c + B)
                        if (q0, q1) != (0, T):
                            v.memset(m.PS[:, :, :], 0.0).then_inc(zs, 1)
                            dve.wait_ge(zs, c + 1)
                    dve.wait_ge(ex, i * (NS * G) + G * s + G + B)
                    dve.wait_ge(pa, i * NS + s + B)
                    dst = m.PS[:, :, q0:q1]
                    if k == 0 and (q0, q1) == (0, T):
                        v.tensor_copy(dst, m.PB[:, s % 2]).then_inc(pa, 1)
                    else:
                        v.tensor_tensor(dst, dst, m.PB[:, s % 2, :, q0:q1], ALU.add).then_inc(pa, 1)
                    if k == 1 and c:
                        add_up(c - 1)
                add_up(DC - 1)
            over_blocks(dve, L, nb, body)


def project_out(nc, m, L):
    n = L.name + "_out"
    ch, op, xs = m.sem(n + "_dve"), m.sem(n + "_proj"), m.sem(n + "_x")
    with nc.Block() as block:
        @block.tensor
        def _(pe):
            pe.wait_ge(m.wo_loaded, 32)
            for c in range(DC):
                pe.wait_ge(ch, 3 * c + 3)
                for q in range(NQ):
                    last = nc.tensor.matmul(m.bank[4 + q][:, :], m.OACC[:, c, q * P:(q + 1) * P], m.WQ[:, c, :],
                                            start=c == 0, stop=c == DC - 1)
                    if c == DC - 1:
                        last.then_inc(op, 1)

        @block.vector
        def _(dve):
            v = nc.vector
            dve.wait_ge(m.wo_loaded, 32)
            for c in range(DC):
                v.reciprocal(m.DACC[:, c, :], m.DACC[:, c, :]).then_inc(ch, 1)
                dve.wait_ge(ch, 3 * c + 1)
                v.tensor_tensor(m.OACC[:, c, :], m.OACC[:, c, :], m.DACC[:, c, :], ALU.mult).then_inc(ch, 1)
                dve.wait_ge(ch, 3 * c + 2)
                v.tensor_scalar(m.OACC[:, c, :], m.OACC[:, c, :], m.vec(L.bv)[:, c:c + 1], None, ALU.add).then_inc(ch, 1)
            for q in range(NQ):
                v.tensor_tensor(m.X[:, q, :], m.X[:, q, :], m.RAROWS[:, :], ALU.add).then_inc(xs, 1)
            for q in range(NQ):
                dve.wait_ge(op, q + 1)
                dve.wait_ge(xs, NQ)
                v.tensor_tensor(m.X[:, q, :], m.X[:, q, :], m.bank[4 + q][:, :], ALU.add).then_inc(xs, 1)
            dve.wait_ge(xs, 2 * NQ)


def attention(nc, m, L):
    normalise(nc, m, L.name, L)
    queries(nc, m, L)
    row_maxima(nc, m, L)
    shifts(nc, m, L)
    weighted_values(nc, m, L)
    project_out(nc, m, L)


def route(nc, m, tag, router, probs):
    ld, ch, mm, ac = m.sem(tag + "_router"), m.sem(tag + "_rt_dve"), m.sem(tag + "_rt_pe"), m.sem(tag + "_rt_act")
    s = m.small
    LG = s[:, 0:32]
    ONE = [s[:, 32:64], s[:, 64:96]]
    T1, T2 = s[:, 96:128], s[:, 128:160]
    MM = [s[:, 160:164], s[:, 164:168]]
    IX, AA, BB = s[:, 168:172], s[:, 172:176], s[:, 176:180]
    SM = s[:, 180:212]
    NE, RD, CU = s[0:E, 212:213], s[0:E, 213:214], s[0:E, 214:215]
    LE = s[0:E, 216:232]
    RK = s[:, 232:264]
    def r3(x):
        return x.rearrange("p (t e) -> p t e", e=E)
    def bc(x):
        return x.unsqueeze(2).to_broadcast([P, NQ, E])
    ramp8 = m.ramp[:, 0:E].unsqueeze(1).to_broadcast([P, NQ, E])
    with nc.Block() as block:
        @block.sync
        def _(sp):
            sp.dma_start(m.WR[:, :, :], m.d[router].rearrange("(c p) e -> p c e", p=P)).then_inc(ld, 16)

        @block.vector
        def _(dve):
            v = nc.vector
            m.steps = 0

            def do(ins):
                m.steps += 1
                ins.then_inc(ch, 1)
                dve.wait_ge(ch, m.steps)

            dve.wait_ge(mm, 1)
            do(v.tensor_copy(LG, m.bank[0][:, 0:32]))
            if probs:
                do(v.tensor_reduce(AA, r3(LG), AX.X, ALU.max))
                do(v.tensor_tensor(r3(LG), r3(LG), bc(AA), ALU.subtract))
                m.mark["exp"] = m.steps
                dve.wait_ge(ac, 1)
                do(v.tensor_reduce(AA, r3(LG), AX.X, ALU.add))
                do(v.reciprocal(AA, AA))
                do(v.tensor_tensor(r3(LG), r3(LG), bc(AA), ALU.mult))
            do(v.tensor_copy(T1, LG))
            for k in range(2):
                do(v.tensor_reduce(MM[k], r3(T1), AX.X, ALU.max))
                do(v.tensor_tensor(r3(T2), r3(T1), bc(MM[k]), ALU.is_equal))
                do(v.tensor_scalar(T2, T2, -float(E), float(E), ALU.mult, ALU.add))
                do(v.tensor_tensor(r3(T2), r3(T2), ramp8, ALU.add))
                do(v.tensor_reduce(IX, r3(T2), AX.X, ALU.min))
                do(v.tensor_tensor(r3(ONE[k]), ramp8, bc(IX), ALU.is_equal))
                if k == 0:
                    do(v.scalar_tensor_tensor(T1, ONE[0], LOWEST, LG, ALU.mult, ALU.add))
            do(v.tensor_tensor(SM, ONE[0], ONE[1], ALU.add))
            m.mark["selected"] = m.steps
            GW = m.GW[:, :].rearrange("p (t k) -> p t k", k=2)
            if probs:
                do(v.tensor_tensor(AA, MM[0], MM[1], ALU.add))
                do(v.tensor_scalar(AA, AA, 1e-8, None, ALU.add))
                do(v.reciprocal(BB, AA))
                do(v.tensor_tensor(GW[:, :, 0], MM[0], BB, ALU.mult))
                do(v.tensor_tensor(GW[:, :, 1], MM[1], BB, ALU.mult))
            else:
                do(v.tensor_tensor(AA, MM[1], MM[0], ALU.subtract))
                m.mark["exp"] = m.steps
                dve.wait_ge(ac, 1)
                do(v.tensor_scalar(BB, AA, 1.0, None, ALU.add))
                do(v.reciprocal(BB, BB))
                do(v.tensor_copy(GW[:, :, 0], BB))
                do(v.tensor_tensor(GW[:, :, 1], AA, BB, ALU.mult))
            dve.wait_ge(mm, 2)
            do(v.tensor_copy(NE, m.bank[2][0:E, 0:1]))
            do(v.tensor_scalar(RD, NE, 0.0, None, ALU.is_gt))
            for k in range(1, NQ):
                do(v.scalar_tensor_tensor(RD, NE, float(P * k), RD, ALU.is_gt, ALU.add))
            m.mark["rounds"] = m.steps
            do(v.tensor_copy(RK, m.bank[1][:, 0:32]))
            dve.wait_ge(mm, 3)
            do(v.tensor_copy(CU, m.bank[3][0:E, 0:1]))
            do(v.tensor_scalar(LE, m.ramp[0:E, 0:16], CU, None, ALU.is_ge))
            m.mark["of_round"] = m.steps
            do(v.tensor_scalar(T1[:, 0:E], m.bank[4][:, 0:E], float(P), None, ALU.mult))
            do(v.tensor_tensor(r3(RK), r3(RK), T1[:, 0:E].unsqueeze(1).to_broadcast([P, NQ, E]), ALU.add))
            GS = m.GS[:, :].rearrange("p (t k) -> p t k", k=2)
            for k in range(2):
                do(v.tensor_tensor(T2, RK, ONE[k], ALU.mult))
                do(v.tensor_reduce(GS[:, :, k], r3(T2), AX.X, ALU.add))
            do(v.tensor_copy(m.CTL[0:1, C_NR:C_NR + 1], m.bank[5][0:1, 0:1]))
            dve.wait_ge(mm, 4)
            do(v.tensor_copy(m.CTL[0:1, C_E:C_E + 16], m.bank[6][0:1, 0:16]))

        @block.tensor
        def _(pe):
            t = nc.tensor
            pe.wait_ge(ld, 16)
            for q in range(NQ):
                for d in range(DC):
                    last = t.matmul(m.bank[0][:, E * q:E * q + E], m.XNT[:, d, q * P:(q + 1) * P], m.WR[:, d, :],
                                    start=d == 0, stop=d == DC - 1)
            last.then_inc(mm, 1)
            pe.wait_ge(ch, m.mark["selected"])
            for q in range(NQ):
                for b in range(q + 1):
                    t.matmul(m.bank[1][:, E * q:E * q + E], (m.before if b == q else m.ones)[:, :], r3(SM)[:, b, :],
                             start=b == 0, stop=b == q)
            for q in range(NQ):
                last = t.matmul(m.bank[2][0:E, 0:1], r3(SM)[:, q, :], m.ones[:, 0:1], start=q == 0, stop=q == NQ - 1)
            last.then_inc(mm, 1)
            pe.wait_ge(ch, m.mark["rounds"])
            t.matmul(m.bank[3][0:E, 0:1], m.upto[0:E, 0:E], RD, start=True, stop=True)
            t.matmul(m.bank[4][:, 0:E], RD.to_broadcast([E, P]), m.before[0:E, 0:E], start=True, stop=True)
            t.matmul(m.bank[5][0:1, 0:1], RD, m.ones[0:E, 0:1], start=True, stop=True).then_inc(mm, 1)
            pe.wait_ge(ch, m.mark["of_round"])
            t.matmul(m.bank[6][0:1, 0:16], m.ones[0:E, 0:1], LE, start=True, stop=True).then_inc(mm, 1)

        @block.scalar
        def _(act):
            act.wait_ge(ch, m.mark["exp"])
            if probs:
                nc.scalar.activation(LG, LG, ACT.Exp).then_inc(ac, 1)
            else:
                nc.scalar.activation(AA, AA, ACT.Exp).then_inc(ac, 1)


def experts(nc, m, tag, w1, w2, F, relu2):
    m.fresh = []
    NF = F // KB
    l1, l2 = ([m.sem(f"{tag}_{w}_{k}") for k in range(NF)] for w in ("w1", "w2"))
    dd, xe, xs = (m.sem(tag + x) for x in ("_onehot", "_gather", "_gathered"))
    hp, hs, yo, sc = (m.sem(tag + x) for x in ("_h", "_act", "_yout", "_scatter"))
    xa, tr, tc, u1, ex, gc = (m.sem(tag + x) for x in ("_xadd", "_tr", "_trout", "_used", "_exp", "_dve"))
    def slots(a, b):
        return [t[:, 8 * k:8 * k + 8, :].bitcast(F32).rearrange("p (c x) n -> p c (x n)", x=2) for t in (a, b) for k in range(2)]
    W1, W2 = slots(m.QA, m.QB), slots(m.KA, m.KBS)
    DG, DW, XE = m.KF, m.V, m.CT[:, 0, :]
    HT = m.PB[:, :, :, :].rearrange("p a b (c n) -> p (a b c) n", n=P)
    HS = HT[:, 0:4 * NF, :]
    EX = m.MI[:, :, :].bitcast(F32)
    HR = m.MB
    DGT, Y = m.CT[:, 1, :], m.CT[:, 2, :]
    B = raised(nc, m, True)
    with nc.Block() as block:
        @block.sync
        def _(sp):
            nr = sp.value_load(m.CTL[0:1, C_NR:C_NR + 1], min_val=0, max_val=NR)
            with sp.Fori(0, NR) as i:
                with sp.If(i < nr):
                    e = sp.value_load(m.CTL[0:1, bass.ds(i + C_E, 1)], min_val=0, max_val=E - 1)
                    for k in range(NF):
                        wait_alone(sp, hp, i * NF + B)
                        sp.dma_start(W1[k], m.d[w1][bass.ds(e, 1), :, k * KB:(k + 1) * KB].rearrange("a (c p) n -> p (a c) n", p=P)).then_inc(l1[k], 16)
                    for k in range(NF):
                        wait_alone(sp, u1, i * NF + B)
                        sp.dma_start(W2[k], m.d[w2][bass.ds(e, 1), k * KB:(k + 1) * KB, :].rearrange("a (c p) n -> p (a c) n", p=P)).then_inc(l2[k], 16)

        @block.vector
        def _(dve):
            v = nc.vector
            nr = dve.value_load(m.CTL[0:1, C_NR:C_NR + 1], min_val=0, max_val=NR)
            with dve.Fori(0, NR) as i:
                with dve.If(i < nr):
                    dve.wait_ge(xe, i + B)
                    dve.wait_ge(tr, i + B)
                    dve.wait_ge(gc, i + B)
                    dve.wait_ge(xa, i * NQ + B)
                    for q in range(NQ):
                        v.tensor_scalar(DG[:, q, 0:P], m.ramp[:, :], m.GS[:, 2 * q:2 * q + 1], None, ALU.is_equal)
                        v.tensor_scalar(DG[:, q, P:2 * P], m.ramp[:, :], m.GS[:, 2 * q + 1:2 * q + 2], None, ALU.is_equal)
                        v.tensor_scalar(DW[:, q, 0:P], m.ramp[:, :], m.GS[:, 2 * q:2 * q + 1], m.GW[:, 2 * q:2 * q + 1],
                                        ALU.is_equal, ALU.mult)
                        last = v.tensor_scalar(DW[:, q, P:2 * P], m.ramp[:, :], m.GS[:, 2 * q + 1:2 * q + 2],
                                               m.GW[:, 2 * q + 1:2 * q + 2], ALU.is_equal, ALU.mult)
                    last.then_inc(dd, 1)
                    dve.wait_ge(dd, i * 3 + 1 + B)
                    v.tensor_tensor(DG[:, :, 2 * P:3 * P], DG[:, :, 0:P], DG[:, :, P:2 * P], ALU.add).then_inc(dd, 1)
                    v.tensor_tensor(DW[:, :, 2 * P:3 * P], DW[:, :, 0:P], DW[:, :, P:2 * P], ALU.add).then_inc(dd, 1)
                    v.tensor_scalar(m.GS[:, :], m.GS[:, :], float(P), None, ALU.subtract).then_inc(gc, 1)
                    dve.wait_ge(xe, i + 1 + B)
                    v.tensor_copy(XE, m.bank[0][:, :]).then_inc(xs, 1)
                    dve.wait_ge(tr, i + 1 + B)
                    v.tensor_copy(DGT, m.bank[1][:, :]).then_inc(tc, 1)
                    for k in range(NF):
                        hb = m.bank[2 + k % 2][:, :]
                        out = HS[:, 4 * k:4 * k + 4, :].rearrange("p a n -> p (a n)")
                        if relu2:
                            dve.wait_ge(hp, i * NF + k + 1 + B)
                            v.tensor_scalar(HR[:, k, :], hb, 0.0, None, ALU.max).then_inc(ex, 1)
                            dve.wait_ge(ex, i * NF + k + 1 + B)
                            v.tensor_tensor(out, HR[:, k, :], HR[:, k, :], ALU.mult).then_inc(hs, 1)
                        else:
                            dve.wait_ge(ex, i * NF + k + 1 + B)
                            v.tensor_tensor(out, EX[:, k, :], hb, ALU.mult).then_inc(hs, 1)
                    dve.wait_ge(u1, (i + 1) * NF + B)
                    v.tensor_copy(Y, m.bank[0][:, :]).then_inc(yo, 1)
                    for q in range(NQ):
                        dve.wait_ge(sc, i * NQ + q + 1 + B)
                        v.tensor_tensor(m.X[:, q, :], m.X[:, q, :], m.bank[4 + q][:, :], ALU.add).then_inc(xa, 1)
            wait_alone(dve, xa, nr * NQ + B)

        @block.scalar
        def _(act):
            if relu2:
                return
            nr = act.value_load(m.CTL[0:1, C_NR:C_NR + 1], min_val=0, max_val=NR)
            with act.Fori(0, NR) as i:
                with act.If(i < nr):
                    for k in range(NF):
                        act.wait_ge(hp, i * NF + k + 1 + B)
                        nc.scalar.activation(EX[:, k, :], m.bank[2 + k % 2][:, :], ACT.Sigmoid).then_inc(ex, 1)

        @block.tensor
        def _(pe):
            t = nc.tensor
            nr = pe.value_load(m.CTL[0:1, C_NR:C_NR + 1], min_val=0, max_val=NR)
            with pe.Fori(0, NR) as i:
                with pe.If(i < nr):
                    pe.wait_ge(dd, i * 3 + 3 + B)
                    pe.wait_ge(yo, i + B)
                    for d in range(DC):
                        for q in range(NQ):
                            last = t.matmul(m.bank[0][:, d * P:(d + 1) * P], m.XN[:, q, d * P:(d + 1) * P],
                                            DG[:, q, 2 * P:3 * P], start=q == 0, stop=q == NQ - 1)
                    last.then_inc(xe, 1)
                    pe.wait_ge(tc, i + B)
                    for q in range(NQ):
                        last = t.transpose(m.bank[1][:, q * P:(q + 1) * P], DW[:, q, 2 * P:3 * P], m.ident[:, :])
                    last.then_inc(tr, 1)
                    pe.wait_ge(xs, i + 1 + B)
                    for k in range(NF):
                        pe.wait_ge(l1[k], i * 16 + 16 + B)
                        pe.wait_ge(hs, i * NF + max(0, k - 1) + B)
                        for f in range(4):
                            for d in range(DC):
                                last = t.matmul(m.bank[2 + k % 2][:, f * P:(f + 1) * P], W1[k][:, d, f * P:(f + 1) * P],
                                                XE[:, d * P:(d + 1) * P], start=d == 0, stop=d == DC - 1)
                        last.then_inc(hp, 1)
                    for k in range(NF):
                        pe.wait_ge(l2[k], i * 16 + 16 + B)
                        pe.wait_ge(hs, i * NF + k + 1 + B)
                        for f in range(4):
                            last = t.matmul(m.bank[0][:, :], HS[:, 4 * k + f, :], W2[k][:, f, :],
                                            start=k + f == 0, stop=(k == NF - 1 and f == 3))
                        last.then_inc(u1, 1)
                    pe.wait_ge(yo, i + 1 + B)
                    pe.wait_ge(tc, i + 1 + B)
                    for q in range(NQ):
                        pe.wait_ge(xa, i * NQ + B)
                        t.matmul(m.bank[4 + q][:, :], DGT[:, q * P:(q + 1) * P], Y, start=True, stop=True).then_inc(sc, 1)


def build(nc, d, out):
    with ExitStack() as ctx:
        m = Chip()
        m.d = d
        m.mark = {}

        def sb(name, shape, dt=F32):
            return ctx.enter_context(nc.sbuf_tensor(name, shape, dt))

        m.open_sems, m.fresh = [], []

        def sem(name):
            m.open_sems.append(nc.alloc_semaphore(name=name))
            m.fresh.append(m.open_sems[-1])
            return m.open_sems[-1]

        def layer_done():
            nc.clear_and_free_semaphores(m.open_sems)
            nc.all_engine_barrier()
            m.open_sems = []

        m.sem = sem
        m.X, m.XN, m.XNT = sb("X", [P, NQ, D]), sb("XN", [P, NQ, D]), sb("XNT", [P, DC, T])
        m.QA, m.QB, m.KA, m.KBS = (sb(x, [P, H, T], BF16) for x in ("QA", "QB", "KA", "KBS"))
        m.KF, m.CT, m.V = sb("KF", [P, DC, KB]), sb("CT", [P, DC, KB]), sb("V", [P, KT_, D])
        m.PB, m.PS = sb("PB", [P, 2, G, T]), sb("PS", [P, G, T])
        m.ACC = sb("ACC", [P, 2, DC, T])
        m.OACC, m.DACC = m.ACC[:, 0], m.ACC[:, 1]
        m.PARTS = m.ACC[:, :, :, :].bitcast(BF16).rearrange("p a c n -> p (a c n)")[:, 0:3 * DC * KB].rearrange(
            "p (j c n) -> p j c n", j=3, c=DC)
        m.JUNK = m.PS[:, 0:2, :].bitcast(BF16).rearrange("p a (b n) -> p (a b) n", n=KB)
        m.COUNT = m.KBS[:, :, :].bitcast(I32).rearrange("p (a b) n -> p a (b n)", a=2).rearrange("p a (b n) -> p a b n", n=KB)
        m.WQ, m.WK, m.WV = (sb(x, [P, DC, D]) for x in ("WQ", "WK", "WV"))
        m.MASK = sb("MASK", [P, 2, NQ, KB])
        m.MI, m.MB = m.MASK[:, 0].bitcast(I32), m.MASK[:, 1]
        m.MBK = m.MASK[:, 1, 0:2, :].bitcast(BF16).rearrange("p a (b n) -> p (a b) n", n=KB)
        m.MBF = m.MASK[:, :, :, :].bitcast(BF16).rearrange("p a c n -> p (a c n)")[:, 0:3 * KT_ * T].rearrange(
            "p (j c n) -> p j c n", j=3, c=KT_)
        m.RAROW, m.RNROW, m.RAROWS = sb("RAROW", [P, T]), sb("RNROW", [P, T]), sb("RAROWS", [P, T])
        m.NM, m.NMX = m.KF[0:3 * H, 0, :].bitcast(BF16)[:, 0:T], m.KF[:, 1, 0:NQ * 3 * H]
        m.CON, m.VT = sb("CON", [P, len(CONST), P]), sb("VT", [P, len(VEC), 4])
        m.IDB = sb("IDB", [P, P], BF16)
        m.KMW, m.KBIAS = sb("KM", [P, KB // 4], I32), sb("KBIAS", [P, KT_])
        m.KM = m.KMW[:, :].bitcast(U8)
        m.MX, m.MXB = sb("MX", [P, H * NQ]), sb("MXB", [P, H * NQ], BF16)
        m.RA, m.RN, m.WR = sb("RA", [P, NQ]), sb("RN", [P, NQ]), sb("WR", [P, DC, E])
        m.GS, m.GW = sb("GS", [P, 2 * NQ]), sb("GW", [P, 2 * NQ])
        m.UNMASKED = sb("UNMASKED", [P, NQ, NB])
        m.EPS, m.MINUS1 = sb("EPS", [P, 1]), sb("MINUS1", [P, 1])
        m.RSTD = m.RAROWS[0:H, :]
        m.small, m.CTL = sb("small", [P, 264]), sb("CTL", [1, 96], I32)
        tiles = {k: m.CON[:, i, :] for i, k in enumerate(CONST)}
        m.ident, m.gmean, m.before, m.upto, m.ones, m.ramp, m.index, m.head_mean = (tiles[k] for k in CONST[:8])
        m.spread = [tiles[f"spread{c}"] for c in range(DC)]
        m.vec = lambda name: m.VT[:, VEC.index(name), :]
        m.bank = [ctx.enter_context(nc.psum_tensor(f"bank{i}", [P, 512], F32)) for i in range(8)]
        m.KSAVE = nc.dram_tensor("k_saved", (NB + 1, P, 3, DC, KB), BF16, kind="Internal").ap()
        m.VSAVE = nc.dram_tensor("v_saved", (NB + 1, P, KT_, D), F32, kind="Internal").ap()
        m.QSAVE = nc.dram_tensor("q_saved", (3, P, DC, T), BF16, kind="Internal").ap()
        m.MSAVE = nc.dram_tensor("m_saved", (3 * H, T), BF16, kind="Internal").ap()

        UNWAITED[:] = [nc.alloc_semaphore(name="unwaited")]
        active_blocks(nc, m, "blocks0", None, C_N0)
        layer_done()
        attention(nc, m, Attention("L0x", "L0x_wq", "L0x_wk", "L0x_wv", "L0x_wo", 0, count=C_N0, norm=True))
        layer_done()
        attention(nc, m, Attention("L0a", "L0a_wq", "L0a_wk", "L0a_wv", "L0a_wo", 1, fixed=0))
        layer_done()
        normalise(nc, m, "L0f")
        route(nc, m, "L0f", "L0f_router", False)
        experts(nc, m, "L0f", "L0f_w1", "L0f_w2", 2048, False)
        layer_done()
        active_blocks(nc, m, "blocks1", None, C_N1, m.UNMASKED[:, :, :])
        attention(nc, m, Attention("L1x", "L1x_wq", "L1x_wk", "L1x_wv", "L1x_wo", 2, count=C_N1, row_mask=True))
        layer_done()
        attention(nc, m, Attention("L1a", "L1a_wq", "L1a_wk", "L1a_wv", "L1a_wo", 3, fixed=1))
        layer_done()
        normalise(nc, m, "L1f")
        route(nc, m, "L1f", "L1f_router", True)
        experts(nc, m, "L1f", "L1f_w1", "L1f_w2", 1024, True)
        stored = m.sem("stored")
        with nc.Block() as block:
            @block.sync
            def _(sp):
                sp.dma_start(out.rearrange("(t p) d -> p t d", p=P), m.X[:, :, :]).then_inc(stored, 16)
                sp.wait_ge(stored, 16)
        layer_done()


def laid_out(i):
    a = {k: np.asarray(v) for k, v in i.items()}
    d = {"x": a["x"][0]}
    d["ctx"] = a["ctx_1024"][0].reshape(NB, KB, DC, P).transpose(0, 3, 2, 1)
    mask = a["mask_Bx1xSxS2_ik1"][0, 0]
    d["mask_q"] = mask.reshape(NQ, P, NB, KB).transpose(2, 1, 0, 3)
    d["mask_k"] = mask.T.reshape(NB, KT_, P, T).transpose(0, 2, 1, 3)
    km = a["mask_BxS2_bk0"][0].view(np.uint8)
    d["keymask"] = km.reshape(NB, KB).view(np.int32)
    d["keymask_k"] = np.ascontiguousarray(km.reshape(NB, KT_, P).transpose(0, 2, 1)).view(np.int32)
    wkv = a["L0_xattn_Wkv"]
    d["L0x_wq"], d["L0x_wk"], d["L0x_wv"], d["L0x_wo"] = a["L0_xattn_Wq"].T, wkv[:D].T, wkv[D:].T, a["L0_xattn_Wo"].T
    w = a["L0_attn_w_qkv"]
    d["L0a_wq"], d["L0a_wk"], d["L0a_wv"], d["L0a_wo"] = w[:, :D], w[:, D:2 * D], w[:, 2 * D:], a["L0_attn_w_out"]
    for s, l in (("L1x", "L1_xattn"), ("L1a", "L1_attn")):
        for x in "qkvo":
            d[f"{s}_w{x}"] = a[f"{l}_W{x}"].T
    d["L0f_router"], d["L0f_w1"], d["L0f_w2"] = a["L0_ffn_router"], a["L0_ffn_W1"], a["L0_ffn_W2"]
    d["L1f_router"], d["L1f_w1"], d["L1f_w2"] = a["L1_ffn_Wg"], a["L1_ffn_W1"], a["L1_ffn_W2"]
    b0, ba = a["L0_xattn_bkv"], a["L0_attn_b_qkv"]
    vec = {"L0x_bq": a["L0_xattn_bq"], "L0x_bk": b0[:D], "L0x_bv": b0[D:], "L0a_bq": ba[:D], "L0a_bk": ba[D:2 * D],
           "L0a_bv": ba[2 * D:], "L1x_bq": a["L1_xattn_bq"], "L1x_bk": a["L1_xattn_bk"], "L1x_bv": a["L1_xattn_bv"],
           "zero": np.zeros(D, np.float32)}
    for x in ("qn_w", "qn_b", "kn_w", "kn_b"):
        vec[x] = np.tile(a[f"L0_xattn_{x}"], D // HD)
    d["vectors"] = np.concatenate([vec[n].reshape(DC, P).T for n in VEC], axis=1)
    d["bo"] = np.stack([np.broadcast_to(a[n], (P, D)) for n in ("L0_xattn_bo", "L0_attn_b_out", "L1_xattn_bo", "L1_attn_bo")])
    d["consts"] = consts()
    d["biases"] = fixed_biases()
    d["bias_parts"] = in_parts(d["biases"][:, 1])
    return {k: np.ascontiguousarray(v) for k, v in d.items()}


def kernel(**inputs):
    import concourse.bacc as _bacc
    from concourse.bass_utils import run_bass_kernel_spmd as _run

    nc = _bacc.Bacc("TRN2", target_bir_lowering=False, num_devices=1)
    arrays = {f"in_{k}": v for k, v in laid_out(inputs).items()}
    d = {k[3:]: nc.dram_tensor(k, v.shape, mybir.dt.from_np(v.dtype), kind="ExternalInput").ap()
         for k, v in arrays.items()}
    out = nc.dram_tensor("out", (T, D), F32, kind="ExternalOutput").ap()
    build(nc, d, out)
    r = _run(nc, [arrays], core_ids=[0])
    return np.asarray(r.results[0]["out"]).reshape(1, T, D)
```

```python
from contextlib import ExitStack

import numpy as np
import concourse.bass as bass
from concourse import mybir

F32 = mybir.dt.float32
BF16 = mybir.dt.bfloat16
I32 = mybir.dt.int32
U8 = mybir.dt.uint8
ALU = mybir.AluOpType
ACT = mybir.ActivationFunctionType
AX = mybir.AxisListType

P = 128
D = 512
T = 512
NQ = T // P
DC = D // P
H = 16
HD = D // H
G = P // HD
S2 = 8192
KB = 512
NB = S2 // KB
KT_ = KB // P
E = 8
NR = 15
SCALE = float(HD) ** -0.5
NEG = -1.0e30
LOWEST = -3.0e38
WINDOW = 32

VEC = ["L0x_bq", "L0x_bk", "L0x_bv", "L0a_bq", "L0a_bk", "L0a_bv", "L1x_bq", "L1x_bk", "L1x_bv", "zero",
       "qn_w", "qn_b", "kn_w", "kn_b"]
C_N0, C_L0, C_N1, C_L1, C_NR, C_E = 0, 1, 32, 33, 64, 65


def consts():
    p = np.arange(P)
    heads = np.zeros((P, P))
    spread = np.zeros((DC, P, P))
    for c in range(DC):
        heads[p, H * c + G * c + p // HD] = 1.0 / HD
        spread[c, G * c + p // HD, p] = 1.0
    c = {"ident": np.eye(P), "group_mean": (p[:, None] // HD == p[None, :] // HD) / HD,
         "before": (p[:, None] < p[None, :]) * 1.0, "upto": (p[:, None] <= p[None, :]) * 1.0,
         "ones": np.ones((P, P)), "ramp": np.tile(p[None, :], (P, 1)) * 1.0,
         "index": np.tile(p[:, None], (1, P)) * 1.0, "head_mean": heads,
         **{f"spread{k}": spread[k] for k in range(DC)}}
    return np.concatenate([c[k] for k in CONST], axis=1).astype(np.float32)


CONST = ["ident", "group_mean", "before", "upto", "ones", "ramp", "index", "head_mean",
         "spread0", "spread1", "spread2", "spread3"]


def fixed_biases():
    i = np.arange(T)
    later = np.where(i[None, :] >= i[:, None], 0.0, NEG)
    count = np.zeros((T, T))
    for off in range(-WINDOW, WINDOW):
        np.add.at(count, (i, np.clip(i + off, 0, T - 1)), 1.0)
    window = np.where(count > 0, np.log(np.maximum(count, 1.0)), NEG)
    out = np.zeros((2, 2, P, NQ, T), np.float32)
    for n, b in enumerate((later, window)):
        out[n, 0] = b.reshape(NQ, P, T).transpose(1, 0, 2)
        out[n, 1] = b.T.reshape(NQ, P, T).transpose(1, 0, 2)
    return out


def in_parts(a):
    bf = mybir.dt.np(BF16)
    parts = []
    for _ in range(3):
        parts.append(a.astype(bf))
        a = a - parts[-1].astype(np.float32)
    return np.stack(parts, axis=-3)


class Attention:

    def __init__(self, name, wq, wk, wv, wo, bo, fixed=None, count=None, norm=False, row_mask=False):
        self.name, self.wq, self.wk, self.wv, self.wo, self.bo = name, wq, wk, wv, wo, bo
        self.fixed = fixed
        self.count = count
        self.norm = norm
        self.row_mask = row_mask
        self.keys_of, self.queries_of = [(0, KB)] * NQ, [(0, T)] * KT_
        if fixed is not None:
            self.keys_of = [(max(0, P * q - WINDOW) if fixed else P * q, min(KB, P * q + P + WINDOW) if fixed else KB)
                            for q in range(NQ)]
            self.queries_of = [(max(0, P * k - WINDOW) if fixed else 0, min(T, P * k + P + WINDOW) if fixed else P * k + P)
                               for k in range(KT_)]
        self.order = list(range(KT_))[::-1] if fixed == 0 else list(range(KT_))
        self.bq, self.bk, self.bv = [f"{name}_b{x}" if name != "L1a" else "zero" for x in "qkv"]


class Chip:
    pass


def blocks_to_do(eng, m, L):
    if L.fixed is not None:
        return 1
    return eng.value_load(m.CTL[0:1, L.count:L.count + 1], min_val=0, max_val=NB)


UNWAITED = []


def wait_alone(eng, sem, value):
    eng.wait_ge(sem, value)
    eng.sem_inc(UNWAITED[0], 1)


def raised(nc, m, loops):
    fresh, m.fresh = m.fresh, []
    if not loops:
        return 0
    for j, sem in enumerate(fresh):
        (nc.gpsimd, nc.sync, nc.vector)[j % 3].sem_inc(sem, 1)
    nc.all_engine_barrier()
    return 1


def one(j):
    return slice(j, j + 1) if isinstance(j, int) else bass.ds(j, 1)


def first_iterations(nc, i):
    return nc.s_assert_within(i, 0, NB // 4 - 1, skip_runtime_bounds_check_because="inside If(i < NB // 4)")


def over_blocks(eng, L, n, body):
    if L.fixed is not None:
        body(0)
        return
    with eng.Fori(0, NB) as i:
        with eng.If(i < n):
            body(i)


def active_blocks(nc, m, tag, flags, count, unmasked=None):
    ch, mm, ld = m.sem(tag + "_dve"), m.sem(tag + "_pe"), m.sem(tag + "_loaded")
    F, POS, LST, RF = m.small[0:NB, 80:81], m.small[0:NB, 82:83], m.small[0:NB, 84:84 + NB], m.small[:, 116:120]
    with nc.Block() as block:
        @block.sync
        def _(sp):
            if unmasked is None:
                sp.dma_start(m.CON[:, :, :], m.d["consts"].rearrange("p (k n) -> p k n", n=P)).then_inc(ld, 16)
                sp.dma_start(m.KMW[0:NB, :], m.d["keymask"]).then_inc(ld, 16)
                sp.wait_ge(ld, 32)
                for t, src in ((m.VT[:, :, :], m.d["vectors"].rearrange("p (v c) -> p v c", c=4)),
                               (m.X[:, :, :], m.d["x"].rearrange("(t p) d -> p t d", p=P))):
                    sp.dma_start(t, src).then_inc(ld, 16)
                sp.wait_ge(ld, 64)

        @block.vector
        def _(dve):
            v = nc.vector
            k = 0
            if unmasked is None:
                v.memset(m.CTL[:, :], 0).then_inc(ch, 1)
                v.memset(m.MINUS1[:, :], -1.0).then_inc(ch, 1)
                dve.wait_ge(ld, 32)
                v.tensor_copy(m.IDB[:, :], m.ident[:, :]).then_inc(ch, 1)
                v.tensor_reduce(F, m.KM[0:NB, 0:KB], AX.X, ALU.max).then_inc(ch, 1)
                k = 4
            else:
                v.tensor_reduce(RF, unmasked, AX.X, ALU.max).then_inc(ch, 1)
                dve.wait_ge(ch, 1)
                v.tensor_scalar(m.RA[:, :], RF, 0.0, None, ALU.is_gt).then_inc(ch, 1)
                v.tensor_scalar(RF, RF, 0.0, None, ALU.is_le).then_inc(ch, 1)
                v.tensor_scalar(unmasked, unmasked, 0.0, None, ALU.is_gt).then_inc(ch, 1)
                dve.wait_ge(mm, 1)
                v.tensor_reduce(F, m.bank[0][0:NB, 0:5], AX.X, ALU.add).then_inc(ch, 1)
                v.tensor_copy(m.RAROW[:, :], m.bank[1][:, :]).then_inc(ch, 1)
                dve.wait_ge(ch, 6)
                v.tensor_scalar(m.RN[:, :], m.RA[:, :], NEG, None, ALU.mult).then_inc(ch, 1)
                v.tensor_scalar(m.RNROW[:, :], m.RAROW[:, :], NEG, None, ALU.mult).then_inc(ch, 1)
                k = 8
            dve.wait_ge(ch, k)
            v.tensor_scalar(F, F, 0.0, None, ALU.is_gt).then_inc(ch, 1)
            dve.wait_ge(mm, 1 if unmasked is None else 2)
            v.tensor_copy(POS, m.bank[2][0:NB, 0:1]).then_inc(ch, 1)
            dve.wait_ge(ch, k + 2)
            v.tensor_scalar(LST, m.ramp[0:NB, 1:NB + 1], POS, F, ALU.is_equal, ALU.mult).then_inc(ch, 1)
            dve.wait_ge(mm, 2 if unmasked is None else 3)
            v.tensor_copy(m.CTL[0:1, count:count + 1 + NB], m.bank[3][0:1, 0:1 + NB]).then_inc(ch, 1)
            dve.wait_ge(ch, k + 4)

        @block.tensor
        def _(pe):
            t = nc.tensor
            k = 5
            if unmasked is not None:
                k = 9
                pe.wait_ge(ch, 4)
                for q in range(NQ):
                    t.matmul(m.bank[0][0:NB, 0:1], unmasked[:, q, :], m.ones[:, 0:1], start=q == 0, stop=q == NQ - 1)
                for q in range(NQ):
                    t.matmul(m.bank[0][0:NB, 1 + q:2 + q], m.ones[:, 0:NB], RF[:, q:q + 1], start=False, stop=True,
                             skip_group_check=True)
                for q in range(NQ):
                    last = t.matmul(m.bank[1][:, q * P:(q + 1) * P], m.RA[:, q:q + 1].to_broadcast([P, P]), m.ident[:, :],
                                    start=True, stop=True)
                last.then_inc(mm, 1)
            else:
                pe.wait_ge(ld, 32)
            pe.wait_ge(ch, k)
            t.matmul(m.bank[2][0:NB, 0:1], m.upto[0:NB, 0:NB], F, start=True, stop=True).then_inc(mm, 1)
            pe.wait_ge(ch, k + 2)
            t.matmul(m.bank[3][0:1, 0:1], m.ones[0:NB, 0:1], F, start=True, stop=True)
            t.matmul(m.bank[3][0:1, 1:1 + NB], m.index[0:NB, 0:1], LST, start=True, stop=True).then_inc(mm, 1)


def normalise(nc, m, tag, L=None):
    ch, sq, tr, ev = m.sem(tag + "_ln"), m.sem(tag + "_ln_sqrt"), m.sem(tag + "_ln_tr"), m.sem(tag + "_ln_xnt")
    ST, MV, SD = m.small[:, 0:24], m.small[:, 24:32], m.small[:, 32:36]
    if L is not None:
        m.wq_loaded, m.wkv_loaded = m.sem(tag + "_wq"), m.sem(tag + "_wkv")
    with nc.Block() as block:
        @block.sync
        def _(sp):
            if L is not None:
                for t, src, sem in ((m.WQ, L.wq, m.wq_loaded), (m.WK, L.wk, m.wkv_loaded), (m.WV, L.wv, m.wkv_loaded)):
                    sp.dma_start(t[:, :, :], m.d[src].rearrange("(c p) n -> p c n", p=P)).then_inc(sem, 16)

        @block.vector
        def _(dve):
            v = nc.vector
            for t in range(NQ):
                v.bn_stats(ST[:, 6 * t:6 * t + 6], m.X[:, t, :]).then_inc(ch, 1)
            dve.wait_ge(ch, 4)
            for t in range(NQ):
                v.bn_aggr(MV[:, 2 * t:2 * t + 2], ST[:, 6 * t:6 * t + 6]).then_inc(ch, 1)
            dve.wait_ge(ch, 8)
            v.tensor_scalar(SD, MV.rearrange("p (t k) -> p t k", k=2)[:, :, 1], 1e-5, None, ALU.add).then_inc(ch, 1)
            dve.wait_ge(sq, 1)
            v.reciprocal(SD, SD).then_inc(ch, 1)
            dve.wait_ge(ch, 10)
            for t in range(NQ):
                v.tensor_scalar(m.XN[:, t, :], m.X[:, t, :], MV[:, 2 * t:2 * t + 1], SD[:, t:t + 1],
                                ALU.subtract, ALU.mult).then_inc(ch, 1)
            for c in (0, 2):
                dve.wait_ge(tr, c + 1)
                v.tensor_copy(m.XNT[:, c, :], m.bank[c][:, :]).then_inc(ev, 1)

        @block.scalar
        def _(act):
            act.wait_ge(ch, 9)
            nc.scalar.activation(SD, SD, ACT.Sqrt).then_inc(sq, 1)
            for c in (1, 3):
                act.wait_ge(tr, c + 1)
                nc.scalar.activation(m.XNT[:, c, :], m.bank[c][:, :], ACT.Copy).then_inc(ev, 1)
            act.wait_ge(ev, DC)

        @block.tensor
        def _(pe):
            pe.wait_ge(ch, 14)
            for c in range(DC):
                for t in range(NQ):
                    last = nc.tensor.transpose(m.bank[c][:, t * P:(t + 1) * P], m.XN[:, t, c * P:(c + 1) * P], m.ident[:, :])
                last.then_inc(tr, 1)


def centre(nc, m, dve, W, ch, k):
    v = nc.vector
    Wg = W[:, :, :].rearrange("p c (h f) -> p (c h) f", f=HD)
    MW = m.small[:, 0:DC * H]
    v.tensor_reduce(MW, Wg, AX.X, ALU.add).then_inc(ch, 1)
    dve.wait_ge(ch, k + 1)
    v.tensor_scalar(MW, MW, 1.0 / HD, None, ALU.mult).then_inc(ch, 1)
    dve.wait_ge(ch, k + 2)
    v.tensor_tensor(Wg, Wg, MW.unsqueeze(2).to_broadcast([P, DC * H, HD]), ALU.subtract).then_inc(ch, 1)
    return k + 3


def queries(nc, m, L):
    n = L.name
    z, ch, pj = m.sem(n + "_zeroed"), m.sem(n + "_q_dve"), m.sem(n + "_q_pe")
    sq, va, p1, r1 = m.sem(n + "_q_sq"), m.sem(n + "_q_var"), m.sem(n + "_q_part1"), m.sem(n + "_q_rest1")
    p2, p3, st, qf = m.sem(n + "_q_part2"), m.sem(n + "_q_part3"), m.sem(n + "_q_stored"), m.sem(n + "_q_full")
    ql = m.q_loaded = m.sem(n + "_q_stacks")
    QF = m.XN
    CENTRED_Q, CENTRED_K, BIASES, INVERTED, SCALED = 5, 8, 13, 14, 18

    class Parts:
        read_out = ch if L.norm else qf
        read_out_at = SCALED if L.norm else DC
        keys_ready = CENTRED_K

        @staticmethod
        def sync(sp):
            for c in range(DC):
                sp.wait_ge(p3, c + 1)
                for j in range(3):
                    sp.dma_start(m.QSAVE[j, :, c, :], m.QP[j][:, c, :]).then_inc(st, 16)
            sp.wait_ge(z, 1)
            for c in range(DC):
                sp.wait_ge(st, 16 * 3 * DC)
                for stack, parts in ((m.QA, (0, 1, 0)), (m.QB, (1, 2, 0))):
                    for j, part in enumerate(parts):
                        sp.dma_start(stack[HD * j:HD * j + HD, G * c:G * c + G, :],
                                     m.QSAVE[part, :, c, :].rearrange("(g f) n -> f g n", f=HD)).then_inc(ql, 16)

        @staticmethod
        def gpsimd(pool):
            g = nc.gpsimd
            g.memset(m.QB[3 * HD:P, :, :], 0.0).then_inc(z, 1)
            pool.wait_ge(z, 1)
            for c in range(DC + 1):
                if c < DC:
                    pool.wait_ge(p1, c + 1)
                    g.tensor_tensor(QF[:, c, :], QF[:, c, :], m.QP[0][:, c, :], ALU.subtract).then_inc(r1, 1)
                if c:
                    pool.wait_ge(p2, c)
                    g.tensor_tensor(m.QP[2][:, c - 1, :], QF[:, c - 1, :], m.QP[1][:, c - 1, :], ALU.subtract).then_inc(p3, 1)

        @staticmethod
        def vector(dve):
            v = nc.vector
            v.memset(m.MX[:, :], LOWEST).then_inc(ch, 1)
            k = 2
            if L.norm:
                v.memset(m.RSTDS[:, :], 0.0).then_inc(ch, 1)
                dve.wait_ge(m.wq_loaded, 16)
                k = centre(nc, m, dve, m.WQ, ch, k)
                dve.wait_ge(m.wkv_loaded, 32)
                dve.wait_ge(ch, k)
                k = centre(nc, m, dve, m.WK, ch, k)
                dve.wait_ge(pj, 1)
                for j, b in enumerate((L.bq, L.bk)):
                    v.tensor_tensor(m.vec(b), m.vec(b), m.bank[7][:, 4 * j:4 * j + 4], ALU.subtract).then_inc(ch, 1)
                for b in ("qn_w", "qn_b"):
                    v.tensor_scalar(m.vec(b), m.vec(b), SCALE, None, ALU.mult).then_inc(ch, 1)
                v.memset(m.EPS[:, :], 1e-6).then_inc(ch, 1)
                k += 5
                dve.wait_ge(sq, 9)
                v.reciprocal(m.RSTD[:, :], m.RSTD[:, :]).then_inc(ch, 1)
                for c in range(DC):
                    dve.wait_ge(va, c + 2)
                    v.tensor_tensor(QF[:, c, :], QF[:, c, :], m.bank[2 + c][:, :], ALU.mult).then_inc(ch, 1)
            else:
                if not L.row_mask:
                    v.memset(m.RAROWS[:, :], SCALE).then_inc(ch, 1)
                else:
                    v.tensor_scalar(m.RAROWS[:, :], m.RAROW[:, :], SCALE, None, ALU.mult).then_inc(ch, 1)
                dve.wait_ge(ch, 2)
                for c in range(DC):
                    dve.wait_ge(pj, c + 1)
                    v.scalar_tensor_tensor(QF[:, c, :], m.bank[c % 2][:, :], m.vec(L.bq)[:, c:c + 1],
                                           m.RAROWS[:, :], ALU.add, ALU.mult).then_inc(qf, 1)

        @staticmethod
        def scalar(act):
            a = nc.scalar
            if L.norm:
                act.wait_ge(ch, BIASES)
                for c in range(DC):
                    act.wait_ge(pj, c + 2)
                    b = m.vec(L.bq)[:, c:c + 1]
                    a.activation(m.PB[:, 0, c, :], m.bank[c % 2][:, :], ACT.Square, bias=b).then_inc(sq, 1)
                    a.activation(QF[:, c, :], m.bank[c % 2][:, :], ACT.Identity, bias=b).then_inc(sq, 1)
                act.wait_ge(va, 1)
                a.activation(m.RSTD[:, :], m.bank[6][0:H, :], ACT.Sqrt, bias=m.EPS[0:H, :]).then_inc(sq, 1)
                for c in range(DC):
                    act.wait_ge(ch, INVERTED + c + 1)
                    a.activation(QF[:, c, :], QF[:, c, :], ACT.Identity, bias=m.vec("qn_b")[:, 0:1],
                                 scale=m.vec("qn_w")[:, 0:1]).then_inc(qf, 1)
            for c in range(DC + 1):
                if c < DC:
                    act.wait_ge(qf, c + 1)
                    a.activation(m.QP[0][:, c, :], QF[:, c, :], ACT.Copy).then_inc(p1, 1)
                if c:
                    act.wait_ge(r1, c)
                    a.activation(m.QP[1][:, c - 1, :], QF[:, c - 1, :], ACT.Copy).then_inc(p2, 1)

        @staticmethod
        def tensor(pe):
            t = nc.tensor
            pe.wait_ge(m.wq_loaded, 16)
            if L.norm:
                for j, b in enumerate((L.bq, L.bk)):
                    last = t.matmul(m.bank[7][:, 4 * j:4 * j + 4], m.gmean[:, :], m.vec(b), start=True, stop=True)
                last.then_inc(pj, 1)
                pe.wait_ge(ch, CENTRED_Q)
            for c in range(DC):
                if c >= 2:
                    pe.wait_ge(sq if L.norm else qf, 2 * (c - 1) if L.norm else c - 1)
                for d in range(DC):
                    last = t.matmul(m.bank[c % 2][:, :], m.WQ[:, d, c * P:(c + 1) * P], m.XNT[:, d, :],
                                    start=d == 0, stop=d == DC - 1)
                last.then_inc(pj, 1)
            if L.norm:
                pe.wait_ge(sq, 8)
                for c in range(DC):
                    last = t.matmul(m.bank[6][0:H, :], m.head_mean[:, H * c:H * c + H], m.PB[:, 0, c, :],
                                    start=c == 0, stop=c == DC - 1)
                last.then_inc(va, 1)
                pe.wait_ge(ch, INVERTED)
                for c in range(DC):
                    t.matmul(m.bank[2 + c][:, :], m.spread[c][:, :], m.RSTDS[:, :], start=True, stop=True).then_inc(va, 1)

    return Parts


def row_maxima(nc, m, L):
    Q = queries(nc, m, L)
    m.fresh = []
    n = L.name + "_max"
    ld = [m.sem(f"{n}_ctx{kb}") for kb in range(KT_)]
    lm, pj, sq, ve = m.sem(n + "_mask"), m.sem(n + "_proj"), m.sem(n + "_sq"), m.sem(n + "_v")
    sc, mx, bi = m.sem(n + "_scores"), m.sem(n + "_taken"), m.sem(n + "_bias")
    p1, r1, p2, p3 = m.sem(n + "_part1"), m.sem(n + "_rest1"), m.sem(n + "_part2"), m.sem(n + "_part3")
    sv, va, sd, rs, kn, kf = (m.sem(n + x) for x in ("_vstored", "_var", "_std", "_rstd", "_knorm", "_kfull"))
    la = [m.sem(f"{n}_stack{c}") for c in range(DC)]
    sk = [m.sem(f"{n}_kstored{c}") for c in range(DC)]
    cl, cc = [m.sem(f"{n}_count_mask{u}") for u in range(4)], m.sem(n + "_counted")
    NS = H * NQ
    dyn = L.fixed is None
    src = m.CT if dyn else m.XNT
    counting = L.norm
    K_AT = list(range(4, 36, 2))
    VAR_AT, INVERSE_AT, SPREAD_AT, SCALE_AT = 36, 43, [46, 50, 54, 58], [48, 52, 56, 60]
    V_AT = [40, 41, 42, 43, 45, 47, 48, 49, 51, 52, 53, 55, 56, 57, 59, 60] if L.norm else \
        [35, 37, 39, 40, 42, 44, 46, 47, 49, 51, 53, 54, 56, 58, 60, 61]
    STORES = "x0 x1 k0 x2 k1 s0 x3 k2 s1 v k3 s2 s3" if L.norm else "k0 k1 s0 k2 k3 s1 x0 x1 s2 x2 x3 v s3"
    B = raised(nc, m, dyn)

    with nc.Block() as block:
        @block.sync
        def _(sp):
            nb = blocks_to_do(sp, m, L)

            def load_context(j, kb):
                b = sp.value_load(m.CTL[0:1, (bass.ds(j + (L.count + 1), 1) if not isinstance(j, int) else slice(j + L.count + 1, j + L.count + 2))],
                                  min_val=0, max_val=NB - 1)
                sp.dma_start(m.CT[:, :, kb * P:(kb + 1) * P],
                             m.d["ctx"][bass.ds(b, 1), :, :, kb * P:(kb + 1) * P].rearrange("a p c k -> (a p) c k")).then_inc(ld[kb], 16)

            def load_mask(j):
                b = sp.value_load(m.CTL[0:1, (bass.ds(j + (L.count + 1), 1) if not isinstance(j, int) else slice(j + L.count + 1, j + L.count + 2))],
                                  min_val=0, max_val=NB - 1)
                if L.row_mask:
                    sp.dma_start(m.MI[:, :, :], m.d["mask_q"][bass.ds(b, 1)].rearrange("a p t k -> (a p) t k")).then_inc(lm, 16)
                else:
                    sp.dma_start(m.KMW[:, :], m.d["keymask"][bass.ds(b, 1)].to_broadcast([P, KB // 4])).then_inc(lm, 16)

            def keep_keys(j, c):
                wait_alone(sp, p3, j * DC + c + 1 + B)
                sp.dma_start(m.KSAVE[one(j), :, :, c, :].rearrange("a p k n -> (a p) k n"), m.PARTS[:, :, c, :]).then_inc(sk[c], 16)

            def keep_values(j):
                wait_alone(sp, ve, j * KT_ + KT_ + B)
                sp.dma_start(m.VSAVE[one(j)].rearrange("a p k n -> (a p) k n"), m.V[:, :, :]).then_inc(sv, 16)

            def stack(j, c):
                wait_alone(sp, sk[c], j * 16 + 16 + B)
                for r, part in enumerate((0, 0, 1)):
                    sp.dma_start(m.KA[HD * r:HD * r + HD, G * c:G * c + G, :],
                                 m.KSAVE[one(j), :, part, c, :].rearrange("a (g f) n -> (a f) g n", f=HD)).then_inc(la[c], 16)

            if dyn:
                for kb in range(KT_):
                    load_context(0, kb)
                load_mask(0)
            else:
                sp.dma_start(m.MB[:, :, :], m.d["biases"][L.fixed, 0]).then_inc(lm, 16)
            Q.sync(sp)
            for c in range(DC):
                keep_keys(0, c)
                if c:
                    stack(0, c - 1)
            stack(0, DC - 1)
            if dyn:
                wait_alone(sp, pj, 2 * DC + B)
                for kb in range(KT_):
                    load_context(1, kb)
            keep_values(0)
            if not dyn:
                sp.wait_ge(sv, 16)
                return

            with sp.Fori(0, NB) as i:
                if counting:
                    with sp.If(i < NB // 4):
                        i4 = first_iterations(nc, i)
                        wait_alone(sp, cc, i * 4 * NQ + B)
                        for u in range(4):
                            sp.dma_start(m.COUNT[u], m.d["mask_q"][bass.ds(i4 * 4 + u, 1)].rearrange("a p t k -> (a p) t k")).then_inc(cl[u], 16)
                with sp.If(i < nb):
                    wait_alone(sp, bi, i + 1 + B)
                    load_mask(i + 1)

                    for step in STORES.split():
                        c = int(step[1:] or 0)
                        if step[0] == "k":
                            keep_keys(i + 1, c)
                        elif step[0] == "s":
                            wait_alone(sp, mx, i * NS + (c + 1) * G * NQ + B)
                            stack(i + 1, c)
                        elif step[0] == "x":
                            wait_alone(sp, pj, i * (2 * DC) + 3 * DC + c + 1 + B)
                            load_context(i + 2, c)
                        else:
                            keep_values(i + 1)
            wait_alone(sp, sv, nb * 16 + 16 + B)
            m.past = (la, [(lm, 16)] + [(s, 32) for s in ld])

        @block.tensor
        def _(pe):
            nb = blocks_to_do(pe, m, L)
            t = nc.tensor

            def project_keys(j, x, d):
                if x == 0 and d == 0 and dyn:
                    for kb in range(KT_):
                        pe.wait_ge(ld[kb], j * 16 + 16 + B)
                if d == 0:
                    pe.wait_ge(sq, j * (2 * DC) + max(0, x - 1) * 2 + B)
                last = t.matmul(m.bank[x % 2][:, :], m.WK[:, d, x * P:(x + 1) * P], src[:, d, :],
                                start=d == 0, stop=d == DC - 1)
                if d == DC - 1:
                    last.then_inc(pj, 1)

            def variances(j):
                pe.wait_ge(sq, j * (2 * DC) + 2 * DC + B)
                pe.wait_ge(kn, j * DC + B)
                for d in range(DC):
                    last = t.matmul(m.bank[3][0:H, :], m.head_mean[:, H * d:H * d + H], m.PB[:, 0, d, :],
                                    start=d == 0, stop=d == DC - 1)
                last.then_inc(va, 1)

            def project_values(j, kb, d):
                if d == 0:
                    pe.wait_ge(ve, j * KT_ + kb + B)
                last = t.matmul(m.bank[2][:, :], src[:, d, kb * P:(kb + 1) * P], m.WV[:, d, :],
                                start=d == 0, stop=d == DC - 1)
                if d == DC - 1:
                    last.then_inc(pj, 1)

            def spread(j, c):
                pe.wait_ge(rs, j + 1 + B)
                pe.wait_ge(kn, j * DC + c + B)
                t.matmul(m.bank[3][:, :], m.spread[c][:, :], m.RSTDS[:, :], start=True, stop=True).then_inc(va, 1)

            def scores(i, ahead):
                for k in range(NS):
                    h, q = k // NQ, k % NQ
                    k0, k1 = L.keys_of[q]
                    if k % (G * NQ) == 0:
                        pe.wait_ge(la[h // G], i * 48 + 48 + B)
                    pe.wait_ge(mx, i * NS + max(0, k - 3) + B)
                    t.matmul(m.bank[4 + k % 4][:, k0:k1], m.QA[0:3 * HD, h, q * P:(q + 1) * P], m.KA[0:3 * HD, h, k0:k1],
                             start=True, stop=True).then_inc(sc, 1)
                    if ahead and k in K_AT:
                        project_keys(i + 1, K_AT.index(k) // DC, K_AT.index(k) % DC)
                    if ahead and L.norm and k == VAR_AT:
                        variances(i + 1)
                    if ahead and L.norm and k in SPREAD_AT:
                        spread(i + 1, SPREAD_AT.index(k))
                    if ahead and k in V_AT:
                        project_values(i + 1, V_AT.index(k) // DC, V_AT.index(k) % DC)

            Q.tensor(pe)
            pe.wait_ge(m.wkv_loaded, 32)
            if L.norm:
                pe.wait_ge(Q.read_out, Q.keys_ready)
            else:
                pe.wait_ge(Q.read_out, Q.read_out_at)
            for x in range(DC):
                for d in range(DC):
                    project_keys(0, x, d)
            pe.wait_ge(Q.read_out, Q.read_out_at)
            if L.norm:
                variances(0)
            for kb in range(KT_):
                for d in range(DC):
                    project_values(0, kb, d)
                if L.norm:
                    spread(0, kb)
            pe.wait_ge(m.q_loaded, 16 * 3 * 2 * DC)
            if not dyn:
                scores(0, False)
                return
            with pe.Fori(0, NB) as i:
                with pe.If(i < nb):
                    scores(i, True)

        @block.scalar
        def _(act):
            nb = blocks_to_do(act, m, L)
            a = nc.scalar

            def count(i, u):
                act.wait_ge(cl[u], i * 16 + 16 + B)
                for q in range(NQ):
                    a.activation(m.COUNT[u][:, q, :], m.COUNT[u][:, q, :], ACT.Square, bias=m.MINUS1[:, :],
                                 accum_out=m.UNMASKED[:, q, bass.ds(i * 4 + u, 1)]).then_inc(cc, 1)

            def evacuate(j):
                def second(c):
                    act.wait_ge(r1, j * DC + c + 1 + B)
                    a.activation(m.PARTS[:, 1, c, :], m.KF[:, c, :], ACT.Copy).then_inc(p2, 1)

                def values(kb):
                    act.wait_ge(pj, j * (2 * DC) + DC + kb + 1 + B)
                    a.activation(m.V[:, kb, :], m.bank[2][:, :], ACT.Copy).then_inc(ve, 1)

                for c in range(DC):
                    act.wait_ge(sk[c], j * 16 + B)
                    act.wait_ge(pj, j * (2 * DC) + c + 1 + B)
                    b = m.vec(L.bk)[:, c:c + 1]
                    if L.norm:
                        a.activation(m.PB[:, 0, c, :], m.bank[c % 2][:, :], ACT.Square, bias=b).then_inc(sq, 1)
                        a.activation(m.KF[:, c, :], m.bank[c % 2][:, :], ACT.Identity, bias=b).then_inc(sq, 1)
                    else:
                        a.activation(m.KF[:, c, :], m.bank[c % 2][:, :], ACT.Identity, bias=b).then_inc(sq, 1)
                        a.activation(m.PARTS[:, 0, c, :], m.bank[c % 2][:, :], ACT.Identity, bias=b).then_inc(sq, 1)
                        if c:
                            second(c - 1)
                if L.norm:
                    act.wait_ge(va, j * 5 + 1 + B)
                    a.activation(m.RSTD[:, :], m.bank[3][0:H, :], ACT.Sqrt, bias=m.EPS[0:H, :]).then_inc(sd, 1)
                act.wait_ge(sv, j * 16 + B)
                for kb in range(KT_):
                    values(kb)
                    if L.norm:
                        act.wait_ge(kn, j * DC + kb + 1 + B)
                        a.activation(m.KF[:, kb, :], m.KF[:, kb, :], ACT.Identity, bias=m.vec("kn_b")[:, 0:1],
                                     scale=m.vec("kn_w")[:, 0:1]).then_inc(kf, 1)
                        act.wait_ge(kf, j * DC + kb + 1 + B)
                        a.activation(m.PARTS[:, 0, kb, :], m.KF[:, kb, :], ACT.Copy).then_inc(p1, 1)
                        if kb:
                            second(kb - 1)
                    elif kb == 0:
                        second(DC - 1)
                if L.norm:
                    second(DC - 1)

            Q.scalar(act)
            evacuate(0)
            if not dyn:
                return
            with act.Fori(0, NB) as i:
                with act.If(i < nb):
                    evacuate(i + 1)
                if counting:
                    with act.If(i < NB // 4):
                        i4 = first_iterations(nc, i)
                        for u in range(4):
                            count(i4, u)
            if counting:
                act.wait_ge(cc, NB * NQ + B)

        @block.gpsimd
        def _(pool):
            nb = blocks_to_do(pool, m, L)
            g = nc.gpsimd

            def split(j):
                for c in range(DC + 1):
                    if c < DC:
                        if L.norm:
                            pool.wait_ge(p1, j * DC + c + 1 + B)
                        else:
                            pool.wait_ge(sq, j * (2 * DC) + 2 * c + 2 + B)
                        g.tensor_tensor(m.KF[:, c, :], m.KF[:, c, :], m.PARTS[:, 0, c, :], ALU.subtract).then_inc(r1, 1)
                    if c:
                        pool.wait_ge(p2, j * DC + c + B)
                        g.tensor_tensor(m.PARTS[:, 2, c - 1, :], m.KF[:, c - 1, :], m.PARTS[:, 1, c - 1, :],
                                        ALU.subtract).then_inc(p3, 1)

            Q.gpsimd(pool)
            split(0)
            if not dyn:
                return
            with pool.Fori(0, NB) as i:
                with pool.If(i < nb):
                    split(i + 1)

        @block.vector
        def _(dve):
            nb = blocks_to_do(dve, m, L)
            v = nc.vector

            def inverse(j):
                dve.wait_ge(sd, j + 1 + B)
                v.reciprocal(m.RSTD[:, :], m.RSTD[:, :]).then_inc(rs, 1)

            def scale(j, c):
                dve.wait_ge(va, j * 5 + 2 + c + B)
                v.tensor_tensor(m.KF[:, c, :], m.KF[:, c, :], m.bank[3][:, :], ALU.mult).then_inc(kn, 1)

            def maxima(i, ahead):
                if dyn:
                    dve.wait_ge(mx, i * NS + B)
                    dve.wait_ge(lm, i * 16 + 16 + B)
                    if L.row_mask:
                        for q in range(NQ):
                            last = v.tensor_scalar(m.MB[:, q, :], m.MI[:, q, :], 1.0, m.RN[:, q:q + 1], ALU.is_equal, ALU.mult)
                    else:
                        last = v.tensor_scalar(m.MB[:, 0, :], m.KM[:, 0:KB], 1.0, -NEG, ALU.subtract, ALU.mult)
                    last.then_inc(bi, 1)
                    dve.wait_ge(bi, i + 1 + B)
                else:
                    dve.wait_ge(lm, 16)
                for k in range(NS):
                    q = k % NQ
                    k0, k1 = L.keys_of[q]
                    bias = m.MB[:, q if (L.row_mask or not dyn) else 0, k0:k1]
                    dve.wait_ge(mx, i * NS + max(0, k - 3) + B)
                    wait_alone(dve, sc, i * NS + k + 1 + B)
                    v.tensor_tensor_reduce(m.JUNK[:, k % 4, k0:k1], m.bank[4 + k % 4][:, k0:k1], bias, 1.0, m.MX[:, k:k + 1],
                                           ALU.add, ALU.max, m.MX[:, k:k + 1]).then_inc(mx, 1)
                    if ahead and L.norm:
                        if k == INVERSE_AT:
                            inverse(i + 1)
                        if k in SCALE_AT:
                            scale(i + 1, SCALE_AT.index(k))

            Q.vector(dve)
            if L.norm:
                inverse(0)
                for c in range(DC):
                    scale(0, c)
            if not dyn:
                maxima(0, False)
                return
            with dve.Fori(0, NB) as i:
                with dve.If(i < nb):
                    maxima(i, True)


def shifts(nc, m, L):
    n = L.name
    ch, tr, st = m.sem(n + "_shift_dve"), m.sem(n + "_shift_tr"), m.sem(n + "_shift_stored")
    z = m.sem(n + "_ones")
    m.wo_loaded = m.sem(n + "_wo")
    R, PART = m.small[:, 0:64], m.MXB

    class Parts:
        zeroed, stored = z, st

        @staticmethod
        def load_output_weights(sp):
            sp.dma_start(m.WQ[:, :, :], m.d[L.wo].rearrange("(c p) n -> p c n", p=P)).then_inc(m.wo_loaded, 16)
            sp.dma_start(m.RAROWS[:, :], m.d["bo"][L.bo]).then_inc(m.wo_loaded, 16)

        @staticmethod
        def sync(sp):
            sp.wait_ge(ch, 11)
            sp.dma_start(m.MSAVE, m.NM[:, :]).then_inc(st, 16)
            sp.wait_ge(st, 16)
            sp.dma_start(m.QB[3 * HD:3 * HD + 3, :, :], m.MSAVE.rearrange("(j h) n -> j h n", h=H)).then_inc(st, 16)

        @staticmethod
        def gpsimd(pool):
            nc.gpsimd.memset(m.KBS[3 * HD:P, :, :], 1.0).then_inc(z, 1)
            pool.wait_ge(z, 1)
            nc.gpsimd.memset(m.OACC[:, :, :], 0.0).then_inc(z, 1)
            nc.gpsimd.memset(m.DACC[:, :, :], 0.0).then_inc(z, 1)

        @staticmethod
        def vector(dve):
            v = nc.vector
            v.tensor_scalar(R, m.MX[:, :], -1.0, None, ALU.mult).then_inc(ch, 1)
            k = 1
            out = m.NMX[:, :].rearrange("p (q j h) -> p j q h", q=NQ, j=3)
            for j in range(3):
                dve.wait_ge(ch, k)
                v.tensor_copy(PART[:, :], R).then_inc(ch, 1)
                dve.wait_ge(ch, k + 1)
                v.tensor_copy(out[:, j], PART[:, :].rearrange("p (h q) -> p q h", q=NQ)).then_inc(ch, 1)
                v.tensor_tensor(R, R, PART[:, :], ALU.subtract).then_inc(ch, 1)
                k += 3
            dve.wait_ge(tr, 1)
            v.tensor_copy(m.NM[:, :], m.bank[0][0:3 * H, :]).then_inc(ch, 1)

        @staticmethod
        def tensor(pe):
            pe.wait_ge(ch, 10)
            for q in range(NQ):
                last = nc.tensor.transpose(m.bank[0][0:3 * H, q * P:(q + 1) * P], m.NMX[:, q * 3 * H:(q + 1) * 3 * H], m.ident[:, :])
            last.then_inc(tr, 1)

    return Parts


def weighted_values(nc, m, L):
    M = shifts(nc, m, L)
    m.fresh = []
    n = L.name + "_pv"
    lm, sc, ex, pv, pa = (m.sem(n + x) for x in ("_mask", "_scores", "_exp", "_product", "_psum"))
    dn, oa, bi, zs = (m.sem(n + x) for x in ("_den", "_acc", "_bias", "_zeroed"))
    lk = [m.sem(f"{n}_keys{c}") for c in range(DC)]
    steps = [(c, k) for c in range(DC) for k in range(KT_)]
    NS = len(steps)
    dyn = L.fixed is None
    kt = L.order
    PER = 7 * 16
    NBI = KT_ if L.row_mask else 1
    B = raised(nc, m, dyn)
    with nc.Block() as block:
        @block.sync
        def _(sp):
            nb = blocks_to_do(sp, m, L)

            def load_mask(j):
                b = sp.value_load(m.CTL[0:1, (bass.ds(j + (L.count + 1), 1) if not isinstance(j, int) else slice(j + L.count + 1, j + L.count + 2))],
                                  min_val=0, max_val=NB - 1)
                if L.row_mask:
                    sp.dma_start(m.MI[:, :, :], m.d["mask_k"][bass.ds(b, 1)].rearrange("a p t k -> (a p) t k")).then_inc(lm, 16)
                else:
                    sp.dma_start(m.KMW[:, 0:1], m.d["keymask_k"][bass.ds(b, 1)].rearrange("a p t -> (a p) t")).then_inc(lm, 16)

            def load_keys(j, c):
                for stack, parts in ((m.KA, (0, 0, 1)), (m.KBS, (1, 0, 2))):
                    for r, part in enumerate(parts):
                        sp.dma_start(stack[HD * r:HD * r + HD, G * c:G * c + G, :],
                                     m.KSAVE[one(j), :, part, c, :].rearrange("a (g f) n -> (a f) g n", f=HD)).then_inc(lk[c], 16)
                sp.dma_start(m.V[:, :, c * P:(c + 1) * P],
                             m.VSAVE[one(j), :, :, c * P:(c + 1) * P].rearrange("a p k n -> (a p) k n")).then_inc(lk[c], 16)

            if dyn:
                load_mask(0)
            else:
                sp.dma_start(m.MBF, m.d["bias_parts"][L.fixed]).then_inc(lm, 16)
            M.sync(sp)
            if dyn:
                for sem in m.past[0]:
                    wait_alone(sp, sem, nb * 48 + 48 + B)
                for sem, more in m.past[1]:
                    wait_alone(sp, sem, nb * 16 + more + B)
            for c in range(DC):
                load_keys(0, c)
            M.load_output_weights(sp)
            if not dyn:
                return
            with sp.Fori(0, NB) as i:
                with sp.If(i < nb):
                    wait_alone(sp, bi, i * NBI + NBI + B)
                    load_mask(i + 1)
                    for c in range(DC):
                        wait_alone(sp, pv, i * NS + (c + 1) * KT_ + B)
                        load_keys(i + 1, c)
            wait_alone(sp, lm, nb * 16 + 16 + B)
            for c in range(DC):
                wait_alone(sp, lk[c], nb * PER + PER + B)

        @block.tensor
        def _(pe):
            nb = blocks_to_do(pe, m, L)
            t = nc.tensor

            def times_values(i, s):
                c, k = steps[s]
                q0, q1 = L.queries_of[kt[k]]
                if k == 0:
                    pe.wait_ge(oa, i * (2 * DC) + 2 * max(0, c - 1) + B)
                pe.wait_ge(ex, i * (NS * G) + G * s + G + B)
                for g in range(G):
                    h = G * c + g
                    last = t.matmul(m.bank[2 + c % 2][HD * g:HD * g + HD, q0:q1], m.V[:, kt[k], HD * h:HD * h + HD],
                                    m.PB[:, s % 2, g, q0:q1], start=k == 0, stop=k == KT_ - 1,
                                    skip_group_check=not dyn)
                last.then_inc(pv, 1)

            def denominators(i, c):
                pe.wait_ge(pa, i * NS + KT_ * c + KT_ + B)
                for g in range(G):
                    last = t.matmul(m.bank[c % 2][HD * g:HD * g + HD, :], m.ones[:, 0:HD], m.PS[:, g, :],
                                    start=True, stop=True)
                last.then_inc(dn, 1)

            def scores(i, s):
                c, k = steps[s]
                q0, q1 = L.queries_of[kt[k]]
                if c == 0 and L.row_mask:
                    pe.wait_ge(bi, i * NBI + k + 1 + B)
                if k == 0:
                    pe.wait_ge(lk[c], i * PER + PER + B)
                for g in range(G):
                    h = G * c + g
                    pe.wait_ge(ex, i * (NS * G) + (G * (s - 1) + g + 1 if s or not isinstance(i, int) else 0) + B)
                    o = m.bank[4 + g][:, q0:q1]
                    ks = slice(kt[k] * P, (kt[k] + 1) * P)
                    biases = []
                    if L.row_mask:
                        biases = [m.MBK[:, kt[k], q0:q1]]
                    elif not dyn:
                        parts = 3 if L.fixed and kt[k] in (0, KT_ - 1) else 1
                        biases = [m.MBF[:, j, kt[k], q0:q1] for j in range(parts)]
                    for j, b in enumerate(biases):
                        t.matmul(o, m.IDB[:, :], b, start=j == 0, stop=False)
                    t.matmul(o, m.KA[0:3 * HD, h, ks], m.QA[0:3 * HD, h, q0:q1], start=not biases, stop=False)
                    t.matmul(o, m.KBS[:, h, ks], m.QB[:, h, q0:q1], start=False, stop=True).then_inc(sc, 1)

            def body(i):
                for s in range(1, NS + 1):
                    if s < NS:
                        scores(i, s)
                    elif dyn:
                        scores(i + 1, 0)
                    times_values(i, s - 1)
                    if s % KT_ == 0 and s < NS:
                        denominators(i, s // KT_ - 1)
                denominators(i, DC - 1)

            M.tensor(pe)
            pe.wait_ge(M.stored, 32)
            pe.wait_ge(M.zeroed, 1)
            if not dyn:
                pe.wait_ge(lm, 16)
            scores(0, 0)
            over_blocks(pe, L, nb, body)

        @block.gpsimd
        def _(pool):
            M.gpsimd(pool)

        @block.scalar
        def _(act):
            nb = blocks_to_do(act, m, L)
            a = nc.scalar

            def exponentials(i, s):
                c, k = steps[s]
                q0, q1 = L.queries_of[kt[k]]
                if s == 0 and dyn and not L.row_mask:
                    act.wait_ge(bi, i + 1 + B)
                before = s - 1 if s or not isinstance(i, int) else 0
                act.wait_ge(pv, i * NS + before + B)
                act.wait_ge(pa, i * NS + before + B)
                for g in range(G):
                    act.wait_ge(sc, i * (NS * G) + G * s + g + 1 + B)
                    kw = {}
                    if dyn and not L.row_mask:
                        kw["bias"] = m.KBIAS[:, kt[k]:kt[k] + 1]
                    a.activation(m.PB[:, s % 2, g, q0:q1], m.bank[4 + g][:, q0:q1], ACT.Exp, **kw).then_inc(ex, 1)

            def body(i):
                for s in range(1, NS):
                    exponentials(i, s)
                if dyn:
                    exponentials(i + 1, 0)

            exponentials(0, 0)
            over_blocks(act, L, nb, body)

        @block.vector
        def _(dve):
            nb = blocks_to_do(dve, m, L)
            v = nc.vector

            def bias(i, kb):
                dve.wait_ge(lm, i * 16 + 16 + B)
                if L.row_mask:
                    v.scalar_tensor_tensor(m.MBK[:, kb, :], m.MI[:, kb, :], 1.0, m.RNROW[:, :],
                                           ALU.is_equal, ALU.mult).then_inc(bi, 1)
                else:
                    v.tensor_scalar(m.KBIAS[:, :], m.KM[:, 0:KT_], 1.0, -NEG, ALU.subtract, ALU.mult).then_inc(bi, 1)

            def body(i):
                def add_up(c):
                    dve.wait_ge(oa, i * (2 * DC) + 2 * c + B)
                    dve.wait_ge(pv, i * NS + KT_ * c + KT_ + B)
                    v.tensor_tensor(m.OACC[:, c, :], m.OACC[:, c, :], m.bank[2 + c % 2][:, :], ALU.add).then_inc(oa, 1)
                    dve.wait_ge(dn, i * DC + c + 1 + B)
                    v.tensor_tensor(m.DACC[:, c, :], m.DACC[:, c, :], m.bank[c % 2][:, :], ALU.add).then_inc(oa, 1)

                for s, (c, k) in enumerate(steps):
                    q0, q1 = L.queries_of[kt[k]]
                    if k == 0:
                        dve.wait_ge(dn, i * DC + c + B)
                        if (q0, q1) != (0, T):
                            v.memset(m.PS[:, :, :], 0.0).then_inc(zs, 1)
                            dve.wait_ge(zs, c + 1)
                    dve.wait_ge(ex, i * (NS * G) + G * s + G + B)
                    dve.wait_ge(pa, i * NS + s + B)
                    dst = m.PS[:, :, q0:q1]
                    if k == 0 and (q0, q1) == (0, T):
                        v.tensor_copy(dst, m.PB[:, s % 2]).then_inc(pa, 1)
                    else:
                        v.tensor_tensor(dst, dst, m.PB[:, s % 2, :, q0:q1], ALU.add).then_inc(pa, 1)
                    if k == 1 and c:
                        add_up(c - 1)
                    if dyn and NS - s <= NBI:
                        bias(i + 1, s - (NS - NBI))
                add_up(DC - 1)

            M.vector(dve)
            if dyn:
                for kb in range(NBI):
                    bias(0, kb)
            dve.wait_ge(M.zeroed, 3)
            over_blocks(dve, L, nb, body)


def project_out(nc, m, L):
    n = L.name + "_out"
    ch, op, xs, pe_, vb = (m.sem(n + x) for x in ("_dve", "_proj", "_x", "_pe", "_biased"))
    RQ, RT = m.small[:, 0:NQ * H], m.KF[:, 0, :]
    with nc.Block() as block:
        @block.tensor
        def _(pe):
            t = nc.tensor
            for q in range(NQ):
                for c in range(DC):
                    last = t.matmul(m.bank[4][:, H * q:H * q + H], m.DACC[:, c, q * P:(q + 1) * P],
                                    m.head_mean[:, H * c:H * c + H], start=c == 0, stop=c == DC - 1)
            last.then_inc(pe_, 1)
            pe.wait_ge(ch, 2)
            for q in range(NQ):
                last = t.transpose(m.bank[5][0:H, q * P:(q + 1) * P], RQ[:, H * q:H * q + H], m.ident[:, :])
            last.then_inc(pe_, 1)
            pe.wait_ge(ch, 3)
            for c in range(DC):
                t.matmul(m.bank[c][:, :], m.spread[c][:, :], RT, start=True, stop=True).then_inc(pe_, 1)
            pe.wait_ge(m.wo_loaded, 32)
            for c in range(DC):
                pe.wait_ge(vb, c + 1)
                for q in range(NQ):
                    last = t.matmul(m.bank[4 + q][:, :], m.OACC[:, c, q * P:(q + 1) * P], m.WQ[:, c, :],
                                    start=c == 0, stop=c == DC - 1)
                    if c == DC - 1:
                        last.then_inc(op, 1)

        @block.scalar
        def _(act):
            for c in range(DC):
                act.wait_ge(ch, 4 + c)
                nc.scalar.activation(m.OACC[:, c, :], m.OACC[:, c, :], ACT.Identity,
                                     bias=m.vec(L.bv)[:, c:c + 1]).then_inc(vb, 1)

        @block.vector
        def _(dve):
            v = nc.vector
            v.memset(RT, 0.0).then_inc(ch, 1)
            dve.wait_ge(pe_, 1)
            v.reciprocal(RQ, m.bank[4][:, 0:NQ * H]).then_inc(ch, 1)
            dve.wait_ge(pe_, 2)
            dve.wait_ge(ch, 1)
            v.tensor_copy(RT[0:H, :], m.bank[5][0:H, :]).then_inc(ch, 1)
            for c in range(DC):
                dve.wait_ge(pe_, 3 + c)
                v.tensor_tensor(m.OACC[:, c, :], m.OACC[:, c, :], m.bank[c][:, :], ALU.mult).then_inc(ch, 1)
            dve.wait_ge(m.wo_loaded, 32)
            for q in range(NQ):
                v.tensor_tensor(m.X[:, q, :], m.X[:, q, :], m.RAROWS[:, :], ALU.add).then_inc(xs, 1)
            for q in range(NQ):
                dve.wait_ge(op, q + 1)
                dve.wait_ge(xs, NQ)
                v.tensor_tensor(m.X[:, q, :], m.X[:, q, :], m.bank[4 + q][:, :], ALU.add).then_inc(xs, 1)
            dve.wait_ge(xs, 2 * NQ)


def attention(nc, m, L):
    normalise(nc, m, L.name, L)
    row_maxima(nc, m, L)
    weighted_values(nc, m, L)
    project_out(nc, m, L)


def route(nc, m, tag, router, probs):
    ld, ch, mm, ac = m.sem(tag + "_router"), m.sem(tag + "_rt_dve"), m.sem(tag + "_rt_pe"), m.sem(tag + "_rt_act")
    s = m.small
    LG = s[:, 0:32]
    ONE = [s[:, 32:64], s[:, 64:96]]
    T1, T2 = s[:, 96:128], s[:, 128:160]
    MM = [s[:, 160:164], s[:, 164:168]]
    IX, AA, BB = s[:, 168:172], s[:, 172:176], s[:, 176:180]
    SM = s[:, 180:212]
    NE, RD, CU = s[0:E, 212:213], s[0:E, 213:214], s[0:E, 214:215]
    LE = s[0:E, 216:232]
    RK = s[:, 232:264]
    def r3(x):
        return x.rearrange("p (t e) -> p t e", e=E)
    def bc(x):
        return x.unsqueeze(2).to_broadcast([P, NQ, E])
    ramp8 = m.ramp[:, 0:E].unsqueeze(1).to_broadcast([P, NQ, E])
    with nc.Block() as block:
        @block.sync
        def _(sp):
            sp.dma_start(m.WR[:, :, :], m.d[router].rearrange("(c p) e -> p c e", p=P)).then_inc(ld, 16)

        @block.vector
        def _(dve):
            v = nc.vector
            m.steps = 0

            def do(ins):
                m.steps += 1
                ins.then_inc(ch, 1)
                dve.wait_ge(ch, m.steps)

            dve.wait_ge(mm, 1)
            do(v.tensor_copy(LG, m.bank[0][:, 0:32]))
            if probs:
                do(v.tensor_reduce(AA, r3(LG), AX.X, ALU.max))
                do(v.tensor_tensor(r3(LG), r3(LG), bc(AA), ALU.subtract))
                m.mark["exp"] = m.steps
                dve.wait_ge(ac, 1)
                do(v.tensor_reduce(AA, r3(LG), AX.X, ALU.add))
                do(v.reciprocal(AA, AA))
                do(v.tensor_tensor(r3(LG), r3(LG), bc(AA), ALU.mult))
            do(v.tensor_copy(T1, LG))
            for k in range(2):
                do(v.tensor_reduce(MM[k], r3(T1), AX.X, ALU.max))
                do(v.tensor_tensor(r3(T2), r3(T1), bc(MM[k]), ALU.is_equal))
                do(v.tensor_scalar(T2, T2, -float(E), float(E), ALU.mult, ALU.add))
                do(v.tensor_tensor(r3(T2), r3(T2), ramp8, ALU.add))
                do(v.tensor_reduce(IX, r3(T2), AX.X, ALU.min))
                do(v.tensor_tensor(r3(ONE[k]), ramp8, bc(IX), ALU.is_equal))
                if k == 0:
                    do(v.scalar_tensor_tensor(T1, ONE[0], LOWEST, LG, ALU.mult, ALU.add))
            do(v.tensor_tensor(SM, ONE[0], ONE[1], ALU.add))
            m.mark["selected"] = m.steps
            GW = m.GW[:, :].rearrange("p (t k) -> p t k", k=2)
            if probs:
                do(v.tensor_tensor(AA, MM[0], MM[1], ALU.add))
                do(v.tensor_scalar(AA, AA, 1e-8, None, ALU.add))
                do(v.reciprocal(BB, AA))
                do(v.tensor_tensor(GW[:, :, 0], MM[0], BB, ALU.mult))
                do(v.tensor_tensor(GW[:, :, 1], MM[1], BB, ALU.mult))
            else:
                do(v.tensor_tensor(AA, MM[1], MM[0], ALU.subtract))
                m.mark["exp"] = m.steps
                dve.wait_ge(ac, 1)
                do(v.tensor_scalar(BB, AA, 1.0, None, ALU.add))
                do(v.reciprocal(BB, BB))
                do(v.tensor_copy(GW[:, :, 0], BB))
                do(v.tensor_tensor(GW[:, :, 1], AA, BB, ALU.mult))
            dve.wait_ge(mm, 2)
            do(v.tensor_copy(NE, m.bank[2][0:E, 0:1]))
            do(v.tensor_scalar(RD, NE, 0.0, None, ALU.is_gt))
            for k in range(1, NQ):
                do(v.scalar_tensor_tensor(RD, NE, float(P * k), RD, ALU.is_gt, ALU.add))
            m.mark["rounds"] = m.steps
            do(v.tensor_copy(RK, m.bank[1][:, 0:32]))
            dve.wait_ge(mm, 3)
            do(v.tensor_copy(CU, m.bank[3][0:E, 0:1]))
            do(v.tensor_scalar(LE, m.ramp[0:E, 0:16], CU, None, ALU.is_ge))
            m.mark["of_round"] = m.steps
            do(v.tensor_scalar(T1[:, 0:E], m.bank[4][:, 0:E], float(P), None, ALU.mult))
            do(v.tensor_tensor(r3(RK), r3(RK), T1[:, 0:E].unsqueeze(1).to_broadcast([P, NQ, E]), ALU.add))
            GS = m.GS[:, :].rearrange("p (t k) -> p t k", k=2)
            for k in range(2):
                do(v.tensor_tensor(T2, RK, ONE[k], ALU.mult))
                do(v.tensor_reduce(GS[:, :, k], r3(T2), AX.X, ALU.add))
            do(v.tensor_copy(m.CTL[0:1, C_NR:C_NR + 1], m.bank[5][0:1, 0:1]))
            dve.wait_ge(mm, 4)
            do(v.tensor_copy(m.CTL[0:1, C_E:C_E + 16], m.bank[6][0:1, 0:16]))

        @block.tensor
        def _(pe):
            t = nc.tensor
            pe.wait_ge(ld, 16)
            for q in range(NQ):
                for d in range(DC):
                    last = t.matmul(m.bank[0][:, E * q:E * q + E], m.XNT[:, d, q * P:(q + 1) * P], m.WR[:, d, :],
                                    start=d == 0, stop=d == DC - 1)
            last.then_inc(mm, 1)
            pe.wait_ge(ch, m.mark["selected"])
            for q in range(NQ):
                for b in range(q + 1):
                    t.matmul(m.bank[1][:, E * q:E * q + E], (m.before if b == q else m.ones)[:, :], r3(SM)[:, b, :],
                             start=b == 0, stop=b == q)
            for q in range(NQ):
                last = t.matmul(m.bank[2][0:E, 0:1], r3(SM)[:, q, :], m.ones[:, 0:1], start=q == 0, stop=q == NQ - 1)
            last.then_inc(mm, 1)
            pe.wait_ge(ch, m.mark["rounds"])
            t.matmul(m.bank[3][0:E, 0:1], m.upto[0:E, 0:E], RD, start=True, stop=True)
            t.matmul(m.bank[4][:, 0:E], RD.to_broadcast([E, P]), m.before[0:E, 0:E], start=True, stop=True)
            t.matmul(m.bank[5][0:1, 0:1], RD, m.ones[0:E, 0:1], start=True, stop=True).then_inc(mm, 1)
            pe.wait_ge(ch, m.mark["of_round"])
            t.matmul(m.bank[6][0:1, 0:16], m.ones[0:E, 0:1], LE, start=True, stop=True).then_inc(mm, 1)

        @block.scalar
        def _(act):
            act.wait_ge(ch, m.mark["exp"])
            if probs:
                nc.scalar.activation(LG, LG, ACT.Exp).then_inc(ac, 1)
            else:
                nc.scalar.activation(AA, AA, ACT.Exp).then_inc(ac, 1)


def experts(nc, m, tag, w1, w2, F, relu2):
    m.fresh = []
    NF = F // KB
    l1, l2 = ([m.sem(f"{tag}_{w}_{k}") for k in range(NF)] for w in ("w1", "w2"))
    dg, dw, xe, xs = (m.sem(tag + x) for x in ("_token_of_slot", "_weight_of_slot", "_gather", "_gathered"))
    hp, hs, yo, sc = (m.sem(tag + x) for x in ("_h", "_act", "_yout", "_scatter"))
    xa, tr, tc, u1, ex, gc = (m.sem(tag + x) for x in ("_xadd", "_tr", "_trout", "_used", "_exp", "_dve"))
    def slots(a, b):
        return [t[:, 8 * k:8 * k + 8, :].bitcast(F32).rearrange("p (c x) n -> p c (x n)", x=2) for t in (a, b) for k in range(2)]
    W1, W2 = slots(m.QA, m.QB), slots(m.KA, m.KBS)
    DG, DW, XE = m.KF, m.V, m.CT[:, 0, :]
    HT = m.PB[:, :, :, :].rearrange("p a b (c n) -> p (a b c) n", n=P)
    HS = HT[:, 0:4 * NF, :]
    EX = m.MI[:, :, :].bitcast(F32)
    HR = m.MB
    DGT, Y = m.CT[:, 1, :], m.CT[:, 2, :]
    B = raised(nc, m, True)
    with nc.Block() as block:
        @block.sync
        def _(sp):
            nr = sp.value_load(m.CTL[0:1, C_NR:C_NR + 1], min_val=0, max_val=NR)
            with sp.Fori(0, NR) as i:
                with sp.If(i < nr):
                    e = sp.value_load(m.CTL[0:1, bass.ds(i + C_E, 1)], min_val=0, max_val=E - 1)
                    for k in range(NF):
                        wait_alone(sp, hp, i * NF + B)
                        sp.dma_start(W1[k], m.d[w1][bass.ds(e, 1), :, k * KB:(k + 1) * KB].rearrange("a (c p) n -> p (a c) n", p=P)).then_inc(l1[k], 16)
                    for k in range(NF):
                        wait_alone(sp, u1, i * NF + B)
                        sp.dma_start(W2[k], m.d[w2][bass.ds(e, 1), k * KB:(k + 1) * KB, :].rearrange("a (c p) n -> p (a c) n", p=P)).then_inc(l2[k], 16)

        @block.vector
        def _(dve):
            v = nc.vector
            nr = dve.value_load(m.CTL[0:1, C_NR:C_NR + 1], min_val=0, max_val=NR)
            def token_hots(i):
                for q in range(NQ):
                    for k in range(2):
                        j = 2 * q + k
                        last = v.tensor_scalar(DG[:, q, P * k:P * k + P], m.ramp[:, :], m.GS[:, j:j + 1], None, ALU.is_equal)
                last.then_inc(dg, 1)
                dve.wait_ge(dg, i * 2 + 1 + B)
                v.tensor_tensor(DG[:, :, 2 * P:3 * P], DG[:, :, 0:P], DG[:, :, P:2 * P], ALU.add).then_inc(dg, 1)

            def weight_hots(i):
                for q in range(NQ):
                    for k in range(2):
                        j = 2 * q + k
                        last = v.tensor_scalar(DW[:, q, P * k:P * k + P], m.ramp[:, :], m.GS[:, j:j + 1], m.GW[:, j:j + 1],
                                               ALU.is_equal, ALU.mult)
                last.then_inc(dw, 1)
                dve.wait_ge(dw, i * 2 + 1 + B)
                v.tensor_tensor(DW[:, :, 2 * P:3 * P], DW[:, :, 0:P], DW[:, :, P:2 * P], ALU.add).then_inc(dw, 1)
                v.tensor_scalar(m.GS[:, :], m.GS[:, :], float(P), None, ALU.subtract).then_inc(gc, 1)

            token_hots(0)
            weight_hots(0)
            dve.wait_ge(xe, 1 + B)
            v.tensor_copy(XE, m.bank[1][:, :]).then_inc(xs, 1)
            with dve.Fori(0, NR) as i:
                with dve.If(i < nr):
                    dve.wait_ge(xe, i + 1 + B)
                    dve.wait_ge(gc, i + 1 + B)
                    dve.wait_ge(dg, i * 2 + 2 + B)
                    token_hots(i + 1)
                    for k in range(NF):
                        hb = m.bank[2 + k % 2][:, :]
                        out = HS[:, 4 * k:4 * k + 4, :].rearrange("p a n -> p (a n)")
                        if relu2:
                            dve.wait_ge(hp, i * NF + k + 1 + B)
                            v.tensor_scalar(HR[:, k, :], hb, 0.0, None, ALU.max).then_inc(ex, 1)
                            dve.wait_ge(ex, i * NF + k + 1 + B)
                            v.tensor_tensor(out, HR[:, k, :], HR[:, k, :], ALU.mult).then_inc(hs, 1)
                        else:
                            dve.wait_ge(ex, i * NF + k + 1 + B)
                            v.tensor_tensor(out, EX[:, k, :], hb, ALU.mult).then_inc(hs, 1)
                    dve.wait_ge(tr, i + 1 + B)
                    dve.wait_ge(sc, i * NQ + B)
                    v.tensor_copy(DGT, m.bank[1][:, :]).then_inc(tc, 1)
                    dve.wait_ge(dw, i * 2 + 2 + B)
                    weight_hots(i + 1)
                    dve.wait_ge(u1, (i + 1) * NF + B)
                    v.tensor_copy(Y, m.bank[0][:, :]).then_inc(yo, 1)
                    dve.wait_ge(xe, i + 2 + B)
                    dve.wait_ge(hp, i * NF + NF + B)
                    v.tensor_copy(XE, m.bank[1][:, :]).then_inc(xs, 1)
                    dve.wait_ge(xa, i * NQ + B)
                    for q in range(NQ):
                        dve.wait_ge(sc, i * NQ + q + 1 + B)
                        v.tensor_tensor(m.X[:, q, :], m.X[:, q, :], m.bank[4 + q][:, :], ALU.add).then_inc(xa, 1)
            wait_alone(dve, xa, nr * NQ + B)

        @block.scalar
        def _(act):
            if relu2:
                return
            nr = act.value_load(m.CTL[0:1, C_NR:C_NR + 1], min_val=0, max_val=NR)
            with act.Fori(0, NR) as i:
                with act.If(i < nr):
                    for k in range(NF):
                        act.wait_ge(hp, i * NF + k + 1 + B)
                        nc.scalar.activation(EX[:, k, :], m.bank[2 + k % 2][:, :], ACT.Sigmoid).then_inc(ex, 1)

        @block.tensor
        def _(pe):
            t = nc.tensor
            nr = pe.value_load(m.CTL[0:1, C_NR:C_NR + 1], min_val=0, max_val=NR)

            def gather(i):
                pe.wait_ge(dg, i * 2 + 2 + B)
                for d in range(DC):
                    for q in range(NQ):
                        last = t.matmul(m.bank[1][:, d * P:(d + 1) * P], m.XN[:, q, d * P:(d + 1) * P],
                                        DG[:, q, 2 * P:3 * P], start=q == 0, stop=q == NQ - 1)
                last.then_inc(xe, 1)

            gather(0)
            with pe.Fori(0, NR) as i:
                with pe.If(i < nr):
                    pe.wait_ge(xs, i + 1 + B)
                    for k in range(NF):
                        pe.wait_ge(l1[k], i * 16 + 16 + B)
                        pe.wait_ge(hs, i * NF + max(0, k - 1) + B)
                        for f in range(4):
                            for d in range(DC):
                                last = t.matmul(m.bank[2 + k % 2][:, f * P:(f + 1) * P], W1[k][:, d, f * P:(f + 1) * P],
                                                XE[:, d * P:(d + 1) * P], start=d == 0, stop=d == DC - 1)
                        last.then_inc(hp, 1)
                    pe.wait_ge(dw, i * 2 + 2 + B)
                    for q in range(NQ):
                        last = t.transpose(m.bank[1][:, q * P:(q + 1) * P], DW[:, q, 2 * P:3 * P], m.ident[:, :])
                    last.then_inc(tr, 1)
                    pe.wait_ge(yo, i + B)
                    for k in range(NF):
                        pe.wait_ge(l2[k], i * 16 + 16 + B)
                        pe.wait_ge(hs, i * NF + k + 1 + B)
                        for f in range(4):
                            last = t.matmul(m.bank[0][:, :], HS[:, 4 * k + f, :], W2[k][:, f, :],
                                            start=k + f == 0, stop=(k == NF - 1 and f == 3))
                        last.then_inc(u1, 1)
                    pe.wait_ge(tc, i + 1 + B)
                    gather(i + 1)
                    pe.wait_ge(yo, i + 1 + B)
                    for q in range(NQ):
                        pe.wait_ge(xa, i * NQ + B)
                        t.matmul(m.bank[4 + q][:, :], DGT[:, q * P:(q + 1) * P], Y, start=True, stop=True).then_inc(sc, 1)


def build(nc, d, out):
    with ExitStack() as ctx:
        m = Chip()
        m.d = d
        m.mark = {}

        def sb(name, shape, dt=F32):
            return ctx.enter_context(nc.sbuf_tensor(name, shape, dt))

        m.open_sems, m.fresh = [], []

        def sem(name):
            m.open_sems.append(nc.alloc_semaphore(name=name))
            m.fresh.append(m.open_sems[-1])
            return m.open_sems[-1]

        def layer_done():
            nc.clear_and_free_semaphores(m.open_sems)
            nc.all_engine_barrier()
            m.open_sems = []

        m.sem = sem
        m.X, m.XN, m.XNT = sb("X", [P, NQ, D]), sb("XN", [P, NQ, D]), sb("XNT", [P, DC, T])
        m.QA, m.QB, m.KA, m.KBS = (sb(x, [P, H, T], BF16) for x in ("QA", "QB", "KA", "KBS"))
        m.KF, m.CT, m.V = sb("KF", [P, DC, KB]), sb("CT", [P, DC, KB]), sb("V", [P, KT_, D])
        m.PB, m.PS = sb("PB", [P, 2, G, T]), sb("PS", [P, G, T])
        m.ACC = sb("ACC", [P, 2, DC, T])
        m.OACC, m.DACC = m.ACC[:, 0], m.ACC[:, 1]
        m.PARTS = m.ACC[:, :, :, :].bitcast(BF16).rearrange("p a c n -> p (a c n)")[:, 0:3 * DC * KB].rearrange(
            "p (j c n) -> p j c n", j=3, c=DC)
        m.JUNK = m.PS[:, 0:2, :].bitcast(BF16).rearrange("p a (b n) -> p (a b) n", n=KB)
        m.WQ, m.WK, m.WV = (sb(x, [P, DC, D]) for x in ("WQ", "WK", "WV"))
        m.MASK = sb("MASK", [P, 2, NQ, KB])
        m.MI, m.MB = m.MASK[:, 0].bitcast(I32), m.MASK[:, 1]
        m.MBK = m.MASK[:, 1, 0:2, :].bitcast(BF16).rearrange("p a (b n) -> p (a b) n", n=KB)
        m.MBF = m.MASK[:, :, :, :].bitcast(BF16).rearrange("p a c n -> p (a c n)")[:, 0:3 * KT_ * T].rearrange(
            "p (j c n) -> p j c n", j=3, c=KT_)
        m.RAROW, m.RNROW, m.RAROWS = sb("RAROW", [P, T]), sb("RNROW", [P, T]), sb("RAROWS", [P, T])
        m.NM, m.NMX = m.KF[0:3 * H, 0, :].bitcast(BF16)[:, 0:T], m.KF[:, 1, 0:NQ * 3 * H]
        m.CON, m.VT = sb("CON", [P, len(CONST), P]), sb("VT", [P, len(VEC), 4])
        m.IDB = sb("IDB", [P, P], BF16)
        m.KMW, m.KBIAS = sb("KM", [P, KB // 4], I32), sb("KBIAS", [P, KT_])
        m.KM = m.KMW[:, :].bitcast(U8)
        m.MX, m.MXB = sb("MX", [P, H * NQ]), sb("MXB", [P, H * NQ], BF16)
        m.RA, m.RN, m.WR = sb("RA", [P, NQ]), sb("RN", [P, NQ]), sb("WR", [P, DC, E])
        m.GS, m.GW = sb("GS", [P, 2 * NQ]), sb("GW", [P, 2 * NQ])
        m.UNMASKED = sb("UNMASKED", [P, NQ, NB])
        m.EPS, m.MINUS1 = sb("EPS", [P, 1]), sb("MINUS1", [P, 1])
        m.RSTDS, m.RSTD = m.RAROWS, m.RAROWS[0:H, :]
        qp = m.PB[:, 1].bitcast(BF16).rearrange("p g n -> p (g n)").rearrange("p (j c n) -> p j c n", j=2, c=DC)
        m.QP = [qp[:, 0], qp[:, 1], m.PS[:, 2:4, :].bitcast(BF16).rearrange("p a (b n) -> p (a b) n", n=T)]
        halves = m.KBS[:, :, :].bitcast(I32).rearrange("p h n -> p (h n)").rearrange("p (a q n) -> p a q n", a=2, n=KB)
        m.COUNT = [halves[:, 0], halves[:, 1], m.XN[:, :, :].bitcast(I32), m.MI]
        m.small, m.CTL = sb("small", [P, 264]), sb("CTL", [1, 96], I32)
        tiles = {k: m.CON[:, i, :] for i, k in enumerate(CONST)}
        m.ident, m.gmean, m.before, m.upto, m.ones, m.ramp, m.index, m.head_mean = (tiles[k] for k in CONST[:8])
        m.spread = [tiles[f"spread{c}"] for c in range(DC)]
        m.vec = lambda name: m.VT[:, VEC.index(name), :]
        m.bank = [ctx.enter_context(nc.psum_tensor(f"bank{i}", [P, 512], F32)) for i in range(8)]
        m.KSAVE = nc.dram_tensor("k_saved", (NB + 1, P, 3, DC, KB), BF16, kind="Internal").ap()
        m.VSAVE = nc.dram_tensor("v_saved", (NB + 1, P, KT_, D), F32, kind="Internal").ap()
        m.QSAVE = nc.dram_tensor("q_saved", (3, P, DC, T), BF16, kind="Internal").ap()
        m.MSAVE = nc.dram_tensor("m_saved", (3 * H, T), BF16, kind="Internal").ap()

        UNWAITED[:] = [nc.alloc_semaphore(name="unwaited")]
        active_blocks(nc, m, "blocks0", None, C_N0)
        layer_done()
        attention(nc, m, Attention("L0x", "L0x_wq", "L0x_wk", "L0x_wv", "L0x_wo", 0, count=C_N0, norm=True))
        layer_done()
        attention(nc, m, Attention("L0a", "L0a_wq", "L0a_wk", "L0a_wv", "L0a_wo", 1, fixed=0))
        layer_done()
        normalise(nc, m, "L0f")
        route(nc, m, "L0f", "L0f_router", False)
        experts(nc, m, "L0f", "L0f_w1", "L0f_w2", 2048, False)
        layer_done()
        active_blocks(nc, m, "blocks1", None, C_N1, m.UNMASKED[:, :, :])
        attention(nc, m, Attention("L1x", "L1x_wq", "L1x_wk", "L1x_wv", "L1x_wo", 2, count=C_N1, row_mask=True))
        layer_done()
        attention(nc, m, Attention("L1a", "L1a_wq", "L1a_wk", "L1a_wv", "L1a_wo", 3, fixed=1))
        layer_done()
        normalise(nc, m, "L1f")
        route(nc, m, "L1f", "L1f_router", True)
        experts(nc, m, "L1f", "L1f_w1", "L1f_w2", 1024, True)
        stored = m.sem("stored")
        with nc.Block() as block:
            @block.sync
            def _(sp):
                sp.dma_start(out.rearrange("(t p) d -> p t d", p=P), m.X[:, :, :]).then_inc(stored, 16)
                sp.wait_ge(stored, 16)
        layer_done()


def laid_out(i):
    a = {k: np.asarray(v) for k, v in i.items()}
    d = {"x": a["x"][0]}
    d["ctx"] = a["ctx_1024"][0].reshape(NB, KB, DC, P).transpose(0, 3, 2, 1)
    mask = a["mask_Bx1xSxS2_ik1"][0, 0]
    d["mask_q"] = mask.reshape(NQ, P, NB, KB).transpose(2, 1, 0, 3)
    d["mask_k"] = mask.T.reshape(NB, KT_, P, T).transpose(0, 2, 1, 3)
    km = a["mask_BxS2_bk0"][0].view(np.uint8)
    d["keymask"] = km.reshape(NB, KB).view(np.int32)
    d["keymask_k"] = np.ascontiguousarray(km.reshape(NB, KT_, P).transpose(0, 2, 1)).view(np.int32)
    wkv = a["L0_xattn_Wkv"]
    d["L0x_wq"], d["L0x_wk"], d["L0x_wv"], d["L0x_wo"] = a["L0_xattn_Wq"].T, wkv[:D].T, wkv[D:].T, a["L0_xattn_Wo"].T
    w = a["L0_attn_w_qkv"]
    d["L0a_wq"], d["L0a_wk"], d["L0a_wv"], d["L0a_wo"] = w[:, :D], w[:, D:2 * D], w[:, 2 * D:], a["L0_attn_w_out"]
    for s, l in (("L1x", "L1_xattn"), ("L1a", "L1_attn")):
        for x in "qkvo":
            d[f"{s}_w{x}"] = a[f"{l}_W{x}"].T
    d["L0f_router"], d["L0f_w1"], d["L0f_w2"] = a["L0_ffn_router"], a["L0_ffn_W1"], a["L0_ffn_W2"]
    d["L1f_router"], d["L1f_w1"], d["L1f_w2"] = a["L1_ffn_Wg"], a["L1_ffn_W1"], a["L1_ffn_W2"]
    b0, ba = a["L0_xattn_bkv"], a["L0_attn_b_qkv"]
    vec = {"L0x_bq": a["L0_xattn_bq"], "L0x_bk": b0[:D], "L0x_bv": b0[D:], "L0a_bq": ba[:D], "L0a_bk": ba[D:2 * D],
           "L0a_bv": ba[2 * D:], "L1x_bq": a["L1_xattn_bq"], "L1x_bk": a["L1_xattn_bk"], "L1x_bv": a["L1_xattn_bv"],
           "zero": np.zeros(D, np.float32)}
    for x in ("qn_w", "qn_b", "kn_w", "kn_b"):
        vec[x] = np.tile(a[f"L0_xattn_{x}"], D // HD)
    d["vectors"] = np.concatenate([vec[n].reshape(DC, P).T for n in VEC], axis=1)
    d["bo"] = np.stack([np.broadcast_to(a[n], (P, D)) for n in ("L0_xattn_bo", "L0_attn_b_out", "L1_xattn_bo", "L1_attn_bo")])
    d["consts"] = consts()
    d["biases"] = fixed_biases()
    d["bias_parts"] = in_parts(d["biases"][:, 1])
    return {k: np.ascontiguousarray(v) for k, v in d.items()}


def kernel(**inputs):
    import concourse.bacc as _bacc
    from concourse.bass_utils import run_bass_kernel_spmd as _run

    nc = _bacc.Bacc("TRN2", target_bir_lowering=False, num_devices=1)
    arrays = {f"in_{k}": v for k, v in laid_out(inputs).items()}
    d = {k[3:]: nc.dram_tensor(k, v.shape, mybir.dt.from_np(v.dtype), kind="ExternalInput").ap()
         for k, v in arrays.items()}
    out = nc.dram_tensor("out", (T, D), F32, kind="ExternalOutput").ap()
    build(nc, d, out)
    r = _run(nc, [arrays], core_ids=[0])
    return np.asarray(r.results[0]["out"]).reshape(1, T, D)
```

```python
from contextlib import ExitStack

import numpy as np
import concourse.bass as bass
from concourse import mybir

F32 = mybir.dt.float32
BF16 = mybir.dt.bfloat16
I32 = mybir.dt.int32
U8 = mybir.dt.uint8
ALU = mybir.AluOpType
ACT = mybir.ActivationFunctionType
AX = mybir.AxisListType

P = 128
D = 512
T = 512
NQ = T // P
DC = D // P
H = 16
HD = D // H
G = P // HD
S2 = 8192
KB = 512
NB = S2 // KB
KT_ = KB // P
E = 8
NR = 15
SCALE = float(HD) ** -0.5
NEG = -1.0e30
LOWEST = -3.0e38
WINDOW = 32

BIAS_PARTS = (1, 3)

VEC = ["L0x_bq", "L0x_bk", "L0x_bv", "L0a_bq", "L0a_bk", "L0a_bv", "L1x_bq", "L1x_bk", "L1x_bv", "zero",
       "qn_w", "qn_b", "kn_w", "kn_b"]
C_N0, C_L0, C_N1, C_L1, C_NR, C_E, C_M = 0, 1, 32, 33, 64, 65, 81


def consts():
    p = np.arange(P)
    heads = np.zeros((P, P))
    spread = np.zeros((DC, P, P))
    for c in range(DC):
        heads[p, H * c + G * c + p // HD] = 1.0 / HD
        spread[c, G * c + p // HD, p] = 1.0
    c = {"ident": np.eye(P), "group_mean": (p[:, None] // HD == p[None, :] // HD) / HD,
         "before": (p[:, None] < p[None, :]) * 1.0, "upto": (p[:, None] <= p[None, :]) * 1.0,
         "ones": np.ones((P, P)), "ramp": np.tile(p[None, :], (P, 1)) * 1.0,
         "index": np.tile(p[:, None], (1, P)) * 1.0, "head_mean": heads,
         **{f"spread{k}": spread[k] for k in range(DC)}}
    return np.concatenate([c[k] for k in CONST], axis=1).astype(np.float32)


CONST = ["ident", "group_mean", "before", "upto", "ones", "ramp", "index", "head_mean",
         "spread0", "spread1", "spread2", "spread3"]


def fixed_biases():
    i = np.arange(T)
    later = np.where(i[None, :] >= i[:, None], 0.0, NEG)
    count = np.zeros((T, T))
    for off in range(-WINDOW, WINDOW):
        np.add.at(count, (i, np.clip(i + off, 0, T - 1)), 1.0)
    window = np.where(count > 0, np.log(np.maximum(count, 1.0)), NEG)
    out = np.zeros((2, 2, P, NQ, T), np.float32)
    for n, b in enumerate((later, window)):
        out[n, 0] = b.reshape(NQ, P, T).transpose(1, 0, 2)
        out[n, 1] = b.T.reshape(NQ, P, T).transpose(1, 0, 2)
    return out


def in_parts(a):
    bf = mybir.dt.np(BF16)
    parts = []
    for _ in range(3):
        parts.append(a.astype(bf))
        a = a - parts[-1].astype(np.float32)
    return np.stack(parts, axis=-3)


class Attention:

    def __init__(self, name, wq, wk, wv, wo, bo, fixed=None, count=None, norm=False, row_mask=False):
        self.name, self.wq, self.wk, self.wv, self.wo, self.bo = name, wq, wk, wv, wo, bo
        self.fixed = fixed
        self.count = count
        self.norm = norm
        self.row_mask = row_mask
        self.keys_of, self.queries_of = [(0, KB)] * NQ, [(0, T)] * KT_
        if fixed is not None:
            self.keys_of = [(max(0, P * q - WINDOW) if fixed else P * q, min(KB, P * q + P + WINDOW) if fixed else KB)
                            for q in range(NQ)]
            self.queries_of = [(max(0, P * k - WINDOW) if fixed else 0, min(T, P * k + P + WINDOW) if fixed else P * k + P)
                               for k in range(KT_)]
        self.order = list(range(KT_))[::-1] if fixed == 0 else list(range(KT_))
        self.bq, self.bk, self.bv = [f"{name}_b{x}" if name != "L1a" else "zero" for x in "qkv"]


class Chip:
    pass


def blocks_to_do(eng, m, L):
    if L.fixed is not None:
        return 1
    return eng.value_load(m.CTL[0:1, L.count:L.count + 1], min_val=0, max_val=NB)


UNWAITED = []


def wait_alone(eng, sem, value):
    eng.wait_ge(sem, value)
    eng.sem_inc(UNWAITED[0], 1)


def raised(nc, m, loops):
    fresh, m.fresh = m.fresh, []
    if not loops:
        return 0
    for j, sem in enumerate(fresh):
        (nc.gpsimd, nc.sync, nc.vector)[j % 3].sem_inc(sem, 1)
    nc.all_engine_barrier()
    return 1


def one(j):
    return slice(j, j + 1) if isinstance(j, int) else bass.ds(j, 1)


def first_iterations(nc, i):
    return nc.s_assert_within(i, 0, NB // 4 - 1, skip_runtime_bounds_check_because="inside If(i < NB // 4)")


def active_loop(eng, n, body, also=None):
    with eng.Fori(0, NB // 4) as group:
        with eng.If(group * 4 < n):
            with eng.Fori(0, 4) as j:
                i = group * 4 + j
                with eng.If(i < n):
                    body(i)
                if also is not None:
                    also(i)


def over_blocks(eng, L, n, body):
    if L.fixed is not None:
        body(0)
        return
    active_loop(eng, n, body)


def active_blocks(nc, m, tag, flags, count, unmasked=None):
    steps_done, products_done, loaded = m.sem(tag + "_dve"), m.sem(tag + "_pe"), m.sem(tag + "_loaded")
    F, POS, LST, RF = m.small[0:NB, 80:81], m.small[0:NB, 82:83], m.small[0:NB, 84:84 + NB], m.small[:, 116:120]
    with nc.Block() as block:
        @block.sync
        def _(sp):
            if unmasked is None:
                sp.dma_start(m.CON[:, :, :], m.d["consts"].rearrange("p (k n) -> p k n", n=P)).then_inc(loaded, 16)
                sp.dma_start(m.KMW[0:NB, :], m.d["keymask"]).then_inc(loaded, 16)
                sp.wait_ge(loaded, 32)
                for t, src in ((m.VT[:, :, :], m.d["vectors"].rearrange("p (v c) -> p v c", c=4)),
                               (m.X[:, :, :], m.d["x"].rearrange("(t p) d -> p t d", p=P))):
                    sp.dma_start(t, src).then_inc(loaded, 16)
                sp.wait_ge(loaded, 64)

        @block.vector
        def _(dve):
            v = nc.vector
            k = 0
            if unmasked is None:
                v.memset(m.CTL[:, :], 0).then_inc(steps_done, 1)
                v.memset(m.MINUS1[:, :], -1.0).then_inc(steps_done, 1)
                dve.wait_ge(loaded, 32)
                v.tensor_copy(m.IDB[:, :], m.ident[:, :]).then_inc(steps_done, 1)
                v.tensor_reduce(F, m.KM[0:NB, 0:KB], AX.X, ALU.max).then_inc(steps_done, 1)
                k = 4
            else:
                v.tensor_reduce(RF, unmasked, AX.X, ALU.max).then_inc(steps_done, 1)
                dve.wait_ge(steps_done, 1)
                v.tensor_scalar(m.RA[:, :], RF, 0.0, None, ALU.is_gt).then_inc(steps_done, 1)
                v.tensor_scalar(RF, RF, 0.0, None, ALU.is_le).then_inc(steps_done, 1)
                v.tensor_scalar(unmasked, unmasked, 0.0, None, ALU.is_gt).then_inc(steps_done, 1)
                dve.wait_ge(products_done, 1)
                v.tensor_reduce(F, m.bank[0][0:NB, 0:5], AX.X, ALU.add).then_inc(steps_done, 1)
                v.tensor_copy(m.RAROW[:, :], m.bank[1][:, :]).then_inc(steps_done, 1)
                dve.wait_ge(steps_done, 6)
                v.tensor_scalar(m.RN[:, :], m.RA[:, :], NEG, None, ALU.mult).then_inc(steps_done, 1)
                v.tensor_scalar(m.RNROW[:, :], m.RAROW[:, :], NEG, None, ALU.mult).then_inc(steps_done, 1)
                k = 8
            dve.wait_ge(steps_done, k)
            v.tensor_scalar(F, F, 0.0, None, ALU.is_gt).then_inc(steps_done, 1)
            dve.wait_ge(products_done, 1 if unmasked is None else 2)
            v.tensor_copy(POS, m.bank[2][0:NB, 0:1]).then_inc(steps_done, 1)
            dve.wait_ge(steps_done, k + 2)
            v.tensor_scalar(LST, m.ramp[0:NB, 1:NB + 1], POS, F, ALU.is_equal, ALU.mult).then_inc(steps_done, 1)
            dve.wait_ge(products_done, 2 if unmasked is None else 3)
            v.tensor_copy(m.CTL[0:1, count:count + 1 + NB], m.bank[3][0:1, 0:1 + NB]).then_inc(steps_done, 1)
            dve.wait_ge(steps_done, k + 4)

        @block.tensor
        def _(pe):
            t = nc.tensor
            k = 5
            if unmasked is not None:
                k = 9
                pe.wait_ge(steps_done, 4)
                for q in range(NQ):
                    t.matmul(m.bank[0][0:NB, 0:1], unmasked[:, q, :], m.ones[:, 0:1], start=q == 0, stop=q == NQ - 1)
                for q in range(NQ):
                    t.matmul(m.bank[0][0:NB, 1 + q:2 + q], m.ones[:, 0:NB], RF[:, q:q + 1], start=False, stop=True,
                             skip_group_check=True)
                for q in range(NQ):
                    last = t.matmul(m.bank[1][:, q * P:(q + 1) * P], m.RA[:, q:q + 1].to_broadcast([P, P]), m.ident[:, :],
                                    start=True, stop=True)
                last.then_inc(products_done, 1)
            else:
                pe.wait_ge(loaded, 32)
            pe.wait_ge(steps_done, k)
            t.matmul(m.bank[2][0:NB, 0:1], m.upto[0:NB, 0:NB], F, start=True, stop=True).then_inc(products_done, 1)
            pe.wait_ge(steps_done, k + 2)
            t.matmul(m.bank[3][0:1, 0:1], m.ones[0:NB, 0:1], F, start=True, stop=True)
            t.matmul(m.bank[3][0:1, 1:1 + NB], m.index[0:NB, 0:1], LST, start=True, stop=True).then_inc(products_done, 1)


def normalise(nc, m, tag, L=None):
    steps_done, std_ready, transposed, copied = m.sem(tag + "_ln"), m.sem(tag + "_ln_sqrt"), m.sem(tag + "_ln_tr"), m.sem(tag + "_ln_xnt")
    ST, MV, SD = m.small[:, 0:24], m.small[:, 24:32], m.small[:, 32:36]
    if L is not None:
        m.wq_loaded, m.wkv_loaded = m.sem(tag + "_wq"), m.sem(tag + "_wkv")
    with nc.Block() as block:
        @block.sync
        def _(sp):
            if L is not None:
                for t, src, sem in ((m.WQ, L.wq, m.wq_loaded), (m.WK, L.wk, m.wkv_loaded), (m.WV, L.wv, m.wkv_loaded)):
                    sp.dma_start(t[:, :, :], m.d[src].rearrange("(c p) n -> p c n", p=P)).then_inc(sem, 16)

        @block.vector
        def _(dve):
            v = nc.vector
            for t in range(NQ):
                v.bn_stats(ST[:, 6 * t:6 * t + 6], m.X[:, t, :]).then_inc(steps_done, 1)
            dve.wait_ge(steps_done, 4)
            for t in range(NQ):
                v.bn_aggr(MV[:, 2 * t:2 * t + 2], ST[:, 6 * t:6 * t + 6]).then_inc(steps_done, 1)
            dve.wait_ge(steps_done, 8)
            v.tensor_scalar(SD, MV.rearrange("p (t k) -> p t k", k=2)[:, :, 1], 1e-5, None, ALU.add).then_inc(steps_done, 1)
            dve.wait_ge(std_ready, 1)
            v.reciprocal(SD, SD).then_inc(steps_done, 1)
            dve.wait_ge(steps_done, 10)
            for t in range(NQ):
                v.tensor_scalar(m.XN[:, t, :], m.X[:, t, :], MV[:, 2 * t:2 * t + 1], SD[:, t:t + 1],
                                ALU.subtract, ALU.mult).then_inc(steps_done, 1)
            for c in (0, 2):
                dve.wait_ge(transposed, c + 1)
                v.tensor_copy(m.XNT[:, c, :], m.bank[c][:, :]).then_inc(copied, 1)

        @block.scalar
        def _(act):
            act.wait_ge(steps_done, 9)
            nc.scalar.activation(SD, SD, ACT.Sqrt).then_inc(std_ready, 1)
            for c in (1, 3):
                act.wait_ge(transposed, c + 1)
                nc.scalar.activation(m.XNT[:, c, :], m.bank[c][:, :], ACT.Copy).then_inc(copied, 1)
            act.wait_ge(copied, DC)

        @block.tensor
        def _(pe):
            pe.wait_ge(steps_done, 14)
            for c in range(DC):
                for t in range(NQ):
                    last = nc.tensor.transpose(m.bank[c][:, t * P:(t + 1) * P], m.XN[:, t, c * P:(c + 1) * P], m.ident[:, :])
                last.then_inc(transposed, 1)


def centre(nc, m, dve, W, steps_done, k):
    v = nc.vector
    Wg = W[:, :, :].rearrange("p c (h f) -> p (c h) f", f=HD)
    MW = m.small[:, 0:DC * H]
    v.tensor_reduce(MW, Wg, AX.X, ALU.add).then_inc(steps_done, 1)
    dve.wait_ge(steps_done, k + 1)
    v.tensor_scalar(MW, MW, 1.0 / HD, None, ALU.mult).then_inc(steps_done, 1)
    dve.wait_ge(steps_done, k + 2)
    v.tensor_tensor(Wg, Wg, MW.unsqueeze(2).to_broadcast([P, DC * H, HD]), ALU.subtract).then_inc(steps_done, 1)
    return k + 3


def queries(nc, m, L):
    n = L.name
    zeroed, steps_done, projected = m.sem(n + "_zeroed"), m.sem(n + "_q_dve"), m.sem(n + "_q_pe")
    squared, spread_ready, part1_ready, rest1_ready = m.sem(n + "_q_sq"), m.sem(n + "_q_var"), m.sem(n + "_q_part1"), m.sem(n + "_q_rest1")
    part2_ready, part3_ready, parts_stored, query_ready = m.sem(n + "_q_part2"), m.sem(n + "_q_part3"), m.sem(n + "_q_stored"), m.sem(n + "_q_full")
    stacks_loaded = m.q_loaded = m.sem(n + "_q_stacks")
    QF = m.XN
    CENTRED_Q, CENTRED_K, BIASES, INVERTED, SCALED = 5, 8, 13, 14, 18

    class Parts:
        read_out = steps_done if L.norm else query_ready
        read_out_at = SCALED if L.norm else DC
        keys_ready = CENTRED_K

        @staticmethod
        def sync(sp):
            for c in range(DC):
                sp.wait_ge(part3_ready, c + 1)
                for j in range(3):
                    sp.dma_start(m.QSAVE[j, :, c, :], m.QP[j][:, c, :]).then_inc(parts_stored, 16)
            if L.fixed is None:
                sp.wait_ge(zeroed, 1)
            for c in range(DC):
                sp.wait_ge(parts_stored, 16 * 3 * DC)
                for stack, parts in ((m.QA, (0, 1, 0)), (m.QB, (1, 2, 0))):
                    for j, part in enumerate(parts):
                        sp.dma_start(stack[HD * j:HD * j + HD, G * c:G * c + G, :],
                                     m.QSAVE[part, :, c, :].rearrange("(g f) n -> f g n", f=HD)).then_inc(stacks_loaded, 16)

        @staticmethod
        def gpsimd(pool):
            g = nc.gpsimd
            if L.fixed is None:
                g.memset(m.QB[3 * HD:P, :, :], 0.0).then_inc(zeroed, 1)
                pool.wait_ge(zeroed, 1)
            for c in range(DC + 1):
                if c < DC:
                    pool.wait_ge(part1_ready, c + 1)
                    g.tensor_tensor(QF[:, c, :], QF[:, c, :], m.QP[0][:, c, :], ALU.subtract).then_inc(rest1_ready, 1)
                if c:
                    pool.wait_ge(part2_ready, c)
                    g.tensor_tensor(m.QP[2][:, c - 1, :], QF[:, c - 1, :], m.QP[1][:, c - 1, :], ALU.subtract).then_inc(part3_ready, 1)

        @staticmethod
        def vector(dve):
            v = nc.vector
            v.memset(m.MX[:, :], LOWEST).then_inc(steps_done, 1)
            k = 2
            if L.norm:
                v.memset(m.RSTDS[:, :], 0.0).then_inc(steps_done, 1)
                dve.wait_ge(m.wq_loaded, 16)
                k = centre(nc, m, dve, m.WQ, steps_done, k)
                dve.wait_ge(m.wkv_loaded, 32)
                dve.wait_ge(steps_done, k)
                k = centre(nc, m, dve, m.WK, steps_done, k)
                dve.wait_ge(projected, 1)
                for j, b in enumerate((L.bq, L.bk)):
                    v.tensor_tensor(m.vec(b), m.vec(b), m.bank[7][:, 4 * j:4 * j + 4], ALU.subtract).then_inc(steps_done, 1)
                for b in ("qn_w", "qn_b"):
                    v.tensor_scalar(m.vec(b), m.vec(b), SCALE, None, ALU.mult).then_inc(steps_done, 1)
                v.memset(m.EPS[:, :], 1e-6).then_inc(steps_done, 1)
                k += 5
                dve.wait_ge(squared, 9)
                v.reciprocal(m.RSTD[:, :], m.RSTD[:, :]).then_inc(steps_done, 1)
                for c in range(DC):
                    dve.wait_ge(spread_ready, c + 2)
                    v.tensor_tensor(QF[:, c, :], QF[:, c, :], m.bank[2 + c][:, :], ALU.mult).then_inc(steps_done, 1)
            else:
                if not L.row_mask:
                    v.memset(m.RAROWS[:, :], SCALE).then_inc(steps_done, 1)
                else:
                    v.tensor_scalar(m.RAROWS[:, :], m.RAROW[:, :], SCALE, None, ALU.mult).then_inc(steps_done, 1)
                dve.wait_ge(steps_done, 2)
                for c in range(DC):
                    dve.wait_ge(projected, c + 1)
                    v.scalar_tensor_tensor(QF[:, c, :], m.bank[c % 2][:, :], m.vec(L.bq)[:, c:c + 1],
                                           m.RAROWS[:, :], ALU.add, ALU.mult).then_inc(query_ready, 1)

        @staticmethod
        def scalar(act):
            a = nc.scalar
            if L.norm:
                act.wait_ge(steps_done, BIASES)
                for c in range(DC):
                    act.wait_ge(projected, c + 2)
                    b = m.vec(L.bq)[:, c:c + 1]
                    a.activation(m.PB[:, 0, c, :], m.bank[c % 2][:, :], ACT.Square, bias=b).then_inc(squared, 1)
                    a.activation(QF[:, c, :], m.bank[c % 2][:, :], ACT.Identity, bias=b).then_inc(squared, 1)
                act.wait_ge(spread_ready, 1)
                a.activation(m.RSTD[:, :], m.bank[6][0:H, :], ACT.Sqrt, bias=m.EPS[0:H, :]).then_inc(squared, 1)
                for c in range(DC):
                    act.wait_ge(steps_done, INVERTED + c + 1)
                    a.activation(QF[:, c, :], QF[:, c, :], ACT.Identity, bias=m.vec("qn_b")[:, 0:1],
                                 scale=m.vec("qn_w")[:, 0:1]).then_inc(query_ready, 1)
            for c in range(DC + 1):
                if c < DC:
                    act.wait_ge(query_ready, c + 1)
                    a.activation(m.QP[0][:, c, :], QF[:, c, :], ACT.Copy).then_inc(part1_ready, 1)
                if c:
                    act.wait_ge(rest1_ready, c)
                    a.activation(m.QP[1][:, c - 1, :], QF[:, c - 1, :], ACT.Copy).then_inc(part2_ready, 1)

        @staticmethod
        def tensor(pe):
            t = nc.tensor
            pe.wait_ge(m.wq_loaded, 16)
            if L.norm:
                for j, b in enumerate((L.bq, L.bk)):
                    last = t.matmul(m.bank[7][:, 4 * j:4 * j + 4], m.gmean[:, :], m.vec(b), start=True, stop=True)
                last.then_inc(projected, 1)
                pe.wait_ge(steps_done, CENTRED_Q)
            for c in range(DC):
                if c >= 2:
                    pe.wait_ge(squared if L.norm else query_ready, 2 * (c - 1) if L.norm else c - 1)
                for d in range(DC):
                    last = t.matmul(m.bank[c % 2][:, :], m.WQ[:, d, c * P:(c + 1) * P], m.XNT[:, d, :],
                                    start=d == 0, stop=d == DC - 1)
                last.then_inc(projected, 1)
            if L.norm:
                pe.wait_ge(squared, 8)
                for c in range(DC):
                    last = t.matmul(m.bank[6][0:H, :], m.head_mean[:, H * c:H * c + H], m.PB[:, 0, c, :],
                                    start=c == 0, stop=c == DC - 1)
                last.then_inc(spread_ready, 1)
                pe.wait_ge(steps_done, INVERTED)
                for c in range(DC):
                    t.matmul(m.bank[2 + c][:, :], m.spread[c][:, :], m.RSTDS[:, :], start=True, stop=True).then_inc(spread_ready, 1)

    return Parts


def row_maxima(nc, m, L):
    Q = queries(nc, m, L)
    m.fresh = []
    n = L.name + "_max"
    context_loaded = [m.sem(f"{n}_ctx{kb}") for kb in range(KT_)]
    mask_loaded, projected, bank_read, values_ready = m.sem(n + "_mask"), m.sem(n + "_proj"), m.sem(n + "_sq"), m.sem(n + "_v")
    scores_ready, scores_taken, bias_ready = m.sem(n + "_scores"), m.sem(n + "_taken"), m.sem(n + "_bias")
    part1_ready, rest1_ready, part2_ready, part3_ready = m.sem(n + "_part1"), m.sem(n + "_rest1"), m.sem(n + "_part2"), m.sem(n + "_part3")
    values_stored, spread_ready, std_ready, inverse_ready, keys_scaled, keys_final = (m.sem(n + x) for x in ("_vstored", "_var", "_std", "_rstd", "_knorm", "_kfull"))
    stack_loaded = [m.sem(f"{n}_stack{c}") for c in range(DC)]
    keys_stored = [m.sem(f"{n}_kstored{c}") for c in range(DC)]
    count_loaded, counted = [m.sem(f"{n}_count_mask{u}") for u in range(4)], m.sem(n + "_counted")
    NS = H * NQ
    dyn = L.fixed is None
    src = m.CT if dyn else m.XNT
    counting = L.norm
    mask_summed = m.sem(n + "_summed")
    if not dyn:
        m.kbs_loaded = m.sem(n + "_kbs")
    K_AT = list(range(4, 36, 2))
    VAR_AT, INVERSE_AT, SPREAD_AT, SCALE_AT = [15, 23, 31, 36], 42, [47, 51, 55, 59], [49, 53, 57, 61]
    V_AT = [37, 39, 41, 43, 44, 45, 46, 48, 49, 50, 52, 54, 56, 58, 60, 61] if L.norm else \
        [35, 37, 39, 40, 42, 44, 46, 47, 49, 51, 53, 54, 56, 58, 60, 61]
    STORES = "k0 k1 s0 k2 s1 k3 v s2 s3" if L.norm else "k0 k1 s0 k2 k3 s1 s2 v s3"
    B = raised(nc, m, dyn)

    def load_context(eng, j, kbs):
        at = slice(L.count + 1 + j, L.count + 2 + j) if isinstance(j, int) else bass.ds(j + (L.count + 1), 1)
        b = eng.value_load(m.CTL[0:1, at], min_val=0, max_val=NB - 1)
        for kb in kbs:
            eng.dma_start(m.CT[:, :, kb * P:(kb + 1) * P],
                          m.d["ctx"][bass.ds(b, 1), :, :, kb * P:(kb + 1) * P].rearrange("a p c k -> (a p) c k")).then_inc(context_loaded[kb], 16)

    with nc.Block() as block:
        @block.sync
        def _(sp):
            nb = blocks_to_do(sp, m, L)

            def load_mask(j):
                b = sp.value_load(m.CTL[0:1, (bass.ds(j + (L.count + 1), 1) if not isinstance(j, int) else slice(j + L.count + 1, j + L.count + 2))],
                                  min_val=0, max_val=NB - 1)
                if L.row_mask:
                    sp.dma_start(m.MI[:, :, :], m.d["mask_q"][bass.ds(b, 1)].rearrange("a p t k -> (a p) t k")).then_inc(mask_loaded, 16)
                else:
                    sp.dma_start(m.KMW[:, :], m.d["keymask"][bass.ds(b, 1)].to_broadcast([P, KB // 4])).then_inc(mask_loaded, 16)

            def keep_keys(j, c):
                wait_alone(sp, part3_ready, j * DC + c + 1 + B)
                sp.dma_start(m.KSAVE[one(j), :, :, c, :].rearrange("a p k n -> (a p) k n"), m.PARTS[:, :, c, :]).then_inc(keys_stored[c], 16)

            def keep_values(j):
                wait_alone(sp, values_ready, j * KT_ + KT_ + B)
                sp.dma_start(m.VSAVE[one(j)].rearrange("a p k n -> (a p) k n"), m.V[:, :, :]).then_inc(values_stored, 16)

            def stack(j, c):
                wait_alone(sp, keys_stored[c], j * 16 + 16 + B)
                for r, part in enumerate((0, 0, 1)):
                    sp.dma_start(m.KA[HD * r:HD * r + HD, G * c:G * c + G, :],
                                 m.KSAVE[one(j), :, part, c, :].rearrange("a (g f) n -> (a f) g n", f=HD)).then_inc(stack_loaded[c], 16)

            if dyn:
                load_context(sp, 0, range(KT_))
                load_mask(0)
            else:
                sp.dma_start(m.MB[:, :, :], m.d["biases"][L.fixed, 0]).then_inc(mask_loaded, 16)
            Q.sync(sp)
            for c in range(DC):
                keep_keys(0, c)
                if c:
                    stack(0, c - 1)
            stack(0, DC - 1)
            if not dyn:
                for c in range(DC):
                    for r, part in enumerate((1, 0, 2)):
                        sp.dma_start(m.KBS[HD * r:HD * r + HD, G * c:G * c + G, :],
                                     m.KSAVE[0, :, part, c, :].rearrange("(g f) n -> f g n", f=HD)).then_inc(m.kbs_loaded, 16)
                for j in range(BIAS_PARTS[L.fixed]):
                    sp.dma_start(m.MBF[j], m.d["bias_parts"][L.fixed, :, j]).then_inc(m.kbs_loaded, 16)
                return
            keep_values(0)

            def keep_next(i):
                wait_alone(sp, bias_ready, i + 1 + B)
                load_mask(i + 1)
                for step in STORES.split():
                    c = int(step[1:] or 0)
                    if step[0] == "k":
                        keep_keys(i + 1, c)
                    elif step[0] == "s":
                        wait_alone(sp, scores_taken, i * NS + (c + 1) * G * NQ + B)
                        stack(i + 1, c)
                    else:
                        keep_values(i + 1)

            def load_counted(i):
                with sp.If(i < NB // 4):
                    i4 = first_iterations(nc, i)
                    wait_alone(sp, counted, i * 4 * NQ + B)
                    for u in range(4):
                        sp.dma_start(m.COUNT[u], m.d["mask_q"][bass.ds(i4 * 4 + u, 1)].rearrange("a p t k -> (a p) t k")).then_inc(count_loaded[u], 16)

            def body(i):
                if counting:
                    load_counted(i)
                with sp.If(i + 1 < nb):
                    keep_next(i)

            def count_rest(i):
                with sp.If(i >= nb):
                    load_counted(i)

            active_loop(sp, nb, body, count_rest if counting else None)
            wait_alone(sp, values_stored, nb * 16 + B)
            m.past = context_loaded

        @block.tensor
        def _(pe):
            nb = blocks_to_do(pe, m, L)
            t = nc.tensor

            def project_keys(j, x, d):
                if x == 0 and d == 0 and dyn:
                    for kb in range(KT_):
                        pe.wait_ge(context_loaded[kb], j * 16 + 16 + B)
                if d == 0:
                    pe.wait_ge(bank_read, j * (2 * DC) + max(0, x - 1) * 2 + B)
                last = t.matmul(m.bank[x % 2][:, :], m.WK[:, d, x * P:(x + 1) * P], src[:, d, :],
                                start=d == 0, stop=d == DC - 1)
                if d == DC - 1:
                    last.then_inc(projected, 1)

            def variances(j, d):
                if d == 0:
                    pe.wait_ge(keys_scaled, j * DC + B)
                pe.wait_ge(bank_read, j * (2 * DC) + 2 * d + 2 + B)
                last = t.matmul(m.bank[3][0:H, :], m.head_mean[:, H * d:H * d + H], m.PB[:, 0, d, :],
                                start=d == 0, stop=d == DC - 1)
                if d == DC - 1:
                    last.then_inc(spread_ready, 1)

            def project_values(j, kb, d):
                if d == 0:
                    pe.wait_ge(values_ready, j * KT_ + kb + B)
                last = t.matmul(m.bank[2][:, :], src[:, d, kb * P:(kb + 1) * P], m.WV[:, d, :],
                                start=d == 0, stop=d == DC - 1)
                if d == DC - 1:
                    last.then_inc(projected, 1)

            def spread(j, c):
                pe.wait_ge(inverse_ready, j + 1 + B)
                pe.wait_ge(keys_scaled, j * DC + c + B)
                t.matmul(m.bank[3][:, :], m.spread[c][:, :], m.RSTDS[:, :], start=True, stop=True).then_inc(spread_ready, 1)

            def scores(i, ahead):
                for k in range(NS):
                    h, q = k // NQ, k % NQ
                    k0, k1 = L.keys_of[q]
                    if k % (G * NQ) == 0:
                        pe.wait_ge(stack_loaded[h // G], i * 48 + 48 + B)
                    pe.wait_ge(scores_taken, i * NS + max(0, k - 3) + B)
                    t.matmul(m.bank[4 + k % 4][:, k0:k1], m.QA[0:3 * HD, h, q * P:(q + 1) * P], m.KA[0:3 * HD, h, k0:k1],
                             start=True, stop=True).then_inc(scores_ready, 1)
                    if ahead and k in K_AT:
                        project_keys(i + 1, K_AT.index(k) // DC, K_AT.index(k) % DC)
                    if ahead and L.norm and k in VAR_AT:
                        variances(i + 1, VAR_AT.index(k))
                    if ahead and L.norm and k in SPREAD_AT:
                        spread(i + 1, SPREAD_AT.index(k))
                    if ahead and k in V_AT:
                        project_values(i + 1, V_AT.index(k) // DC, V_AT.index(k) % DC)

            Q.tensor(pe)
            pe.wait_ge(m.wkv_loaded, 32)
            if L.norm:
                pe.wait_ge(Q.read_out, Q.keys_ready)
            else:
                pe.wait_ge(Q.read_out, Q.read_out_at)
            for x in range(DC):
                for d in range(DC):
                    project_keys(0, x, d)
            pe.wait_ge(Q.read_out, Q.read_out_at)
            if L.norm:
                for d in range(DC):
                    variances(0, d)
            for kb in range(KT_):
                for d in range(DC):
                    project_values(0, kb, d)
                if L.norm and kb:
                    spread(0, kb - 1)
            if L.norm:
                spread(0, DC - 1)
            pe.wait_ge(m.q_loaded, 16 * 3 * 2 * DC)
            if not dyn:
                scores(0, False)
                return

            def body(i):
                with pe.If(i + 1 < nb):
                    scores(i, True)
                with pe.If(i + 1 >= nb):
                    scores(i, False)

            active_loop(pe, nb, body)

        @block.scalar
        def _(act):
            nb = blocks_to_do(act, m, L)
            a = nc.scalar

            def count(i, u):
                act.wait_ge(count_loaded[u], i * 16 + 16 + B)
                for q in range(NQ):
                    a.activation(m.COUNT[u][:, q, :], m.COUNT[u][:, q, :], ACT.Square, bias=m.MINUS1[:, :],
                                 accum_out=m.UNMASKED[:, q, bass.ds(i * 4 + u, 1)]).then_inc(counted, 1)

            def evacuate(j, meanwhile=lambda u: None):
                def second(c):
                    act.wait_ge(rest1_ready, j * DC + c + 1 + B)
                    a.activation(m.PARTS[:, 1, c, :], m.KF[:, c, :], ACT.Copy).then_inc(part2_ready, 1)

                def values(kb):
                    act.wait_ge(projected, j * (2 * DC) + DC + kb + 1 + B)
                    a.activation(m.V[:, kb, :], m.bank[2][:, :], ACT.Copy).then_inc(values_ready, 1)
                    if dyn:
                        load_context(act, j + 1, [kb])

                for c in range(DC):
                    act.wait_ge(keys_stored[c], j * 16 + B)
                    act.wait_ge(projected, j * (2 * DC) + c + 1 + B)
                    b = m.vec(L.bk)[:, c:c + 1]
                    if L.norm:
                        a.activation(m.PB[:, 0, c, :], m.bank[c % 2][:, :], ACT.Square, bias=b).then_inc(bank_read, 1)
                        a.activation(m.KF[:, c, :], m.bank[c % 2][:, :], ACT.Identity, bias=b).then_inc(bank_read, 1)
                    else:
                        a.activation(m.KF[:, c, :], m.bank[c % 2][:, :], ACT.Identity, bias=b).then_inc(bank_read, 1)
                        a.activation(m.PARTS[:, 0, c, :], m.bank[c % 2][:, :], ACT.Identity, bias=b).then_inc(bank_read, 1)
                        if c:
                            second(c - 1)
                    if c in (1, 2):
                        meanwhile(c - 1)
                if L.norm:
                    act.wait_ge(spread_ready, j * 5 + 1 + B)
                    a.activation(m.RSTD[:, :], m.bank[3][0:H, :], ACT.Sqrt, bias=m.EPS[0:H, :]).then_inc(std_ready, 1)
                meanwhile(2)
                act.wait_ge(values_stored, j * 16 + B)
                values(0)
                meanwhile(3)
                if not L.norm:
                    second(DC - 1)
                    for kb in range(1, KT_):
                        values(kb)
                    return
                for c in range(DC):
                    if c + 1 < KT_:
                        values(c + 1)
                    act.wait_ge(keys_scaled, j * DC + c + 1 + B)
                    a.activation(m.KF[:, c, :], m.KF[:, c, :], ACT.Identity, bias=m.vec("kn_b")[:, 0:1],
                                 scale=m.vec("kn_w")[:, 0:1]).then_inc(keys_final, 1)
                    act.wait_ge(keys_final, j * DC + c + 1 + B)
                    a.activation(m.PARTS[:, 0, c, :], m.KF[:, c, :], ACT.Copy).then_inc(part1_ready, 1)
                    second(c)

            Q.scalar(act)
            evacuate(0)
            if not dyn:
                return

            def masked(i):
                act.wait_ge(bias_ready, i + 1 + B)
                for q in range(NQ):
                    a.activation(m.PB[:, 0, q, :], m.MB[:, q, :], ACT.Copy, accum_out=m.SUMS[:, q, one(i)]).then_inc(mask_summed, 1)

            def body(i):
                if L.row_mask:
                    masked(i)

                def count_one(c):
                    with act.If(i < NB // 4):
                        count(first_iterations(nc, i), c)

                with act.If(i + 1 < nb):
                    evacuate(i + 1, count_one if counting else lambda c: None)

            def count_four(i):
                with act.If(i < NB // 4):
                    with act.If(i + 1 >= nb):
                        for u in range(4):
                            count(first_iterations(nc, i), u)

            active_loop(act, nb, body, count_four if counting else None)

        @block.gpsimd
        def _(pool):
            nb = blocks_to_do(pool, m, L)
            g = nc.gpsimd

            def rest(j, c):
                if L.norm:
                    pool.wait_ge(part1_ready, j * DC + c + 1 + B)
                else:
                    pool.wait_ge(bank_read, j * (2 * DC) + 2 * c + 2 + B)
                g.tensor_tensor(m.KF[:, c, :], m.KF[:, c, :], m.PARTS[:, 0, c, :], ALU.subtract).then_inc(rest1_ready, 1)

            def third(j, c):
                pool.wait_ge(part2_ready, j * DC + c + 1 + B)
                g.tensor_tensor(m.PARTS[:, 2, c, :], m.KF[:, c, :], m.PARTS[:, 1, c, :], ALU.subtract).then_inc(part3_ready, 1)

            def split(j):
                for c in range(DC):
                    rest(j, c)
                    if L.norm:
                        third(j, c)
                    elif c:
                        third(j, c - 1)
                if not L.norm:
                    third(j, DC - 1)

            Q.gpsimd(pool)
            split(0)
            if not dyn:
                return

            def body(i):
                with pool.If(i + 1 < nb):
                    split(i + 1)

            active_loop(pool, nb, body)

        @block.vector
        def _(dve):
            nb = blocks_to_do(dve, m, L)
            v = nc.vector

            def inverse(j):
                dve.wait_ge(std_ready, j + 1 + B)
                v.reciprocal(m.RSTD[:, :], m.RSTD[:, :]).then_inc(inverse_ready, 1)

            def scale(j, c):
                dve.wait_ge(spread_ready, j * 5 + 2 + c + B)
                v.tensor_tensor(m.KF[:, c, :], m.KF[:, c, :], m.bank[3][:, :], ALU.mult).then_inc(keys_scaled, 1)

            def maxima(i, ahead):
                if dyn:
                    dve.wait_ge(scores_taken, i * NS + B)
                    dve.wait_ge(mask_loaded, i * 16 + 16 + B)
                    if L.row_mask:
                        dve.wait_ge(mask_summed, i * NQ + B)
                        for q in range(NQ):
                            last = v.tensor_scalar(m.MB[:, q, :], m.MI[:, q, :], 1.0, m.RN[:, q:q + 1], ALU.is_equal, ALU.mult)
                    else:
                        last = v.tensor_scalar(m.MB[:, 0, :], m.KM[:, 0:KB], 1.0, -NEG, ALU.subtract, ALU.mult)
                    last.then_inc(bias_ready, 1)
                    dve.wait_ge(bias_ready, i + 1 + B)
                else:
                    dve.wait_ge(mask_loaded, 16)
                for k in range(NS):
                    q = k % NQ
                    k0, k1 = L.keys_of[q]
                    bias = m.MB[:, q if (L.row_mask or not dyn) else 0, k0:k1]
                    dve.wait_ge(scores_taken, i * NS + max(0, k - 3) + B)
                    wait_alone(dve, scores_ready, i * NS + k + 1 + B)
                    v.tensor_tensor_reduce(m.JUNK[:, k % 4, k0:k1], m.bank[4 + k % 4][:, k0:k1], bias, 1.0, m.MX[:, k:k + 1],
                                           ALU.add, ALU.max, m.MX[:, k:k + 1]).then_inc(scores_taken, 1)
                    if ahead and L.norm:
                        if k == INVERSE_AT:
                            inverse(i + 1)
                        if k in SCALE_AT:
                            scale(i + 1, SCALE_AT.index(k))

            Q.vector(dve)
            if L.norm:
                inverse(0)
                for c in range(DC):
                    scale(0, c)
            if not dyn:
                maxima(0, False)
                return

            def body(i):
                with dve.If(i + 1 < nb):
                    maxima(i, True)
                with dve.If(i + 1 >= nb):
                    maxima(i, False)

            active_loop(dve, nb, body)


def shifts(nc, m, L):
    n = L.name
    steps_done, transposed, shifts_stacked = m.sem(n + "_shift_dve"), m.sem(n + "_shift_tr"), m.sem(n + "_shift_stored")
    sums_zeroed, ones_written = m.sem(n + "_sums_zero"), m.sem(n + "_ones")
    m.wo_loaded = m.sem(n + "_wo")
    R, PART = m.small[:, 0:64], m.MXB

    class Parts:
        flags = steps_done
        zeroed = sums_zeroed
        ones_set = ones_written
        stored = shifts_stacked

        @staticmethod
        def load_output_weights(sp):
            sp.dma_start(m.WQ[:, :, :], m.d[L.wo].rearrange("(c p) n -> p c n", p=P)).then_inc(m.wo_loaded, 16)
            sp.dma_start(m.RAROWS[:, :], m.d["bo"][L.bo]).then_inc(m.wo_loaded, 16)

        @staticmethod
        def sync(sp):
            sp.wait_ge(steps_done, 11)
            for j in range(3):
                sp.dma_start(m.QB[3 * HD + j:3 * HD + j + 1, :, :], m.NM[H * j:H * j + H, :]).then_inc(shifts_stacked, 16)

        @staticmethod
        def gpsimd(pool):
            if L.fixed is None:
                nc.gpsimd.memset(m.KBS[3 * HD:P, :, :], 1.0).then_inc(ones_written, 1)
                pool.wait_ge(ones_written, 1)
            nc.gpsimd.memset(m.OACC[:, :, :], 0.0).then_inc(sums_zeroed, 1)
            nc.gpsimd.memset(m.DACC[:, :, :], 0.0).then_inc(sums_zeroed, 1)

        @staticmethod
        def vector(dve):
            v = nc.vector
            v.tensor_scalar(R, m.MX[:, :], -1.0, None, ALU.mult).then_inc(steps_done, 1)
            k = 1
            out = m.NMX[:, :].rearrange("p (q j h) -> p j q h", q=NQ, j=3)
            for j in range(3):
                dve.wait_ge(steps_done, k)
                v.tensor_copy(PART[:, :], R).then_inc(steps_done, 1)
                dve.wait_ge(steps_done, k + 1)
                v.tensor_copy(out[:, j], PART[:, :].rearrange("p (h q) -> p q h", q=NQ)).then_inc(steps_done, 1)
                v.tensor_tensor(R, R, PART[:, :], ALU.subtract).then_inc(steps_done, 1)
                k += 3
            dve.wait_ge(transposed, 1)
            v.tensor_copy(m.NM[:, :], m.bank[0][0:3 * H, :]).then_inc(steps_done, 1)
            if L.row_mask:
                F = m.small[0:1, 64:64 + NB]
                v.tensor_reduce(F, m.bank[1][0:1, 0:NQ * NB].rearrange("p (t b) -> p b t", b=NB), AX.X, ALU.add).then_inc(steps_done, 1)
                dve.wait_ge(steps_done, 12)
                v.tensor_scalar(m.CTL[0:1, C_M:C_M + NB], F, 0.0, None, ALU.is_lt).then_inc(steps_done, 1)

        @staticmethod
        def tensor(pe):
            if L.row_mask:
                nc.tensor.matmul(m.bank[1][0:1, 0:NQ * NB], m.ones[:, 0:1], m.SUMS[:, :, :], start=True, stop=True)
            pe.wait_ge(steps_done, 10)
            for q in range(NQ):
                last = nc.tensor.transpose(m.bank[0][0:3 * H, q * P:(q + 1) * P], m.NMX[:, q * 3 * H:(q + 1) * 3 * H], m.ident[:, :])
            last.then_inc(transposed, 1)

    return Parts


def project_out(nc, m, L):
    n = L.name + "_out"
    steps_done, output_ready, x_added, chunk_ready = (m.sem(n + x) for x in ("_dve", "_proj", "_x", "_biased"))

    class Parts:
        @staticmethod
        def tensor(pe):
            pe.wait_ge(m.wo_loaded, 32)
            for c in range(DC):
                pe.wait_ge(chunk_ready, c + 1)
                for q in range(NQ):
                    last = nc.tensor.matmul(m.bank[4 + q][:, :], m.OACC[:, c, q * P:(q + 1) * P], m.WQ[:, c, :],
                                            start=c == 0, stop=c == DC - 1)
                    if c == DC - 1:
                        last.then_inc(output_ready, 1)

        @staticmethod
        def gpsimd(pool):
            pool.wait_ge(m.wo_loaded, 32)
            for q in range(NQ):
                nc.gpsimd.tensor_tensor(m.X[:, q, :], m.X[:, q, :], m.RAROWS[:, :], ALU.add).then_inc(x_added, 1)

        @staticmethod
        def scalar(act):
            for c in range(DC):
                act.wait_ge(steps_done, 2 * c + 2)
                nc.scalar.activation(m.OACC[:, c, :], m.OACC[:, c, :], ACT.Identity,
                                     bias=m.vec(L.bv)[:, c:c + 1]).then_inc(chunk_ready, 1)

        @staticmethod
        def vector(dve):
            v = nc.vector
            for c in range(DC):
                v.reciprocal(m.DACC[:, c, :], m.DACC[:, c, :]).then_inc(steps_done, 1)
                dve.wait_ge(steps_done, 2 * c + 1)
                v.tensor_tensor(m.OACC[:, c, :], m.OACC[:, c, :], m.DACC[:, c, :], ALU.mult).then_inc(steps_done, 1)
            dve.wait_ge(x_added, NQ)
            for q in range(NQ):
                dve.wait_ge(output_ready, q + 1)
                v.tensor_tensor(m.X[:, q, :], m.X[:, q, :], m.bank[4 + q][:, :], ALU.add).then_inc(x_added, 1)
            dve.wait_ge(x_added, 2 * NQ)

    return Parts


def weighted_values(nc, m, L):
    M, O = shifts(nc, m, L), project_out(nc, m, L)
    m.fresh = []
    n = L.name + "_pv"
    mask_loaded, scores_ready, exp_ready, product_done, sum_taken = (m.sem(n + x) for x in ("_mask", "_scores", "_exp", "_product", "_psum"))
    denominators_ready, added_up, bias_ready, sum_zeroed = (m.sem(n + x) for x in ("_den", "_acc", "_bias", "_zeroed"))
    keys_loaded = [m.sem(f"{n}_keys{c}") for c in range(DC)]
    steps = [(c, k) for c in range(DC) for k in range(KT_)]
    NS = len(steps)
    dyn = L.fixed is None
    kt = L.order
    PER = 7 * 16
    NBI = KT_ if L.row_mask else 1
    B = raised(nc, m, dyn)
    with nc.Block() as block:
        @block.sync
        def _(sp):
            nb = blocks_to_do(sp, m, L)

            def load_mask(j):
                b = sp.value_load(m.CTL[0:1, (bass.ds(j + (L.count + 1), 1) if not isinstance(j, int) else slice(j + L.count + 1, j + L.count + 2))],
                                  min_val=0, max_val=NB - 1)
                if L.row_mask:
                    sp.dma_start(m.MI[:, :, :], m.d["mask_k"][bass.ds(b, 1)].rearrange("a p t k -> (a p) t k")).then_inc(mask_loaded, 16)
                else:
                    sp.dma_start(m.KMW[:, 0:1], m.d["keymask_k"][bass.ds(b, 1)].rearrange("a p t -> (a p) t")).then_inc(mask_loaded, 16)

            def load_keys(j, c):
                for stack, parts in ((m.KA, (0, 0, 1)), (m.KBS, (1, 0, 2))):
                    for r, part in enumerate(parts):
                        sp.dma_start(stack[HD * r:HD * r + HD, G * c:G * c + G, :],
                                     m.KSAVE[one(j), :, part, c, :].rearrange("a (g f) n -> (a f) g n", f=HD)).then_inc(keys_loaded[c], 16)
                sp.dma_start(m.V[:, :, c * P:(c + 1) * P],
                             m.VSAVE[one(j), :, :, c * P:(c + 1) * P].rearrange("a p k n -> (a p) k n")).then_inc(keys_loaded[c], 16)

            if dyn:
                load_mask(0)
                load_keys(0, 0)
            M.sync(sp)
            for c in range(1, DC if dyn else 0):
                load_keys(0, c)
            if dyn:
                for sem in m.past:
                    wait_alone(sp, sem, nb * 16 + 16 + B)
            M.load_output_weights(sp)
            if not dyn:
                return
            def body(i):
                with sp.If(i + 1 < nb):
                    wait_alone(sp, bias_ready, i * NBI + NBI + B)
                    load_mask(i + 1)
                    for c in range(DC):
                        wait_alone(sp, product_done, i * NS + (c + 1) * KT_ + B)
                        load_keys(i + 1, c)

            active_loop(sp, nb, body)

        @block.tensor
        def _(pe):
            nb = blocks_to_do(pe, m, L)
            t = nc.tensor

            def times_values(i, s):
                c, k = steps[s]
                q0, q1 = L.queries_of[kt[k]]
                if k == 0:
                    pe.wait_ge(added_up, i * (2 * DC) + 2 * max(0, c - 1) + B)
                pe.wait_ge(exp_ready, i * (NS * G) + G * s + G + B)
                for g in range(G):
                    h = G * c + g
                    last = t.matmul(m.bank[2 + c % 2][HD * g:HD * g + HD, q0:q1], m.V[:, kt[k], HD * h:HD * h + HD],
                                    m.PB[:, s % 2, g, q0:q1], start=k == 0, stop=k == KT_ - 1,
                                    skip_group_check=not dyn)
                last.then_inc(product_done, 1)

            def denominators(i, c):
                pe.wait_ge(sum_taken, i * NS + KT_ * c + KT_ + B)
                for g in range(G):
                    last = t.matmul(m.bank[c % 2][HD * g:HD * g + HD, :], m.ones[:, 0:HD], m.PS[:, g, :],
                                    start=True, stop=True)
                last.then_inc(denominators_ready, 1)

            def scores(i, s, masked):
                c, k = steps[s]
                q0, q1 = L.queries_of[kt[k]]
                if c == 0 and L.row_mask:
                    pe.wait_ge(bias_ready, i * NBI + k + 1 + B)
                if k == 0 and dyn:
                    pe.wait_ge(keys_loaded[c], i * PER + PER + B)
                for g in range(G):
                    h = G * c + g
                    pe.wait_ge(exp_ready, i * (NS * G) + (G * (s - 1) + g + 1 if s or not isinstance(i, int) else 0) + B)
                    o = m.bank[4 + g][:, q0:q1]
                    ks = slice(kt[k] * P, (kt[k] + 1) * P)
                    biases = []
                    if masked:
                        biases = [m.MBK[:, kt[k], q0:q1]]
                    elif not dyn:
                        parts = BIAS_PARTS[L.fixed] if kt[k] in (0, KT_ - 1) else 1
                        biases = [m.MBF[j][:, kt[k], q0:q1] for j in range(parts)]
                    for j, b in enumerate(biases):
                        t.matmul(o, m.IDB[:, :], b, start=j == 0, stop=False)
                    t.matmul(o, m.KA[0:3 * HD, h, ks], m.QA[0:3 * HD, h, q0:q1], start=not biases, stop=False)
                    t.matmul(o, m.KBS[:, h, ks], m.QB[:, h, q0:q1], start=False, stop=True).then_inc(scores_ready, 1)

            def first_scores(i):
                if not L.row_mask:
                    scores(i, 0, False)
                    return
                flag = pe.value_load(m.CTL[0:1, slice(C_M, C_M + 1) if isinstance(i, int) else bass.ds(i + C_M, 1)], min_val=0, max_val=1)
                with pe.If(flag > 0):
                    scores(i, 0, True)
                with pe.If(flag < 1):
                    scores(i, 0, False)

            def all_steps(i, masked):
                for s in range(1, NS + 1):
                    if s < NS:
                        scores(i, s, masked)
                    elif dyn:
                        with pe.If(i + 1 < nb):
                            first_scores(i + 1)
                    times_values(i, s - 1)
                    if s % KT_ == 0 and s < NS:
                        denominators(i, s // KT_ - 1)
                denominators(i, DC - 1)

            def body(i):
                if not L.row_mask:
                    all_steps(i, False)
                    return
                flag = pe.value_load(m.CTL[0:1, bass.ds(i + C_M, 1)], min_val=0, max_val=1)
                with pe.If(flag > 0):
                    all_steps(i, True)
                with pe.If(flag < 1):
                    all_steps(i, False)

            M.tensor(pe)
            pe.wait_ge(M.stored, 48)
            if dyn:
                pe.wait_ge(M.ones_set, 1)
            if not dyn:
                pe.wait_ge(m.kbs_loaded, 16 * (3 * DC + BIAS_PARTS[L.fixed]))
            if L.row_mask:
                pe.wait_ge(M.flags, 13)
            first_scores(0)
            over_blocks(pe, L, nb, body)
            O.tensor(pe)

        @block.gpsimd
        def _(pool):
            M.gpsimd(pool)
            O.gpsimd(pool)

        @block.scalar
        def _(act):
            nb = blocks_to_do(act, m, L)
            a = nc.scalar

            def exponentials(i, s):
                c, k = steps[s]
                q0, q1 = L.queries_of[kt[k]]
                if s == 0 and dyn and not L.row_mask:
                    act.wait_ge(bias_ready, i + 1 + B)
                before = s - 1 if s or not isinstance(i, int) else 0
                act.wait_ge(product_done, i * NS + before + B)
                act.wait_ge(sum_taken, i * NS + before + B)
                for g in range(G):
                    act.wait_ge(scores_ready, i * (NS * G) + G * s + g + 1 + B)
                    kw = {}
                    if dyn and not L.row_mask:
                        kw["bias"] = m.KBIAS[:, kt[k]:kt[k] + 1]
                    a.activation(m.PB[:, s % 2, g, q0:q1], m.bank[4 + g][:, q0:q1], ACT.Exp, **kw).then_inc(exp_ready, 1)

            def body(i):
                for s in range(1, NS):
                    exponentials(i, s)
                if dyn:
                    with act.If(i + 1 < nb):
                        exponentials(i + 1, 0)

            exponentials(0, 0)
            over_blocks(act, L, nb, body)
            O.scalar(act)

        @block.vector
        def _(dve):
            nb = blocks_to_do(dve, m, L)
            v = nc.vector

            def bias(i, kb):
                dve.wait_ge(mask_loaded, i * 16 + 16 + B)
                if L.row_mask:
                    v.scalar_tensor_tensor(m.MBK[:, kb, :], m.MI[:, kb, :], 1.0, m.RNROW[:, :],
                                           ALU.is_equal, ALU.mult).then_inc(bias_ready, 1)
                else:
                    v.tensor_scalar(m.KBIAS[:, :], m.KM[:, 0:KT_], 1.0, -NEG, ALU.subtract, ALU.mult).then_inc(bias_ready, 1)

            def body(i):
                def add_up(c):
                    dve.wait_ge(added_up, i * (2 * DC) + 2 * c + B)
                    dve.wait_ge(product_done, i * NS + KT_ * c + KT_ + B)
                    v.tensor_tensor(m.OACC[:, c, :], m.OACC[:, c, :], m.bank[2 + c % 2][:, :], ALU.add).then_inc(added_up, 1)
                    dve.wait_ge(denominators_ready, i * DC + c + 1 + B)
                    v.tensor_tensor(m.DACC[:, c, :], m.DACC[:, c, :], m.bank[c % 2][:, :], ALU.add).then_inc(added_up, 1)

                for s, (c, k) in enumerate(steps):
                    q0, q1 = L.queries_of[kt[k]]
                    if k == 0:
                        dve.wait_ge(denominators_ready, i * DC + c + B)
                        if (q0, q1) != (0, T):
                            v.memset(m.PS[:, :, :], 0.0).then_inc(sum_zeroed, 1)
                            dve.wait_ge(sum_zeroed, c + 1)
                    dve.wait_ge(exp_ready, i * (NS * G) + G * s + G + B)
                    dve.wait_ge(sum_taken, i * NS + s + B)
                    dst = m.PS[:, :, q0:q1]
                    if k == 0 and (q0, q1) == (0, T):
                        v.tensor_copy(dst, m.PB[:, s % 2]).then_inc(sum_taken, 1)
                    else:
                        v.tensor_tensor(dst, dst, m.PB[:, s % 2, :, q0:q1], ALU.add).then_inc(sum_taken, 1)
                    if k == 1 and c:
                        add_up(c - 1)
                    if dyn and NS - s <= NBI:
                        with dve.If(i + 1 < nb):
                            bias(i + 1, s - (NS - NBI))
                add_up(DC - 1)

            M.vector(dve)
            if dyn:
                for kb in range(NBI):
                    bias(0, kb)
            dve.wait_ge(M.zeroed, 2)
            over_blocks(dve, L, nb, body)
            O.vector(dve)


def attention(nc, m, L):
    normalise(nc, m, L.name, L)
    row_maxima(nc, m, L)
    weighted_values(nc, m, L)


def route(nc, m, tag, router, probs):
    parts_ready, rest_ready = m.sem(tag + "_parts12"), m.sem(tag + "_rests")
    router_loaded, steps_done, products_done, exp_ready = m.sem(tag + "_router"), m.sem(tag + "_rt_dve"), m.sem(tag + "_rt_pe"), m.sem(tag + "_rt_act")
    s = m.small
    LG = s[:, 0:32]
    ONE = [s[:, 32:64], s[:, 64:96]]
    T1, T2 = s[:, 96:128], s[:, 128:160]
    MM = [s[:, 160:164], s[:, 164:168]]
    IX, AA, BB = s[:, 168:172], s[:, 172:176], s[:, 176:180]
    SM = s[:, 180:212]
    NE, RD, CU = s[0:E, 212:213], s[0:E, 213:214], s[0:E, 214:215]
    LE = s[0:E, 216:232]
    RK = s[:, 232:264]
    def r3(x):
        return x.rearrange("p (t e) -> p t e", e=E)
    def bc(x):
        return x.unsqueeze(2).to_broadcast([P, NQ, E])
    ramp8 = m.ramp[:, 0:E].unsqueeze(1).to_broadcast([P, NQ, E])

    def second_part(act):
        act.wait_ge(rest_ready, 1)
        nc.scalar.activation(m.XP[1], m.PS[:, :, :], ACT.Copy).then_inc(parts_ready, 1)

    with nc.Block() as block:
        @block.sync
        def _(sp):
            sp.dma_start(m.WR[:, :, :], m.d[router].rearrange("(c p) e -> p c e", p=P)).then_inc(router_loaded, 16)

        @block.gpsimd
        def _(pool):
            R = m.PS[:, :, :]
            pool.wait_ge(parts_ready, 1)
            nc.gpsimd.tensor_tensor(R, m.XN[:, :, :], m.XP[0], ALU.subtract).then_inc(rest_ready, 1)
            pool.wait_ge(parts_ready, 2)
            nc.gpsimd.tensor_tensor(m.XP[2], R, m.XP[1], ALU.subtract).then_inc(rest_ready, 1)

        @block.vector
        def _(dve):
            v = nc.vector
            m.steps = 0

            def do(ins):
                m.steps += 1
                ins.then_inc(steps_done, 1)
                dve.wait_ge(steps_done, m.steps)

            dve.wait_ge(products_done, 1)
            do(v.tensor_copy(LG, m.bank[0][:, 0:32]))
            if probs:
                do(v.tensor_reduce(AA, r3(LG), AX.X, ALU.max))
                do(v.tensor_tensor(r3(LG), r3(LG), bc(AA), ALU.subtract))
                m.mark["exp"] = m.steps
                dve.wait_ge(exp_ready, 1)
                do(v.tensor_reduce(AA, r3(LG), AX.X, ALU.add))
                do(v.reciprocal(AA, AA))
                do(v.tensor_tensor(r3(LG), r3(LG), bc(AA), ALU.mult))
            do(v.tensor_copy(T1, LG))
            for k in range(2):
                do(v.tensor_reduce(MM[k], r3(T1), AX.X, ALU.max))
                do(v.tensor_tensor(r3(T2), r3(T1), bc(MM[k]), ALU.is_equal))
                do(v.tensor_scalar(T2, T2, -float(E), float(E), ALU.mult, ALU.add))
                do(v.tensor_tensor(r3(T2), r3(T2), ramp8, ALU.add))
                do(v.tensor_reduce(IX, r3(T2), AX.X, ALU.min))
                do(v.tensor_tensor(r3(ONE[k]), ramp8, bc(IX), ALU.is_equal))
                if k == 0:
                    do(v.scalar_tensor_tensor(T1, ONE[0], LOWEST, LG, ALU.mult, ALU.add))
            do(v.tensor_tensor(SM, ONE[0], ONE[1], ALU.add))
            m.mark["selected"] = m.steps
            GW = m.GW[:, :].rearrange("p (t k) -> p t k", k=2)
            if probs:
                do(v.tensor_tensor(AA, MM[0], MM[1], ALU.add))
                do(v.tensor_scalar(AA, AA, 1e-8, None, ALU.add))
                do(v.reciprocal(BB, AA))
                do(v.tensor_tensor(GW[:, :, 0], MM[0], BB, ALU.mult))
                do(v.tensor_tensor(GW[:, :, 1], MM[1], BB, ALU.mult))
            else:
                do(v.tensor_tensor(AA, MM[1], MM[0], ALU.subtract))
                m.mark["exp"] = m.steps
                dve.wait_ge(exp_ready, 1)
                do(v.tensor_scalar(BB, AA, 1.0, None, ALU.add))
                do(v.reciprocal(BB, BB))
                do(v.tensor_copy(GW[:, :, 0], BB))
                do(v.tensor_tensor(GW[:, :, 1], AA, BB, ALU.mult))
            dve.wait_ge(products_done, 2)
            do(v.tensor_copy(NE, m.bank[2][0:E, 0:1]))
            do(v.tensor_scalar(RD, NE, 0.0, None, ALU.is_gt))
            for k in range(1, NQ):
                do(v.scalar_tensor_tensor(RD, NE, float(P * k), RD, ALU.is_gt, ALU.add))
            m.mark["rounds"] = m.steps
            do(v.tensor_copy(RK, m.bank[1][:, 0:32]))
            dve.wait_ge(products_done, 3)
            do(v.tensor_copy(CU, m.bank[3][0:E, 0:1]))
            do(v.tensor_scalar(LE, m.ramp[0:E, 0:16], CU, None, ALU.is_ge))
            m.mark["of_round"] = m.steps
            do(v.tensor_scalar(T1[:, 0:E], m.bank[4][:, 0:E], float(P), None, ALU.mult))
            do(v.tensor_tensor(r3(RK), r3(RK), T1[:, 0:E].unsqueeze(1).to_broadcast([P, NQ, E]), ALU.add))
            GS = m.GS[:, :].rearrange("p (t k) -> p t k", k=2)
            for k in range(2):
                do(v.tensor_tensor(T2, RK, ONE[k], ALU.mult))
                do(v.tensor_reduce(GS[:, :, k], r3(T2), AX.X, ALU.add))
            do(v.tensor_copy(m.CTL[0:1, C_NR:C_NR + 1], m.bank[5][0:1, 0:1]))
            dve.wait_ge(products_done, 4)
            do(v.tensor_copy(m.CTL[0:1, C_E:C_E + 16], m.bank[6][0:1, 0:16]))

        @block.tensor
        def _(pe):
            t = nc.tensor
            pe.wait_ge(router_loaded, 16)
            for q in range(NQ):
                for d in range(DC):
                    last = t.matmul(m.bank[0][:, E * q:E * q + E], m.XNT[:, d, q * P:(q + 1) * P], m.WR[:, d, :],
                                    start=d == 0, stop=d == DC - 1)
            last.then_inc(products_done, 1)
            pe.wait_ge(steps_done, m.mark["selected"])
            for q in range(NQ):
                for b in range(q + 1):
                    t.matmul(m.bank[1][:, E * q:E * q + E], (m.before if b == q else m.ones)[:, :], r3(SM)[:, b, :],
                             start=b == 0, stop=b == q)
            for q in range(NQ):
                last = t.matmul(m.bank[2][0:E, 0:1], r3(SM)[:, q, :], m.ones[:, 0:1], start=q == 0, stop=q == NQ - 1)
            last.then_inc(products_done, 1)
            pe.wait_ge(steps_done, m.mark["rounds"])
            t.matmul(m.bank[3][0:E, 0:1], m.upto[0:E, 0:E], RD, start=True, stop=True)
            t.matmul(m.bank[4][:, 0:E], RD.to_broadcast([E, P]), m.before[0:E, 0:E], start=True, stop=True)
            t.matmul(m.bank[5][0:1, 0:1], RD, m.ones[0:E, 0:1], start=True, stop=True).then_inc(products_done, 1)
            pe.wait_ge(steps_done, m.mark["of_round"])
            t.matmul(m.bank[6][0:1, 0:16], m.ones[0:E, 0:1], LE, start=True, stop=True).then_inc(products_done, 1)

        @block.scalar
        def _(act):
            nc.scalar.activation(m.XP[0], m.XN[:, :, :], ACT.Copy).then_inc(parts_ready, 1)
            if not probs:
                second_part(act)
            act.wait_ge(steps_done, m.mark["exp"])
            if probs:
                nc.scalar.activation(LG, LG, ACT.Exp).then_inc(exp_ready, 1)
                second_part(act)
            else:
                nc.scalar.activation(AA, AA, ACT.Exp).then_inc(exp_ready, 1)


def experts(nc, m, tag, w1, w2, F, relu2):
    m.fresh = []
    NF = F // KB
    w1_loaded, w2_loaded = ([m.sem(f"{tag}_{w}_{k}") for k in range(NF)] for w in ("w1", "w2"))
    token_hots_ready, weight_hots_ready, gather_ready, tokens_copied = (m.sem(tag + x) for x in ("_token_of_slot", "_weight_of_slot", "_gather", "_gathered"))
    hidden_ready, hidden_copied, output_copied, scatter_ready = (m.sem(tag + x) for x in ("_h", "_act", "_yout", "_scatter"))
    x_added, transposed, transposes_copied, output_ready, activated, slots_moved = (m.sem(tag + x) for x in ("_xadd", "_tr", "_trout", "_used", "_exp", "_dve"))
    def slots(a, b):
        return [t[:, 8 * k:8 * k + 8, :].bitcast(F32).rearrange("p (c x) n -> p c (x n)", x=2) for t in (a, b) for k in range(2)]
    W1, W2 = slots(m.QA, m.QB), slots(m.KA, m.KBS)
    DG, DW, XE = m.KF, m.V, m.CT[:, 0, :]
    DGB = m.KF[:, :, 3 * P:4 * P].bitcast(BF16)[:, :, 0:P]
    HT = m.PB[:, :, :, :].rearrange("p a b (c n) -> p (a b c) n", n=P)
    HS = HT[:, 0:4 * NF, :]
    EX = m.MI[:, :, :].bitcast(F32)
    HR = m.MB
    row = [m.CT[:, c, :].bitcast(BF16) for c in (1, 3)]
    DT, WS, Y, YP = row[0][:, 0:T], m.small[:, 0:1], m.CT[:, 2, :], [row[1][:, 0:D], row[1][:, D:2 * D], row[0][:, T:T + D]]
    weight_ready, parts_ready, rest_ready = m.sem(tag + "_weight"), m.sem(tag + "_yparts"), m.sem(tag + "_yrest")
    B = raised(nc, m, True)
    with nc.Block() as block:
        @block.sync
        def _(sp):
            nr = sp.value_load(m.CTL[0:1, C_NR:C_NR + 1], min_val=0, max_val=NR)
            with sp.Fori(0, NR) as i:
                with sp.If(i < nr):
                    e = sp.value_load(m.CTL[0:1, bass.ds(i + C_E, 1)], min_val=0, max_val=E - 1)
                    for k in range(NF):
                        wait_alone(sp, hidden_ready, i * NF + B)
                        sp.dma_start(W1[k], m.d[w1][bass.ds(e, 1), :, k * KB:(k + 1) * KB].rearrange("a (c p) n -> p (a c) n", p=P)).then_inc(w1_loaded[k], 16)
                    for k in range(NF):
                        wait_alone(sp, output_ready, i * NF + B)
                        sp.dma_start(W2[k], m.d[w2][bass.ds(e, 1), k * KB:(k + 1) * KB, :].rearrange("a (c p) n -> p (a c) n", p=P)).then_inc(w2_loaded[k], 16)

        @block.vector
        def _(dve):
            v = nc.vector
            nr = dve.value_load(m.CTL[0:1, C_NR:C_NR + 1], min_val=0, max_val=NR)
            def token_hots(i):
                for q in range(NQ):
                    for k in range(2):
                        j = 2 * q + k
                        last = v.tensor_scalar(DG[:, q, P * k:P * k + P], m.ramp[:, :], m.GS[:, j:j + 1], None, ALU.is_equal)
                last.then_inc(token_hots_ready, 1)
                dve.wait_ge(token_hots_ready, i * 2 + 1 + B)
                v.tensor_tensor(DGB, DG[:, :, 0:P], DG[:, :, P:2 * P], ALU.add).then_inc(token_hots_ready, 1)

            def weight_hots(i):
                for q in range(NQ):
                    for k in range(2):
                        j = 2 * q + k
                        last = v.tensor_scalar(DW[:, q, P * k:P * k + P], m.ramp[:, :], m.GS[:, j:j + 1], m.GW[:, j:j + 1],
                                               ALU.is_equal, ALU.mult)
                last.then_inc(weight_hots_ready, 1)
                dve.wait_ge(weight_hots_ready, i * 2 + 1 + B)
                v.tensor_tensor(DW[:, :, 2 * P:3 * P], DW[:, :, 0:P], DW[:, :, P:2 * P], ALU.add).then_inc(weight_hots_ready, 1)
                v.tensor_scalar(m.GS[:, :], m.GS[:, :], float(P), None, ALU.subtract).then_inc(slots_moved, 1)

            token_hots(0)
            weight_hots(0)
            dve.wait_ge(gather_ready, 1 + B)
            v.tensor_copy(XE, m.bank[1][:, :]).then_inc(tokens_copied, 1)
            with dve.Fori(0, NR) as i:
                with dve.If(i < nr):
                    dve.wait_ge(gather_ready, i + 1 + B)
                    dve.wait_ge(slots_moved, i + 1 + B)
                    dve.wait_ge(token_hots_ready, i * 2 + 2 + B)
                    token_hots(i + 1)
                    for k in range(NF):
                        hb = m.bank[2 + k % 2][:, :]
                        out = HS[:, 4 * k:4 * k + 4, :].rearrange("p a n -> p (a n)")
                        if relu2:
                            dve.wait_ge(hidden_ready, i * NF + k + 1 + B)
                            v.tensor_scalar(HR[:, k, :], hb, 0.0, None, ALU.max).then_inc(activated, 1)
                            dve.wait_ge(activated, i * NF + k + 1 + B)
                            v.tensor_tensor(out, HR[:, k, :], HR[:, k, :], ALU.mult).then_inc(hidden_copied, 1)
                        else:
                            dve.wait_ge(activated, i * NF + k + 1 + B)
                            v.tensor_tensor(out, EX[:, k, :], hb, ALU.mult).then_inc(hidden_copied, 1)
                    dve.wait_ge(transposed, i + 1 + B)
                    dve.wait_ge(scatter_ready, i * NQ + B)
                    v.tensor_reduce(WS, m.bank[1][:, :], AX.X, ALU.add).then_inc(weight_ready, 1)
                    v.tensor_scalar(DT, m.bank[1][:, :], 0.0, None, ALU.is_gt).then_inc(transposes_copied, 1)
                    dve.wait_ge(weight_hots_ready, i * 2 + 2 + B)
                    weight_hots(i + 1)
                    dve.wait_ge(output_ready, (i + 1) * NF + B)
                    dve.wait_ge(weight_ready, i + 1 + B)
                    v.tensor_scalar(YP[0], m.bank[0][:, :], WS, None, ALU.mult).then_inc(parts_ready, 1)
                    v.tensor_scalar(Y, m.bank[0][:, :], WS, None, ALU.mult).then_inc(output_copied, 1)
                    dve.wait_ge(output_copied, i + 1 + B)
                    dve.wait_ge(parts_ready, i * 3 + 1 + B)
                    v.tensor_tensor(Y, Y, YP[0], ALU.subtract).then_inc(rest_ready, 1)
                    dve.wait_ge(rest_ready, i + 1 + B)
                    v.tensor_copy(YP[1], Y).then_inc(parts_ready, 1)
                    dve.wait_ge(parts_ready, i * 3 + 2 + B)
                    v.tensor_tensor(YP[2], Y, YP[1], ALU.subtract).then_inc(parts_ready, 1)
                    dve.wait_ge(gather_ready, i + 2 + B)
                    dve.wait_ge(hidden_ready, i * NF + NF + B)
                    v.tensor_copy(XE, m.bank[1][:, :]).then_inc(tokens_copied, 1)
                    dve.wait_ge(x_added, i * NQ + B)
                    for q in range(NQ):
                        dve.wait_ge(scatter_ready, i * NQ + q + 1 + B)
                        v.tensor_tensor(m.X[:, q, :], m.X[:, q, :], m.bank[4 + q][:, :], ALU.add).then_inc(x_added, 1)
            wait_alone(dve, x_added, nr * NQ + B)

        @block.scalar
        def _(act):
            if relu2:
                return
            nr = act.value_load(m.CTL[0:1, C_NR:C_NR + 1], min_val=0, max_val=NR)
            with act.Fori(0, NR) as i:
                with act.If(i < nr):
                    for k in range(NF):
                        act.wait_ge(hidden_ready, i * NF + k + 1 + B)
                        nc.scalar.activation(EX[:, k, :], m.bank[2 + k % 2][:, :], ACT.Sigmoid).then_inc(activated, 1)

        @block.tensor
        def _(pe):
            t = nc.tensor
            nr = pe.value_load(m.CTL[0:1, C_NR:C_NR + 1], min_val=0, max_val=NR)

            def gather(i):
                pe.wait_ge(token_hots_ready, i * 2 + 2 + B)
                for d in range(DC):
                    for j in range(3):
                        for q in range(NQ):
                            last = t.matmul(m.bank[1][:, d * P:(d + 1) * P], m.XP[j][:, q, d * P:(d + 1) * P],
                                            DGB[:, q, :], start=j + q == 0, stop=j == 2 and q == NQ - 1)
                last.then_inc(gather_ready, 1)

            gather(0)
            with pe.Fori(0, NR) as i:
                with pe.If(i < nr):
                    pe.wait_ge(tokens_copied, i + 1 + B)
                    for k in range(NF):
                        pe.wait_ge(w1_loaded[k], i * 16 + 16 + B)
                        pe.wait_ge(hidden_copied, i * NF + max(0, k - 1) + B)
                        for f in range(4):
                            for d in range(DC):
                                last = t.matmul(m.bank[2 + k % 2][:, f * P:(f + 1) * P], W1[k][:, d, f * P:(f + 1) * P],
                                                XE[:, d * P:(d + 1) * P], start=d == 0, stop=d == DC - 1)
                        last.then_inc(hidden_ready, 1)
                    pe.wait_ge(weight_hots_ready, i * 2 + 2 + B)
                    for q in range(NQ):
                        last = t.transpose(m.bank[1][:, q * P:(q + 1) * P], DW[:, q, 2 * P:3 * P], m.ident[:, :])
                    last.then_inc(transposed, 1)
                    pe.wait_ge(output_copied, i + B)
                    for k in range(NF):
                        pe.wait_ge(w2_loaded[k], i * 16 + 16 + B)
                        pe.wait_ge(hidden_copied, i * NF + k + 1 + B)
                        for f in range(4):
                            last = t.matmul(m.bank[0][:, :], HS[:, 4 * k + f, :], W2[k][:, f, :],
                                            start=k + f == 0, stop=(k == NF - 1 and f == 3))
                        last.then_inc(output_ready, 1)
                    pe.wait_ge(transposes_copied, i + 1 + B)
                    gather(i + 1)
                    pe.wait_ge(x_added, i * NQ + B)
                    for j in range(3):
                        pe.wait_ge(parts_ready, i * 3 + j + 1 + B)
                        for q in range(NQ):
                            last = t.matmul(m.bank[4 + q][:, :], DT[:, q * P:(q + 1) * P], YP[j], start=j == 0, stop=j == 2)
                            if j == 2:
                                last.then_inc(scatter_ready, 1)


def build(nc, d, out):
    with ExitStack() as ctx:
        m = Chip()
        m.d = d
        m.mark = {}

        def sb(name, shape, dt=F32):
            return ctx.enter_context(nc.sbuf_tensor(name, shape, dt))

        m.open_sems, m.fresh = [], []

        def sem(name):
            m.open_sems.append(nc.alloc_semaphore(name=name))
            m.fresh.append(m.open_sems[-1])
            return m.open_sems[-1]

        def layer_done():
            nc.clear_and_free_semaphores(m.open_sems)
            nc.all_engine_barrier()
            m.open_sems = []

        m.sem = sem
        m.X, m.XN, m.XNT = sb("X", [P, NQ, D]), sb("XN", [P, NQ, D]), sb("XNT", [P, DC, T])
        m.QA, m.QB, m.KA, m.KBS = (sb(x, [P, H, T], BF16) for x in ("QA", "QB", "KA", "KBS"))
        m.KF, m.CT, m.V = sb("KF", [P, DC, KB]), sb("CT", [P, DC, KB]), sb("V", [P, KT_, D])
        m.PB, m.PS = sb("PB", [P, 2, G, T]), sb("PS", [P, G, T])
        m.ACC = sb("ACC", [P, 2, DC, T])
        m.OACC, m.DACC = m.ACC[:, 0], m.ACC[:, 1]
        m.PARTS = m.ACC[:, :, :, :].bitcast(BF16).rearrange("p a c n -> p (a c n)")[:, 0:3 * DC * KB].rearrange(
            "p (j c n) -> p j c n", j=3, c=DC)
        m.XP = [m.PARTS[:, j] for j in range(3)]
        m.JUNK = m.PS[:, 0:2, :].bitcast(BF16).rearrange("p a (b n) -> p (a b) n", n=KB)
        m.WQ, m.WK, m.WV = (sb(x, [P, DC, D]) for x in ("WQ", "WK", "WV"))
        m.MASK = sb("MASK", [P, 2, NQ, KB])
        m.MI, m.MB = m.MASK[:, 0].bitcast(I32), m.MASK[:, 1]
        m.MBK = m.MASK[:, 1, 0:2, :].bitcast(BF16).rearrange("p a (b n) -> p (a b) n", n=KB)
        two = m.CT[:, :, :].bitcast(BF16).rearrange("p c n -> p (c n)").rearrange("p (j c n) -> p j c n", j=2, c=KT_)
        m.MBF = [two[:, 0], two[:, 1], m.MASK[:, 0, 0:2, :].bitcast(BF16).rearrange("p a (b n) -> p (a b) n", n=T)]
        m.RAROW, m.RNROW, m.RAROWS = sb("RAROW", [P, T]), sb("RNROW", [P, T]), sb("RAROWS", [P, T])
        m.NM, m.NMX = m.KF[0:3 * H, 0, :].bitcast(BF16)[:, 0:T], m.KF[:, 1, 0:NQ * 3 * H]
        m.CON, m.VT = sb("CON", [P, len(CONST), P]), sb("VT", [P, len(VEC), 4])
        m.IDB = sb("IDB", [P, P], BF16)
        m.KMW, m.KBIAS = sb("KM", [P, KB // 4], I32), sb("KBIAS", [P, KT_])
        m.KM = m.KMW[:, :].bitcast(U8)
        m.MX, m.MXB = sb("MX", [P, H * NQ]), sb("MXB", [P, H * NQ], BF16)
        m.RA, m.RN, m.WR = sb("RA", [P, NQ]), sb("RN", [P, NQ]), sb("WR", [P, DC, E])
        m.GS, m.GW = sb("GS", [P, 2 * NQ]), sb("GW", [P, 2 * NQ])
        m.UNMASKED = m.SUMS = sb("UNMASKED", [P, NQ, NB])
        m.EPS, m.MINUS1 = sb("EPS", [P, 1]), sb("MINUS1", [P, 1])
        m.RSTDS, m.RSTD = m.RAROWS, m.RAROWS[0:H, :]
        qp = m.PB[:, 1].bitcast(BF16).rearrange("p g n -> p (g n)").rearrange("p (j c n) -> p j c n", j=2, c=DC)
        m.QP = [qp[:, 0], qp[:, 1], m.PS[:, 2:4, :].bitcast(BF16).rearrange("p a (b n) -> p (a b) n", n=T)]
        halves = m.KBS[:, :, :].bitcast(I32).rearrange("p h n -> p (h n)").rearrange("p (a q n) -> p a q n", a=2, n=KB)
        m.COUNT = [halves[:, 0], halves[:, 1], m.XN[:, :, :].bitcast(I32), m.MI]
        m.small, m.CTL = sb("small", [P, 264]), sb("CTL", [1, C_M + NB + 1], I32)
        tiles = {k: m.CON[:, i, :] for i, k in enumerate(CONST)}
        m.ident, m.gmean, m.before, m.upto, m.ones, m.ramp, m.index, m.head_mean = (tiles[k] for k in CONST[:8])
        m.spread = [tiles[f"spread{c}"] for c in range(DC)]
        m.vec = lambda name: m.VT[:, VEC.index(name), :]
        m.bank = [ctx.enter_context(nc.psum_tensor(f"bank{i}", [P, 512], F32)) for i in range(8)]
        m.KSAVE = nc.dram_tensor("k_saved", (NB + 1, P, 3, DC, KB), BF16, kind="Internal").ap()
        m.VSAVE = nc.dram_tensor("v_saved", (NB + 1, P, KT_, D), F32, kind="Internal").ap()
        m.QSAVE = nc.dram_tensor("q_saved", (3, P, DC, T), BF16, kind="Internal").ap()

        UNWAITED[:] = [nc.alloc_semaphore(name="unwaited")]
        active_blocks(nc, m, "blocks0", None, C_N0)
        layer_done()
        attention(nc, m, Attention("L0x", "L0x_wq", "L0x_wk", "L0x_wv", "L0x_wo", 0, count=C_N0, norm=True))
        layer_done()
        attention(nc, m, Attention("L0a", "L0a_wq", "L0a_wk", "L0a_wv", "L0a_wo", 1, fixed=0))
        layer_done()
        normalise(nc, m, "L0f")
        route(nc, m, "L0f", "L0f_router", False)
        experts(nc, m, "L0f", "L0f_w1", "L0f_w2", 2048, False)
        layer_done()
        active_blocks(nc, m, "blocks1", None, C_N1, m.UNMASKED[:, :, :])
        attention(nc, m, Attention("L1x", "L1x_wq", "L1x_wk", "L1x_wv", "L1x_wo", 2, count=C_N1, row_mask=True))
        layer_done()
        attention(nc, m, Attention("L1a", "L1a_wq", "L1a_wk", "L1a_wv", "L1a_wo", 3, fixed=1))
        layer_done()
        normalise(nc, m, "L1f")
        route(nc, m, "L1f", "L1f_router", True)
        experts(nc, m, "L1f", "L1f_w1", "L1f_w2", 1024, True)
        stored = m.sem("stored")
        with nc.Block() as block:
            @block.sync
            def _(sp):
                sp.dma_start(out.rearrange("(t p) d -> p t d", p=P), m.X[:, :, :]).then_inc(stored, 16)
                sp.wait_ge(stored, 16)
        layer_done()


def laid_out(i):
    a = {k: np.asarray(v) for k, v in i.items()}
    d = {"x": a["x"][0]}
    d["ctx"] = a["ctx_1024"][0].reshape(NB, KB, DC, P).transpose(0, 3, 2, 1)
    mask = a["mask_Bx1xSxS2_ik1"][0, 0]
    d["mask_q"] = mask.reshape(NQ, P, NB, KB).transpose(2, 1, 0, 3)
    d["mask_k"] = mask.T.reshape(NB, KT_, P, T).transpose(0, 2, 1, 3)
    km = a["mask_BxS2_bk0"][0].view(np.uint8)
    d["keymask"] = km.reshape(NB, KB).view(np.int32)
    d["keymask_k"] = np.ascontiguousarray(km.reshape(NB, KT_, P).transpose(0, 2, 1)).view(np.int32)
    wkv = a["L0_xattn_Wkv"]
    d["L0x_wq"], d["L0x_wk"], d["L0x_wv"], d["L0x_wo"] = a["L0_xattn_Wq"].T, wkv[:D].T, wkv[D:].T, a["L0_xattn_Wo"].T
    w = a["L0_attn_w_qkv"]
    d["L0a_wq"], d["L0a_wk"], d["L0a_wv"], d["L0a_wo"] = w[:, :D], w[:, D:2 * D], w[:, 2 * D:], a["L0_attn_w_out"]
    for s, l in (("L1x", "L1_xattn"), ("L1a", "L1_attn")):
        for x in "qkvo":
            d[f"{s}_w{x}"] = a[f"{l}_W{x}"].T
    d["L0f_router"], d["L0f_w1"], d["L0f_w2"] = a["L0_ffn_router"], a["L0_ffn_W1"], a["L0_ffn_W2"]
    d["L1f_router"], d["L1f_w1"], d["L1f_w2"] = a["L1_ffn_Wg"], a["L1_ffn_W1"], a["L1_ffn_W2"]
    b0, ba = a["L0_xattn_bkv"], a["L0_attn_b_qkv"]
    vec = {"L0x_bq": a["L0_xattn_bq"], "L0x_bk": b0[:D], "L0x_bv": b0[D:], "L0a_bq": ba[:D], "L0a_bk": ba[D:2 * D],
           "L0a_bv": ba[2 * D:], "L1x_bq": a["L1_xattn_bq"], "L1x_bk": a["L1_xattn_bk"], "L1x_bv": a["L1_xattn_bv"],
           "zero": np.zeros(D, np.float32)}
    for x in ("qn_w", "qn_b", "kn_w", "kn_b"):
        vec[x] = np.tile(a[f"L0_xattn_{x}"], D // HD)
    d["vectors"] = np.concatenate([vec[n].reshape(DC, P).T for n in VEC], axis=1)
    d["bo"] = np.stack([np.broadcast_to(a[n], (P, D)) for n in ("L0_xattn_bo", "L0_attn_b_out", "L1_xattn_bo", "L1_attn_bo")])
    d["consts"] = consts()
    d["biases"] = fixed_biases()
    d["bias_parts"] = in_parts(d["biases"][:, 1])
    return {k: np.ascontiguousarray(v) for k, v in d.items()}


def kernel(**inputs):
    import concourse.bacc as _bacc
    from concourse.bass_utils import run_bass_kernel_spmd as _run

    nc = _bacc.Bacc("TRN2", target_bir_lowering=False, num_devices=1)
    arrays = {f"in_{k}": v for k, v in laid_out(inputs).items()}
    d = {k[3:]: nc.dram_tensor(k, v.shape, mybir.dt.from_np(v.dtype), kind="ExternalInput").ap()
         for k, v in arrays.items()}
    out = nc.dram_tensor("out", (T, D), F32, kind="ExternalOutput").ap()
    build(nc, d, out)
    r = _run(nc, [arrays], core_ids=[0])
    return np.asarray(r.results[0]["out"]).reshape(1, T, D)
```
